# Optimizing a Trainium2 kernel written in Bass

```python
import numpy as np
import jax
import jax.numpy as jnp

def _softmax(x, axis=-1):
    return jax.nn.softmax(x, axis=axis)

def _gelu(x):
    return jax.nn.gelu(x, approximate=True)

def _silu(x):
    return jax.nn.silu(x)

def _sigmoid(x):
    return jax.nn.sigmoid(x)

def _layernorm(x, axis=-1, eps=1e-05):
    m = jnp.mean(x, axis=axis, keepdims=True)
    v = jnp.var(x, axis=axis, keepdims=True)
    return (x - m) / jnp.sqrt(v + eps)

def _scatter_add(tgt, idx, src, axis=0):
    return tgt.at[idx].add(src)

def _segment_sum(src, seg, n):
    return jax.ops.segment_sum(src, seg, n)
kernel_name = 'mk_hybrid_d1_jaxref_r4_ab0bbf'

def setup_inputs(seed: int=0):
    np.random.seed(seed)
    _w = jnp.asarray

    def _L0_attn_a_setup():
        import jax, jax.numpy as jnp
        import numpy as np
        B, T, DM, H, D = (2, 1024, 256, 16, 64)
        HD = H * D
        PHASE_SCALE = 10.0

        def _multiscale_phasors(num_heads, head_dim):
            d = np.arange(head_dim, dtype=np.float32) / head_dim
            base = 10000.0 ** (-d)
            head_scale = 2.0 ** (-np.arange(num_heads, dtype=np.float32))
            return jnp.asarray(2.0 * np.pi * head_scale[:, None] * base[None, :], dtype=jnp.float32)

        def _holo_fused_step(v, binder, probe):
            mem = jnp.cumsum(v * binder, axis=1)
            t = v.shape[1]
            scale = jnp.sqrt(jnp.arange(1, t + 1, dtype=jnp.float32))[None, :, None, None]
            return jnp.real(mem * probe) / scale
        key = jax.random.key(seed)
        k0, k1, k2, k3 = jax.random.split(key, 4)
        x = jax.random.normal(k0, (B, T, DM), jnp.float32)
        Wk = jax.random.normal(k1, (DM, HD), jnp.float32) / np.float32(np.sqrt(DM))
        Wv = jax.random.normal(k2, (DM, HD), jnp.float32) / np.float32(np.sqrt(DM))
        Wo = jax.random.normal(k3, (HD, DM), jnp.float32) / np.float32(np.sqrt(HD))
        gate = jnp.full((H, 2), 0.5, jnp.float32)
        freqs = _multiscale_phasors(H, D)
        return {'x': x, 'Wk': Wk, 'Wv': Wv, 'Wo': Wo, 'gate': gate, 'freqs': freqs}
    _L0_attn_a_in = _L0_attn_a_setup()

    def _L0_attn_b_setup():
        import jax, jax.numpy as jnp
        import numpy as np
        D_MODEL = 256
        NUM_HEADS = 16
        D_K = D_MODEL // NUM_HEADS
        C = 1.0
        EPS = 1e-15

        def poincare_fully_connected(x, z, r, c):
            c_sqrt = jnp.sqrt(c)
            lam = 2.0 / (1.0 - c * jnp.sum(x * x, axis=-1, keepdims=True))
            z_norm = jnp.maximum(jnp.linalg.norm(z, axis=0), EPS)
            two_cr = 2.0 * c_sqrt * r
            inner = x @ (z / z_norm)
            v = 2.0 * z_norm / c_sqrt * jnp.arcsinh(c_sqrt * lam * inner * jnp.cosh(two_cr) - (lam - 1.0) * jnp.sinh(two_cr))
            w = jnp.sinh(c_sqrt * v) / c_sqrt
            return w / (1.0 + jnp.sqrt(1.0 + c * jnp.sum(w * w, axis=-1, keepdims=True)))
        key = jax.random.key(seed)
        ks = jax.random.split(key, 7)
        B, S, D = (4, 512, D_MODEL)
        x = jax.random.normal(ks[0], (B, S, D), jnp.float32)
        x = 0.7 * x / jnp.max(jnp.linalg.norm(x, axis=-1, keepdims=True))
        scale = 1.0 / np.sqrt(D).astype(np.float32)
        return {'x': x, 'z_q': jax.random.normal(ks[1], (D, D), jnp.float32) * scale, 'b_q': jax.random.normal(ks[2], (D,), jnp.float32) * 0.01, 'z_k': jax.random.normal(ks[3], (D, D), jnp.float32) * scale, 'b_k': jax.random.normal(ks[4], (D,), jnp.float32) * 0.01, 'w_v': jax.random.normal(ks[5], (D, D), jnp.float32) * scale, 'b_v': jax.random.normal(ks[6], (D,), jnp.float32) * 0.01}
    _L0_attn_b_in = _L0_attn_b_setup()

    def _L0_ffn_setup():
        import jax, jax.numpy as jnp
        import numpy as np
        B, S, DIM = (4, 1024, 256)
        BASE_COUPLING = 0.1
        NUM_CYCLES = 3

        def _gelu(x):
            return jax.nn.gelu(x, approximate=False)

        def _coupling_net(h, w1, b1, w2, b2, w3, b3, w4, b4):
            h = _gelu(h @ w1 + b1)
            h = _gelu(h @ w2 + b2)
            h = _gelu(h @ w3 + b3)
            return jax.nn.sigmoid(h @ w4 + b4)

        def _global_net(h, w1, b1, w2, b2, w3, b3):
            h = _gelu(h @ w1 + b1)
            h = _gelu(h @ w2 + b2)
            return jax.nn.sigmoid(h @ w3 + b3)

        def _twist(x):
            o_r, o_i, p_r, p_i = jnp.split(x, 4, axis=-1)
            return jnp.concatenate([p_r, -p_i, -o_r, o_i], axis=-1)
        key = jax.random.key(seed)
        ks = jax.random.split(key, 9)
        d = DIM

        def w(k, fan_in, fan_out):
            return jax.random.normal(k, (fan_in, fan_out), dtype=jnp.float32) / np.sqrt(fan_in).astype(np.float32)
        inp = {'x': jax.random.normal(ks[0], (B, S, d), dtype=jnp.float32)}
        cn_dims = [(d, d), (d, d // 2), (d // 2, d // 4), (d // 4, 1)]
        for i, (a, b) in enumerate(cn_dims):
            inp[f'cn_w{i + 1}'] = w(ks[1 + i], a, b)
            inp[f'cn_b{i + 1}'] = jnp.zeros((b,), dtype=jnp.float32)
        gc_dims = [(d, d // 2), (d // 2, d // 4), (d // 4, 1)]
        for i, (a, b) in enumerate(gc_dims):
            inp[f'gc_w{i + 1}'] = w(ks[5 + i], a, b)
            inp[f'gc_b{i + 1}'] = jnp.zeros((b,), dtype=jnp.float32)
        inp['adaptive_range'] = jnp.full((1,), 0.2, dtype=jnp.float32)
        return inp
    _L0_ffn_in = _L0_ffn_setup()
    _d = {'L0_attn_a_x': _L0_attn_a_in['x'], 'L0_attn_a_Wk': _L0_attn_a_in['Wk'], 'L0_attn_a_Wv': _L0_attn_a_in['Wv'], 'L0_attn_a_Wo': _L0_attn_a_in['Wo'], 'L0_attn_a_gate': _L0_attn_a_in['gate'], 'L0_attn_a_freqs': _L0_attn_a_in['freqs'], 'L0_attn_b_z_q': _L0_attn_b_in['z_q'], 'L0_attn_b_b_q': _L0_attn_b_in['b_q'], 'L0_attn_b_z_k': _L0_attn_b_in['z_k'], 'L0_attn_b_b_k': _L0_attn_b_in['b_k'], 'L0_attn_b_w_v': _L0_attn_b_in['w_v'], 'L0_attn_b_b_v': _L0_attn_b_in['b_v'], 'L0_ffn_cn_w1': _L0_ffn_in['cn_w1'], 'L0_ffn_cn_b1': _L0_ffn_in['cn_b1'], 'L0_ffn_cn_w2': _L0_ffn_in['cn_w2'], 'L0_ffn_cn_b2': _L0_ffn_in['cn_b2'], 'L0_ffn_cn_w3': _L0_ffn_in['cn_w3'], 'L0_ffn_cn_b3': _L0_ffn_in['cn_b3'], 'L0_ffn_cn_w4': _L0_ffn_in['cn_w4'], 'L0_ffn_cn_b4': _L0_ffn_in['cn_b4'], 'L0_ffn_gc_w1': _L0_ffn_in['gc_w1'], 'L0_ffn_gc_b1': _L0_ffn_in['gc_b1'], 'L0_ffn_gc_w2': _L0_ffn_in['gc_w2'], 'L0_ffn_gc_b2': _L0_ffn_in['gc_b2'], 'L0_ffn_gc_w3': _L0_ffn_in['gc_w3'], 'L0_ffn_gc_b3': _L0_ffn_in['gc_b3'], 'L0_ffn_adaptive_range': _L0_ffn_in['adaptive_range']}
    _x0 = _d['L0_attn_a_x']
    _d['L0_attn_a_x'] = jax.random.normal(jax.random.fold_in(jax.random.key(seed), 1), (8, 1024, 256), dtype=_x0.dtype)
    del _x0
    return _d

def reference(L0_attn_a_x, L0_attn_a_Wk, L0_attn_a_Wv, L0_attn_a_Wo, L0_attn_a_gate, L0_attn_a_freqs, L0_attn_b_z_q, L0_attn_b_b_q, L0_attn_b_z_k, L0_attn_b_b_k, L0_attn_b_w_v, L0_attn_b_b_v, L0_ffn_cn_w1, L0_ffn_cn_b1, L0_ffn_cn_w2, L0_ffn_cn_b2, L0_ffn_cn_w3, L0_ffn_cn_b3, L0_ffn_cn_w4, L0_ffn_cn_b4, L0_ffn_gc_w1, L0_ffn_gc_b1, L0_ffn_gc_w2, L0_ffn_gc_b2, L0_ffn_gc_w3, L0_ffn_gc_b3, L0_ffn_adaptive_range):

    def _L0_attn_a_ref(x, Wk, Wv, Wo, gate, freqs):
        import jax, jax.numpy as jnp
        import numpy as np
        B, T, DM, H, D = (2, 1024, 256, 16, 64)
        HD = H * D
        PHASE_SCALE = 10.0

        def _multiscale_phasors(num_heads, head_dim):
            d = np.arange(head_dim, dtype=np.float32) / head_dim
            base = 10000.0 ** (-d)
            head_scale = 2.0 ** (-np.arange(num_heads, dtype=np.float32))
            return jnp.asarray(2.0 * np.pi * head_scale[:, None] * base[None, :], dtype=jnp.float32)

        def _holo_fused_step(v, binder, probe):
            mem = jnp.cumsum(v * binder, axis=1)
            t = v.shape[1]
            scale = jnp.sqrt(jnp.arange(1, t + 1, dtype=jnp.float32))[None, :, None, None]
            return jnp.real(mem * probe) / scale
        Bb, Tt, _ = x.shape
        k_real = (x @ Wk).reshape(Bb, Tt, H, D)
        v = (x @ Wv).reshape(Bb, Tt, H, D).astype(jnp.complex64)
        k = jnp.exp(1j * (k_real * PHASE_SCALE))
        t = jnp.arange(Tt, dtype=jnp.float32)
        rotors = jnp.exp(1j * (t[:, None, None] * freqs))[None]
        out_pos = _holo_fused_step(v, rotors, jnp.conj(rotors))
        k_shifted = jnp.roll(k, 1, axis=1).at[:, 0].set(0.0)
        out_assoc = _holo_fused_step(v, jnp.conj(k_shifted), k)
        g_pos = gate[:, 0][None, None, :, None]
        g_assoc = gate[:, 1][None, None, :, None]
        out = out_pos * g_pos + out_assoc * g_assoc
        return out.reshape(Bb, Tt, HD) @ Wo

    def _L0_attn_b_ref(x, z_q, b_q, z_k, b_k, w_v, b_v):
        import jax, jax.numpy as jnp
        import numpy as np
        D_MODEL = 256
        NUM_HEADS = 16
        D_K = D_MODEL // NUM_HEADS
        C = 1.0
        EPS = 1e-15

        def poincare_fully_connected(x, z, r, c):
            c_sqrt = jnp.sqrt(c)
            lam = 2.0 / (1.0 - c * jnp.sum(x * x, axis=-1, keepdims=True))
            z_norm = jnp.maximum(jnp.linalg.norm(z, axis=0), EPS)
            two_cr = 2.0 * c_sqrt * r
            inner = x @ (z / z_norm)
            v = 2.0 * z_norm / c_sqrt * jnp.arcsinh(c_sqrt * lam * inner * jnp.cosh(two_cr) - (lam - 1.0) * jnp.sinh(two_cr))
            w = jnp.sinh(c_sqrt * v) / c_sqrt
            return w / (1.0 + jnp.sqrt(1.0 + c * jnp.sum(w * w, axis=-1, keepdims=True)))
        B, S, D = x.shape
        Q = poincare_fully_connected(x, z_q, b_q, C)
        K = poincare_fully_connected(x, z_k, b_k, C)
        V = x @ w_v.T + b_v

        def split_heads(t):
            return t.reshape(B, S, NUM_HEADS, D_K).transpose(0, 2, 1, 3)
        Qh, Kh, Vh = (split_heads(Q), split_heads(K), split_heads(V))
        scores = jnp.einsum('bhqd,bhkd->bhqk', Qh, Kh) / np.sqrt(D_K).astype(np.float32)
        probs = jax.nn.softmax(scores, axis=-1)
        out = jnp.einsum('bhqk,bhkd->bhqd', probs, Vh)
        return out.transpose(0, 2, 1, 3).reshape(B, S, D)

    def _L0_ffn_ref(x, cn_w1, cn_b1, cn_w2, cn_b2, cn_w3, cn_b3, cn_w4, cn_b4, gc_w1, gc_b1, gc_w2, gc_b2, gc_w3, gc_b3, adaptive_range):
        import jax, jax.numpy as jnp
        import numpy as np
        B, S, DIM = (4, 1024, 256)
        BASE_COUPLING = 0.1
        NUM_CYCLES = 3

        def _gelu(x):
            return jax.nn.gelu(x, approximate=False)

        def _coupling_net(h, w1, b1, w2, b2, w3, b3, w4, b4):
            h = _gelu(h @ w1 + b1)
            h = _gelu(h @ w2 + b2)
            h = _gelu(h @ w3 + b3)
            return jax.nn.sigmoid(h @ w4 + b4)

        def _global_net(h, w1, b1, w2, b2, w3, b3):
            h = _gelu(h @ w1 + b1)
            h = _gelu(h @ w2 + b2)
            return jax.nn.sigmoid(h @ w3 + b3)

        def _twist(x):
            o_r, o_i, p_r, p_i = jnp.split(x, 4, axis=-1)
            return jnp.concatenate([p_r, -p_i, -o_r, o_i], axis=-1)
        global_context = x.mean(axis=1, keepdims=True)
        gf = _global_net(global_context, gc_w1, gc_b1, gc_w2, gc_b2, gc_w3, gc_b3)
        out = x
        for _ in range(NUM_CYCLES):
            tf = _coupling_net(out, cn_w1, cn_b1, cn_w2, cn_b2, cn_w3, cn_b3, cn_w4, cn_b4)
            combined = 0.7 * gf + 0.3 * tf
            coupling = BASE_COUPLING + adaptive_range * (combined - 0.5) * 2.0
            out = out + coupling * _twist(out)
        return out
    x = L0_attn_a_x
    x = x + _L0_attn_a_ref(_layernorm(x, axis=-1), L0_attn_a_Wk, L0_attn_a_Wv, L0_attn_a_Wo, L0_attn_a_gate, L0_attn_a_freqs)
    x = x + _L0_ffn_ref(_layernorm(x, axis=-1), L0_ffn_cn_w1, L0_ffn_cn_b1, L0_ffn_cn_w2, L0_ffn_cn_b2, L0_ffn_cn_w3, L0_ffn_cn_b3, L0_ffn_cn_w4, L0_ffn_cn_b4, L0_ffn_gc_w1, L0_ffn_gc_b1, L0_ffn_gc_w2, L0_ffn_gc_b2, L0_ffn_gc_w3, L0_ffn_gc_b3, L0_ffn_adaptive_range)
    x = x + _L0_attn_b_ref(_layernorm(x, axis=-1), L0_attn_b_z_q, L0_attn_b_b_q, L0_attn_b_z_k, L0_attn_b_b_k, L0_attn_b_w_v, L0_attn_b_b_v)
    x = x + _L0_ffn_ref(_layernorm(x, axis=-1), L0_ffn_cn_w1, L0_ffn_cn_b1, L0_ffn_cn_w2, L0_ffn_cn_b2, L0_ffn_cn_w3, L0_ffn_cn_b3, L0_ffn_cn_w4, L0_ffn_cn_b4, L0_ffn_gc_w1, L0_ffn_gc_b1, L0_ffn_gc_w2, L0_ffn_gc_b2, L0_ffn_gc_w3, L0_ffn_gc_b3, L0_ffn_adaptive_range)
    return x

_drawn_inputs = setup_inputs


def setup_inputs(seed=0):
    import zlib

    import numpy as np

    out = dict(_drawn_inputs(seed))
    spreads = {'L0_attn_a_gate': (0.5, 0.2),
     'L0_ffn_cn_b1': (0.0, 0.8),
     'L0_ffn_cn_b2': (0.0, 0.8),
     'L0_ffn_cn_b3': (0.0, 0.8),
     'L0_ffn_gc_b1': (0.0, 0.8),
     'L0_ffn_gc_b2': (0.0, 0.8)}
    factors = {'L0_attn_b_z_q': 8.0,
     'L0_attn_b_b_q': 8.0,
     'L0_attn_b_z_k': 8.0,
     'L0_attn_b_b_k': 8.0,
     'L0_attn_b_b_v': 8.0,
     'L0_ffn_cn_w1': 4.796,
     'L0_ffn_cn_w2': 5.153,
     'L0_ffn_cn_w3': 3.933,
     'L0_ffn_cn_w4': 4.576,
     'L0_ffn_gc_w1': 7.173,
     'L0_ffn_gc_w2': 5.535,
     'L0_ffn_gc_w3': 6.102}
    for name, (base, spread) in spreads.items():
        noise = np.random.default_rng([zlib.crc32(name.encode()), seed]).standard_normal(out[name].shape)
        drawn = base * np.exp(spread * noise) if base else spread * noise
        out[name] = jnp.asarray(drawn.astype(out[name].dtype))
    for name, factor in factors.items():
        out[name] = (out[name] * factor).astype(out[name].dtype)
    return out
```

```python
from contextlib import ExitStack

import concourse.bass as bass
from concourse import mybir

F32 = mybir.dt.float32
I32 = mybir.dt.int32
BF16 = mybir.dt.bfloat16
ALU = mybir.AluOpType
ACT = mybir.ActivationFunctionType

P = 128
MAGIC = 12582912.0
TWO_PI = 6.283185307179586
TWO_PI_LOW = 6.2831849
PI_LOW = 3.1415925
EPS = 1e-5


class Scope:

    def __init__(self, nc, tag):
        self.nc, self.tag, self.ctx = nc, tag, ExitStack()

    def __enter__(self):
        self.ctx.__enter__()
        self.passed = self.sem("passed")
        return self

    def __exit__(self, *e):
        return self.ctx.__exit__(*e)

    def sb(self, name, shape, dt=F32):
        return self.ctx.enter_context(self.nc.sbuf_tensor(f"{self.tag}_{name}", shape, dt))

    def ps(self, name, shape, dt=F32):
        return self.ctx.enter_context(self.nc.psum_tensor(f"{self.tag}_{name}", shape, dt))

    def sem(self, name):
        return self.ctx.enter_context(self.nc.semaphore(f"{self.tag}_{name}"))


def make_identity(nc, pool, ident, done):
    nc.gpsimd.memset(ident[:], 0.0).then_inc(done, 1)
    pool.wait_ge(done, 1)
    nc.gpsimd.affine_select(out=ident[:], in_=ident[:], compare_op=ALU.not_equal, fill=1.0, base=0,
                            pattern=[[-1, P]], channel_multiplier=1).then_inc(done, 1)


def phase_a(nc, x_in, wk, wv, wo, gate, freqs, x_out):
    B, T, D = x_in.shape
    H, DH = freqs.shape
    HD = H * DH
    KD = D // P
    NT = T // P
    NC = HD // P
    HPT = P // DH
    HC = NC // 2
    NG = NT // 2
    TURN = 10.0 / TWO_PI
    C1 = 6.28125
    C2 = TWO_PI - C1
    xi = x_in.rearrange("b (t p) d -> b p t d", p=P)
    xo = x_out.rearrange("b (t p) d -> b p t d", p=P)

    with Scope(nc, "a") as s:
        passed = s.passed
        wk_sb = s.sb("wk", [P, KD, HD])
        wv_sb = s.sb("wv", [P, KD, HD])
        wo_sb = s.sb("wo", [P, NC, D])
        cos_t = s.sb("cos_t", [P, NC, T])
        sin_t = s.sb("sin_t", [P, NC, T])
        ident = s.sb("ident", [P, P])
        diag = s.sb("diag", [P, NT, P])
        freq = s.sb("freq", [P, NC])
        gates = s.sb("gates", [P, NC, 2])
        sm = s.sb("sm", [P, 8, NT])
        cst = s.sb("cst", [P, 4])
        stats = s.sb("stats", [P, NT, 6])
        mv = s.sb("mv", [P, NT, 2])
        xl = s.sb("xl", [P, NT, D])
        xr = s.sb("xr", [P, NT, D])
        xnT = s.sb("xnT", [P, KD, T])
        rnd = s.sb("rnd", [P, T])
        frac = s.sb("frac", [P, T])
        sin_k = s.sb("sin_k", [P, 2, T + 2])
        cos_k = s.sb("cos_k", [P, 2, T + 2])
        va = s.sb("va", [P, T])
        vp = s.sb("vp", [P, T])
        xs = s.sb("xs", [P, T])
        yc = s.sb("yc", [P, 2, T])
        ys = s.sb("ys", [P, T])
        out = s.sb("out", [P, NC, T])
        pu = s.ps("pu", [P, T])
        pv = s.ps("pv", [P, T])
        pt = s.ps("pt", [P, 2, 512])
        py = s.ps("py", [P, 2, 512])

        w_loaded = s.sem("w_loaded")
        id_done = s.sem("id_done")
        setup_p = s.sem("setup_p")
        setup_v = s.sem("setup_v")
        angle_done = s.sem("angle_done")
        wrap_done = s.sem("wrap_done")
        clamped = s.sem("clamped")
        setup_a = s.sem("setup_a")
        xl_loaded = s.sem("xl_loaded")
        stats_done = s.sem("stats_done")
        mv_done = s.sem("mv_done")
        rstd_done = s.sem("rstd_done")
        xn_done = s.sem("xn_done")
        xt_psum = s.sem("xt_psum")
        xt_done = s.sem("xt_done")
        u_psum = s.sem("u_psum")
        v_psum = s.sem("v_psum")
        rnd_done = s.sem("rnd_done")
        frac_done = s.sem("frac_done")
        abs_done = s.sem("abs_done")
        trig_done = s.sem("trig_done")
        va_done = s.sem("va_done")
        vp_done = s.sem("vp_done")
        xpre = s.sem("xpre")
        ypre = s.sem("ypre")
        xscan = s.sem("xscan")
        yscan = s.sem("yscan")
        xpost = s.sem("xpost")
        ypost = s.sem("ypost")
        unit_done = s.sem("unit_done")
        wo_psum = s.sem("wo_psum")
        wo_done = s.sem("wo_done")
        xr_loaded = s.sem("xr_loaded")
        stored = s.sem("stored")

        mean, var, ve, rstd, nmean = (sm[:, i, :] for i in range(5))
        tcol, root, iroot = sm[:, 5, :], sm[:, 6, :], sm[:, 7, :]
        wrap = ys
        N_W = 16 * (4 + HPT)
        N_SA = 3 * NC

        with nc.Block() as block:

            @block.sync
            def _(sp):
                sp.dma_start(freq[:], freqs.rearrange("(c a) d -> (a d) c", a=HPT), allow_slow_non_contiguous=True).then_inc(w_loaded, 16)
                sp.dma_start(wk_sb[:], wk.rearrange("(k p) n -> p k n", p=P)).then_inc(w_loaded, 16)
                gv = gate.rearrange("(c a) g -> a c g", a=HPT)
                for a in range(HPT):
                    sp.dma_start(gates[a * DH:(a + 1) * DH, :, :], gv[a:a + 1].broadcast_to([DH, NC, 2])).then_inc(w_loaded, 16)
                sp.dma_start(xl[:], xi[0]).then_inc(xl_loaded, 16)
                sp.dma_start(wv_sb[:], wv.rearrange("(k p) n -> p k n", p=P)).then_inc(w_loaded, 16)
                sp.dma_start(wo_sb[:], wo.rearrange("(c p) n -> p c n", p=P)).then_inc(w_loaded, 16)
                sp.dma_start(xr[:], xi[0]).then_inc(xr_loaded, 16 * 1)

                def batch(b, last=False):
                    sp.wait_ge(xt_psum, 4 * b + 4)
                    sp.sem_inc(passed, 1)
                    if last:
                        return
                    sp.dma_start(xl[:], xi[bass.ds(b + 1, 1)].rearrange("o p t d -> (o p) t d")).then_inc(xl_loaded, 16)
                    for g in range(NG):
                        sp.wait_ge(wo_done, 2 * NG * b + NG + g + 1)
                        sp.sem_inc(passed, 1)
                        sp.dma_start(xo[bass.ds(b, 1), :, 2 * g:2 * g + 2, :].rearrange("o p t d -> (o p) t d"),
                                     xr[:, 2 * g:2 * g + 2, :]).then_inc(stored, 16)
                        sp.wait_ge(stored, 16 * NG * b + 16 * (g + 1))
                        sp.sem_inc(passed, 1)
                        sp.dma_start(xr[:, 2 * g:2 * g + 2, :],
                                     xi[bass.ds(b + 1, 1), :, 2 * g:2 * g + 2, :].rearrange("o p t d -> (o p) t d")).then_inc(xr_loaded, 16)

                with sp.Fori(0, B - 1) as b:
                    batch(b)
                for g in range(NG):
                    sp.wait_ge(wo_done, 2 * NG * (B - 1) + NG + g + 1)
                    sp.sem_inc(passed, 1)
                    sp.dma_start(xo[B - 1, :, 2 * g:2 * g + 2, :], xr[:, 2 * g:2 * g + 2, :]).then_inc(stored, 16)
                sp.wait_ge(stored, 16 * NG * B)

            @block.gpsimd
            def _(pool):
                make_identity(nc, pool, ident, id_done)
                nc.gpsimd.iota(rnd[:].bitcast(I32), [[1, T]], base=0, channel_multiplier=0).then_inc(setup_p, 1)
                nc.gpsimd.iota(tcol.bitcast(I32), [[P, NT]], base=1, channel_multiplier=1).then_inc(setup_p, 1)
                nc.gpsimd.memset(cst[:, 0:1], MAGIC).then_inc(setup_p, 1)
                nc.gpsimd.memset(cst[:, 1:2], TWO_PI / 4).then_inc(setup_p, 1)
                nc.gpsimd.memset(cst[:, 2:3], 0.5).then_inc(setup_p, 1)
                nc.gpsimd.memset(cst[:, 3:4], -0.5).then_inc(setup_p, 1)
                for j in range(2):
                    nc.gpsimd.memset(sin_k[:, j, 0:1], 0.0).then_inc(setup_p, 1)
                    nc.gpsimd.memset(cos_k[:, j, 0:1], 0.0).then_inc(setup_p, 1)
                pool.wait_ge(setup_v, 2)
                pool.wait_ge(setup_p, 10)
                nc.gpsimd.tensor_tensor(root, ve, cst[:, 2:3].broadcast_to([P, NT]), ALU.pow).then_inc(setup_p, 1)
                nc.gpsimd.tensor_tensor(iroot, ve, cst[:, 3:4].broadcast_to([P, NT]), ALU.pow).then_inc(setup_p, 1)
                pool.wait_ge(setup_p, 12)
                pool.sem_inc(passed, 1)
                for t in range(NT):
                    nc.gpsimd.tensor_scalar(diag[:, t, :], ident[:], root[:, t:t + 1], None, ALU.mult).then_inc(setup_p, 1)

                def norm(b):
                    pool.wait_ge(mv_done, NT * b + NT)
                    if not isinstance(b, int) or b > 0:
                        pool.wait_ge(xn_done, NT * b)
                    pool.sem_inc(passed, 1)
                    nc.gpsimd.tensor_scalar(ve, mv[:, :, 1], EPS, None, ALU.add).then_inc(rstd_done, 1)
                    nc.gpsimd.tensor_scalar(nmean, mv[:, :, 0], -1.0, None, ALU.mult).then_inc(rstd_done, 1)
                    pool.wait_ge(rstd_done, 3 * b + 1)
                    nc.gpsimd.tensor_tensor(rstd, ve, cst[:, 3:4].broadcast_to([P, NT]), ALU.pow).then_inc(rstd_done, 1)
                    pool.wait_ge(rstd_done, 3 * b + 3)
                    pool.sem_inc(passed, 1)
                    for t in range(NT):
                        nc.gpsimd.tensor_scalar(xl[:, t, :], xl[:, t, :], nmean[:, t:t + 1], rstd[:, t:t + 1],
                                                ALU.add, ALU.mult).then_inc(xn_done, 1)

                def pre(n, c):
                    pool.wait_ge(vp_done, n + 1)
                    nc.gpsimd.tensor_tensor(yc[:, c % 2, :], vp[:], cos_t[:, c, :], ALU.mult).then_inc(ypre, 1)
                    nc.gpsimd.tensor_tensor(ys[:], vp[:], sin_t[:, c, :], ALU.mult).then_inc(ypre, 1)

                def post(n, c):
                    pool.wait_ge(yscan, 2 * n + 1)
                    nc.gpsimd.tensor_tensor(yc[:, c % 2, :], yc[:, c % 2, :], cos_t[:, c, :], ALU.mult).then_inc(ypost, 1)
                    pool.wait_ge(yscan, 2 * n + 2)
                    nc.gpsimd.tensor_tensor(ys[:], ys[:], sin_t[:, c, :], ALU.mult).then_inc(ypost, 1)
                    pool.wait_ge(ypost, 3 * n + 2)
                    nc.gpsimd.tensor_tensor(yc[:, c % 2, :], yc[:, c % 2, :], ys[:], ALU.add).then_inc(ypost, 1)
                    pool.wait_ge(ypost, 3 * n + 3)

                def batch(b, last=False):
                    for c in range(NC):
                        post(NC * b + c, c)
                        if not (last and c == NC - 1):
                            if c >= 1 or not isinstance(b, int) or b > 0:
                                pool.wait_ge(unit_done, NC * b + c)
                            pre(NC * b + c + 1, (c + 1) % NC)
                        if c == HC + 1 and not last:
                            norm(b + 1)

                for c in range(NC):
                    k = wrap[:]
                    pool.wait_ge(angle_done, c + 1)
                    if c >= 1:
                        pool.wait_ge(wrap_done, 3 * c)
                    pool.sem_inc(passed, 1)
                    nc.gpsimd.tensor_scalar(k, sin_t[:, c, :], 1.0 / TWO_PI, MAGIC, ALU.mult, ALU.add).then_inc(wrap_done, 1)
                    pool.wait_ge(wrap_done, 3 * c + 1)
                    pool.sem_inc(passed, 1)
                    nc.gpsimd.tensor_scalar(k, k, -MAGIC, -TWO_PI, ALU.add, ALU.mult).then_inc(wrap_done, 1)
                    pool.wait_ge(wrap_done, 3 * c + 2)
                    nc.gpsimd.tensor_tensor(sin_t[:, c, :], sin_t[:, c, :], k, ALU.add).then_inc(wrap_done, 1)
                    if c == 0:
                        norm(0)
                pool.wait_ge(wrap_done, 3 * NC)
                pool.wait_ge(setup_a, N_SA)
                pre(0, 0)
                batch(0)
                with pool.Fori(1, B - 1) as b:
                    batch(b)
                batch(B - 1, last=True)

            @block.vector
            def _(dve):
                def layernorm_stats(b):
                    dve.wait_ge(xl_loaded, 16 * b + 16)
                    if not isinstance(b, int) or b > 0:
                        dve.wait_ge(mv_done, NT * b)
                        dve.wait_ge(xn_done, NT * b)
                    for t in range(NT):
                        nc.vector.bn_stats(stats[:, t, :], xl[:, t, :]).then_inc(stats_done, 1)
                    dve.wait_ge(stats_done, NT * b + NT)
                    dve.sem_inc(passed, 1)
                    for t in range(NT):
                        nc.vector.bn_aggr(mv[:, t, :], stats[:, t, :]).then_inc(mv_done, 1)

                dve.wait_ge(setup_p, 2)
                nc.vector.tensor_copy(yc[:, 0, :], rnd[:].bitcast(I32)).then_inc(setup_v, 1)
                nc.vector.tensor_copy(ve, tcol.bitcast(I32)).then_inc(setup_v, 1)
                dve.wait_ge(w_loaded, N_W)
                nc.vector.tensor_scalar(wk_sb[:], wk_sb[:], TURN, None, ALU.mult).then_inc(setup_v, 1)
                dve.wait_ge(setup_v, 3)

                layernorm_stats(0)

                def clamp(c):
                    dve.wait_ge(wrap_done, 3 * c + 3)
                    nc.vector.tensor_scalar(sin_t[:, c, :], sin_t[:, c, :], PI_LOW, -PI_LOW, ALU.min, ALU.max).then_inc(clamped, 1)

                for c in range(NC):
                    th, k = sin_t[:, c, :], cos_t[:, c, :]
                    nc.vector.tensor_scalar(th, yc[:, 0, :], freq[:, c:c + 1], None, ALU.mult).then_inc(setup_v, 1)
                    dve.wait_ge(setup_v, 3 + 4 * c + 1)
                    nc.vector.tensor_scalar(k, th, 1.0 / TWO_PI, MAGIC, ALU.mult, ALU.add).then_inc(setup_v, 1)
                    dve.wait_ge(setup_v, 3 + 4 * c + 2)
                    nc.vector.tensor_scalar(k, k, MAGIC, -C1, ALU.subtract, ALU.mult).then_inc(setup_v, 1)
                    dve.wait_ge(setup_v, 3 + 4 * c + 3)
                    nc.vector.tensor_tensor(th, th, k, ALU.add).then_inc(setup_v, 1)
                    dve.wait_ge(setup_v, 3 + 4 * c + 4)
                    nc.vector.scalar_tensor_tensor(th, k, C2 / C1, th, ALU.mult, ALU.add).then_inc(angle_done, 1)
                    if c >= 1:
                        clamp(c - 1)
                clamp(NC - 1)

                def fraction(n):
                    dve.wait_ge(rnd_done, n + 1)
                    if not isinstance(n, int) or n > 0:
                        dve.wait_ge(trig_done, n)
                    nc.vector.scalar_tensor_tensor(frac[:], rnd[:], MAGIC, pu[:], ALU.subtract, ALU.subtract).then_inc(frac_done, 1)

                def finish(n, c):
                    dve.wait_ge(ypost, 3 * n + 3)
                    dve.wait_ge(xpost, 3 * n + 3)
                    nc.vector.tensor_tensor(out[:, c, :], out[:, c, :], yc[:, c % 2, :], ALU.add).then_inc(unit_done, 1)

                def step(n, c, first, last, free):
                    o = out[:, c, :]
                    if not last:
                        fraction(n + 1)
                    dve.wait_ge(trig_done, n + 1)
                    dve.wait_ge(va_done, n + 1)
                    if free is not None:
                        dve.wait_ge(wo_psum, free)
                    nc.vector.tensor_tensor(o, va[:], cos_k[:, c % 2, 0:T], ALU.mult).then_inc(xpre, 1)
                    nc.vector.tensor_tensor(xs[:], va[:], sin_k[:, c % 2, 0:T], ALU.mult).then_inc(xpre, 1)
                    if not first:
                        finish(n - 1, (c - 1) % NC)
                    dve.wait_ge(xpre, 2 * n + 1)
                    nc.vector.tensor_tensor_scan(o, o, o, 0.0, ALU.add, ALU.bypass).then_inc(xscan, 1)
                    dve.wait_ge(xpre, 2 * n + 2)
                    nc.vector.tensor_tensor_scan(xs[:], xs[:], xs[:], 0.0, ALU.add, ALU.bypass).then_inc(xscan, 1)
                    y = yc[:, c % 2, :]
                    dve.wait_ge(ypre, 2 * n + 1)
                    nc.vector.tensor_tensor_scan(y, y, y, 0.0, ALU.add, ALU.bypass).then_inc(yscan, 1)
                    dve.wait_ge(ypre, 2 * n + 2)
                    nc.vector.tensor_tensor_scan(ys[:], ys[:], ys[:], 0.0, ALU.add, ALU.bypass).then_inc(yscan, 1)
                    dve.wait_ge(xscan, 2 * n + 2)
                    nc.vector.tensor_tensor(o, o, cos_k[:, c % 2, 1:T + 1], ALU.mult).then_inc(xpost, 1)
                    nc.vector.tensor_tensor(xs[:], xs[:], sin_k[:, c % 2, 1:T + 1], ALU.mult).then_inc(xpost, 1)
                    dve.wait_ge(xpost, 3 * n + 2)
                    nc.vector.tensor_tensor(o, o, xs[:], ALU.add).then_inc(xpost, 1)
                    dve.wait_ge(xpost, 3 * n + 3)

                def batch(b, first=False, last=False):
                    for c in range(NC):
                        if c == HC + 1 and not last:
                            layernorm_stats(b + 1)
                        free = None
                        if not first and c in (0, HC):
                            free = 2 * NG * (b - 1) + (NG if c == 0 else 2 * NG)
                        step(NC * b + c, c, first and c == 0, last and c == NC - 1, free)

                fraction(0)
                batch(0, first=True)
                with dve.Fori(1, B - 1) as b:
                    batch(b)
                batch(B - 1, last=True)
                finish(NC * B - 1, NC - 1)

            @block.scalar
            def _(act):
                act.wait_ge(setup_p, 12)
                nc.scalar.preload_act_table(ACT.Sin)
                for c in range(NC):
                    th, k = sin_t[:, c, :], cos_t[:, c, :]
                    act.wait_ge(clamped, c + 1)
                    nc.scalar.activation(k, th, ACT.Abs).then_inc(setup_a, 1)
                    act.wait_ge(setup_a, 3 * c + 1)
                    nc.scalar.activation(k, k, ACT.Sin, bias=cst[:, 1:2], scale=-1.0).then_inc(setup_a, 1)
                    nc.scalar.activation(th, th, ACT.Sin).then_inc(setup_a, 1)

                def transposed(b):
                    for g in range(2 * KD):
                        act.wait_ge(xt_psum, 4 * b + g + 1)
                        if g == 0 and (not isinstance(b, int) or b > 0):
                            act.wait_ge(v_psum, NC * b)
                        f, h = g // 2, g % 2
                        nc.scalar.activation(xnT[:, f, h * 512:(h + 1) * 512], pt[:, g % 2, :], ACT.Copy).then_inc(xt_done, 1)

                def front(n, c, first=False):
                    act.wait_ge(u_psum, n + 1)
                    if not first:
                        act.wait_ge(trig_done, n)
                    nc.scalar.activation(rnd[:], pu[:], ACT.Identity, bias=cst[:, 0:1]).then_inc(rnd_done, 1)
                    act.wait_ge(v_psum, n + 1)
                    if not first:
                        act.wait_ge(xpre, 2 * n)
                    nc.scalar.activation(va[:], pv[:], ACT.Copy, scale=gates[:, c, 1:2]).then_inc(va_done, 1)
                    act.wait_ge(frac_done, n + 1)
                    nc.scalar.activation(rnd[:], frac[:], ACT.Abs).then_inc(abs_done, 1)
                    if not first:
                        act.wait_ge(ypre, 2 * n)
                    nc.scalar.activation(vp[:], pv[:], ACT.Copy, scale=gates[:, c, 0:1]).then_inc(vp_done, 1)
                    act.wait_ge(abs_done, n + 1)
                    nc.scalar.activation(cos_k[:, c % 2, 1:T + 1], rnd[:], ACT.Sin, bias=cst[:, 1:2], scale=-TWO_PI_LOW)
                    nc.scalar.activation(sin_k[:, c % 2, 1:T + 1], frac[:], ACT.Sin, scale=-TWO_PI_LOW).then_inc(trig_done, 1)

                def project_out(k, g):
                    act.wait_ge(wo_psum, k + 1)
                    for j in range(2):
                        t = 2 * g + j
                        i = nc.scalar.activation(xr[:, t, :], py[:, g % 2, j * D:(j + 1) * D], ACT.Copy, scale=iroot[:, t:t + 1])
                    i.then_inc(wo_done, 1)

                def batch(b, first=False, last=False):
                    for c in range(NC):
                        if c == NC - 1 and not last:
                            transposed(b + 1)
                        if not (last and c == NC - 1):
                            n = NC * b + c + 1
                            if c >= 1:
                                act.wait_ge(xpost, 3 * (n - 1) - 1)
                            elif not first:
                                act.wait_ge(xpost, 3 * (n - 1) - 1)
                            front(n, (c + 1) % NC)
                        if c >= HC:
                            project_out(2 * NG * b + c - HC, c - HC)
                        elif not first:
                            project_out(2 * NG * (b - 1) + NG + c, c)

                transposed(0)
                act.wait_ge(w_loaded, N_W)
                front(0, 0, first=True)
                batch(0, first=True)
                with act.Fori(1, B - 1) as b:
                    batch(b)
                batch(B - 1, last=True)
                for g in range(NG):
                    project_out(2 * NG * (B - 1) + NG + g, g)

            @block.tensor
            def _(pe):
                def transposes(b):
                    pe.wait_ge(xn_done, NT * b + NT)
                    for g in range(2 * KD):
                        f, h = g // 2, g % 2
                        if g >= 2 or not isinstance(b, int) or b > 0:
                            pe.wait_ge(xt_done, 4 * b + g - 1)
                        for j in range(4):
                            t = 4 * h + j
                            i = nc.tensor.transpose(pt[:, g % 2, j * P:(j + 1) * P], xl[:, t, f * P:(f + 1) * P], ident[:])
                        i.then_inc(xt_psum, 1)

                def project(n, c, first=False):
                    if not first:
                        pe.wait_ge(frac_done, n)
                    for h in range(2):
                        for k in range(KD):
                            i = nc.tensor.matmul(pu[:, h * 512:(h + 1) * 512], wk_sb[:, k, c * P:(c + 1) * P],
                                                 xnT[:, k, h * 512:(h + 1) * 512], start=k == 0, stop=k == KD - 1)
                    i.then_inc(u_psum, 1)
                    if not first:
                        pe.wait_ge(vp_done, n)
                    for h in range(2):
                        for k in range(KD):
                            i = nc.tensor.matmul(pv[:, h * 512:(h + 1) * 512], wv_sb[:, k, c * P:(c + 1) * P],
                                                 xnT[:, k, h * 512:(h + 1) * 512], start=k == 0, stop=k == KD - 1)
                    i.then_inc(v_psum, 1)

                def project_out(k, g, units, c0, x_loads, free):
                    pe.wait_ge(unit_done, units)
                    pe.wait_ge(xr_loaded, x_loads)
                    if free:
                        pe.wait_ge(wo_done, k - 1)
                    for j in range(2):
                        t = 2 * g + j
                        o = py[:, g % 2, j * D:(j + 1) * D]
                        nc.tensor.matmul(o, diag[:, t, :], xr[:, t, :], start=True, stop=False)
                        for c in range(c0, c0 + HC):
                            i = nc.tensor.matmul(o, out[:, c, t * P:(t + 1) * P], wo_sb[:, c, :], start=False, stop=c == c0 + HC - 1)
                    i.then_inc(wo_psum, 1)

                def batch(b, first=False, last=False):
                    for c in range(NC):
                        if c == NC - 1 and not last:
                            transposes(b + 1)
                            pe.wait_ge(xt_done, 4 * (b + 1) + 4)
                        if not (last and c == NC - 1):
                            project(NC * b + c + 1, (c + 1) % NC)
                        if c >= HC:
                            g = c - HC
                            loads = 16 if first else 16 + 16 * (NG * (b - 1) + g + 1)
                            project_out(2 * NG * b + g, g, NC * b + HC, 0, loads, not first or g >= 2)
                        elif not first:
                            project_out(2 * NG * (b - 1) + NG + c, c, NC * b, HC, 16, True)

                pe.wait_ge(id_done, 2)
                transposes(0)
                pe.wait_ge(xt_done, 4)
                pe.wait_ge(setup_v, 3)
                pe.wait_ge(w_loaded, N_W)
                project(0, 0, first=True)
                pe.wait_ge(setup_p, 12 + NT)
                batch(0, first=True)
                with pe.Fori(1, B - 1) as b:
                    batch(b)
                batch(B - 1, last=True)
                for g in range(NG):
                    project_out(2 * NG * (B - 1) + NG + g, g, NC * B, HC, 16, True)


def ffn_steps(first, last):
    late = "skip" if first else None
    early = "skip" if last else None
    out = []
    for k in range(3):
        out.append(("L1", 0, k))
        behind = (k + 2) % 3
        out.append((late if k == 0 and late else "L34", 1, behind))
        if k == 0:
            out.append((late or "outT", 0, None))
        if k == 1:
            out.append((early or "inT", 0, None))
        if k == 2 and not last:
            out.append(("G1", None, None))
        if k == 0:
            out.append(("G3", None, None))
        out.append(("L2", 0, k))
        out.append(("L1", 1, k))
        out.append(("L34", 0, k))
        if k == 0:
            out.append((late or "outT", 1, None))
            if not last:
                out.append(("LN", None, None))
        if k == 1:
            out.append((early or "inT", 1, None))
        if k == 2 and not last:
            out.append(("G2", None, None))
        out.append(("L2", 1, k))
    return out


def tiles_of(step, skipped_as):
    return {"L1": 4, "L2": 2, "L34": 3, "outT": 4, "inT": 4}.get(skipped_as if step == "skip" else step, 0)


def phase_f(nc, tag, x_in, x_out, cn, gc, arange):
    w1, b1, w2, b2, w3, b3, w4, b4 = cn
    gw1, gb1, gw2, gb2, gw3, gb3 = gc
    B, T, D = x_in.shape
    NT = T // P
    KD = D // P
    HT = 512
    NH = T // HT
    M3 = w3.shape[1]
    PAIRS = B // 2
    RING = 7
    TILES, ACT_TILES = 70, 62
    PRO = 2 * KD * NH
    xi = x_in.rearrange("b (t p) d -> b p t d", p=P)
    xo = x_out.rearrange("b (t p) d -> b p t d", p=P)

    with Scope(nc, tag) as s:
        passed = s.passed
        w1_sb = s.sb("w1", [P, KD, D])
        w2_sb = s.sb("w2", [P, KD, P])
        w3_sb = s.sb("w3", [P, M3])
        w4c = s.sb("w4c", [P, 1])
        w4r = s.sb("w4r", [P, 2, P])
        gw1_sb = s.sb("gw1", [P, KD, P])
        gw2_sb = s.sb("gw2", [P, M3])
        gw3c = s.sb("gw3c", [P, 1])
        gw3r = s.sb("gw3r", [P, P])
        b1_sb = s.sb("b1", [P, KD])
        b2_sb = s.sb("b2", [P, 1])
        b3_sb = s.sb("b3", [P, 1])
        gb1_sb = s.sb("gb1", [P, 1])
        gb2_sb = s.sb("gb2", [P, 1])
        sc = s.sb("sc", [P, 12])
        ident = s.sb("ident", [P, P])
        ones = s.sb("ones", [P, P])
        stats = s.sb("stats", [P, 2, NT, 6])
        mv = s.sb("mv", [P, 2, NT, 2])
        sm = s.sb("sm", [P, 3, 2, NT])
        mhalf = s.sb("mhalf", [P, 1])
        xl = s.sb("xl", [P, 2, NT, D])
        xr = s.sb("xr", [P, 2, NT, D])
        S = [s.sb(f"s{i}", [P, 2, KD, T]) for i in range(4)]
        h1 = s.sb("h1", [P, 2, KD, T])
        h2 = s.sb("h2", [P, 2, T])
        h3 = s.sb("h3", [P, 2, HT])
        th = s.sb("th", [P, 2, T])
        cs = s.sb("cs", [P, 2, T])
        sums = s.sb("sums", [P, 2 * KD, 2])
        gh1 = s.sb("gh1", [P, 2])
        gh2 = s.sb("gh2", [P, 2])
        thg = s.sb("thg", [P, 2])
        k2 = s.sb("k2", [P, 2])
        po = s.ps("po", [P, RING, HT])
        pg = s.ps("pg", [P, HT])
        ar, sign, k1, c07, c01, hb4, hgb3 = (sc[:, i:i + 1] for i in range(7))

        w_loaded = s.sem("w_loaded")
        setup_p = s.sem("setup_p")
        setup_v = s.sem("setup_v")
        xl_loaded = s.sem("xl_loaded")
        xr_loaded = s.sem("xr_loaded")
        stored = s.sem("stored")
        stats_done = s.sem("stats_done")
        mv_done = s.sem("mv_done")
        rstd_done = s.sem("rstd_done")
        xn_done = s.sem("xn_done")
        tile_ready = s.sem("tile_ready")
        act_done = s.sem("act_done")
        out_done = s.sem("out_done")
        g_psum = s.sem("g_psum")
        g_act = s.sem("g_act")
        k2_done = s.sem("k2_done")
        cs_done = [s.sem(f"cs_done{x}") for x in range(2)]
        a_done = [s.sem(f"a_done{x}") for x in range(2)]
        b_done = [s.sem(f"b_done{x}") for x in range(2)]
        state_done = [s.sem(f"state_done{x}") for x in range(2)]

        tile_at, act_at, out_at = {}, {}, {}
        plan, t0, a0, o0 = [], 0, 0, 0
        for step in ffn_steps(False, False):
            n = tiles_of(step[0], None)
            tile_at[step] = t0
            if step[0] == "outT":
                out_at[step] = o0
                o0 += n
            else:
                act_at[step] = a0
                a0 += n
            for i in range(n):
                plan.append(("v", out_at[step] + i) if step[0] == "outT" else ("a", act_at[step] + i))
            t0 += n
        assert (t0, a0, o0) == (TILES, ACT_TILES, 8) and TILES % RING == 0
        SKIPPED = {(1, 2): "L34", (0, None): None, (1, None): None}

        def real(step, x, k, at):
            if step != "skip":
                return step
            if k == 2:
                return "L34"
            return "outT" if at < TILES // 3 else "inT"

        with nc.Block() as block:
            N_W = 16 * 18

            @block.sync
            def _(sp):
                def col(v, lo=0):
                    return v.rearrange("(p o) -> p o", o=1)
                sp.dma_start(xl[:, 0], xi[0]).then_inc(xl_loaded, 16)
                sp.dma_start(xl[:, 1], xi[1]).then_inc(xl_loaded, 16)
                loads = [
                    (w1_sb[:], w1.rearrange("(k p) n -> p k n", p=P)),
                    (w2_sb[:], w2.rearrange("(k p) n -> p k n", p=P)),
                    (w3_sb[:], w3), (gw1_sb[:], gw1.rearrange("(k p) n -> p k n", p=P)), (gw2_sb[:], gw2),
                    (w4c[0:M3, :], w4), (w4c[M3:P, :], w4), (gw3c[0:M3, :], gw3),
                    (b1_sb[:, 0:1], col(b1[0:P])), (b1_sb[:, 1:2], col(b1[P:D])), (b2_sb[:], col(b2)),
                    (b3_sb[0:M3, :], col(b3)), (b3_sb[M3:P, :], col(b3)),
                    (gb1_sb[:], col(gb1)), (gb2_sb[0:M3, :], col(gb2)),
                    (ar, arange.rearrange("(a o) -> a o", o=1).broadcast_to([P, 1])),
                    (hb4, b4.rearrange("(a o) -> a o", o=1).broadcast_to([P, 1])),
                    (hgb3, gb3.rearrange("(a o) -> a o", o=1).broadcast_to([P, 1])),
                ]
                assert len(loads) * 16 == N_W
                for dst, src in loads:
                    sp.dma_start(dst, src).then_inc(w_loaded, 16)
                sp.dma_start(xr[:, 0], xi[0]).then_inc(xr_loaded, 16)
                sp.dma_start(xr[:, 1], xi[1]).then_inc(xr_loaded, 16)

                def dram(v, b):
                    return v[b] if isinstance(b, int) else v[bass.ds(b, 1)].rearrange("o p t d -> (o p) t d")

                def pair(j, first=False, last=False):
                    if not last:
                        for x in range(2):
                            if first:
                                sp.wait_ge(tile_ready, PRO)
                            else:
                                sp.wait_ge(tile_ready, PRO + TILES * (j - 1) + tile_at[("inT", x, None)] + 4)
                            sp.sem_inc(passed, 1)
                            sp.dma_start(xl[:, x], dram(xi, 2 * j + 2 + x)).then_inc(xl_loaded, 16)
                    if not first:
                        for x in range(2):
                            sp.wait_ge(out_done, 8 * j + 4 * x + 4)
                            sp.sem_inc(passed, 1)
                            sp.dma_start(dram(xo, 2 * j - 2 + x), xr[:, x]).then_inc(stored, 16)
                        for x in range(2):
                            sp.wait_ge(stored, 32 * j)
                            sp.sem_inc(passed, 1)
                            sp.dma_start(xr[:, x], dram(xi, 2 * j + x)).then_inc(xr_loaded, 16)

                pair(0, first=True)
                with sp.Fori(1, PAIRS - 1) as j:
                    pair(j)
                pair(PAIRS - 1, last=True)
                for x in range(2):
                    sp.wait_ge(out_done, 8 * PAIRS + 4 * x + 4)
                    sp.dma_start(xo[B - 2 + x], xr[:, x]).then_inc(stored, 16)
                sp.wait_ge(stored, 32 * PAIRS)

            @block.gpsimd
            def _(pool):
                make_identity(nc, pool, ident, setup_p)
                nc.gpsimd.memset(ones[:], 1.0).then_inc(setup_p, 1)
                nc.gpsimd.memset(mhalf[:], -0.5).then_inc(setup_p, 1)
                nc.gpsimd.memset(w4r[:], 0.0).then_inc(setup_p, 1)
                ve, rstd, nmean = (sm[:, i] for i in range(3))

                def norm(j):
                    pool.wait_ge(mv_done, 2 * NT * (j + 1))
                    if not isinstance(j, int) or j > 0:
                        pool.wait_ge(xn_done, 2 * NT * j)
                    pool.sem_inc(passed, 1)
                    nc.gpsimd.tensor_scalar(ve, mv[:, :, :, 1], EPS, None, ALU.add).then_inc(rstd_done, 1)
                    nc.gpsimd.tensor_scalar(nmean, mv[:, :, :, 0], -1.0, None, ALU.mult).then_inc(rstd_done, 1)
                    pool.wait_ge(rstd_done, 3 * j + 1)
                    nc.gpsimd.tensor_tensor(rstd, ve, mhalf[:].unsqueeze(2).broadcast_to([P, 2, NT]), ALU.pow).then_inc(rstd_done, 1)
                    pool.wait_ge(rstd_done, 3 * j + 3)
                    pool.sem_inc(passed, 1)
                    for x in range(2):
                        for t in range(NT):
                            nc.gpsimd.tensor_scalar(xl[:, x, t, :], xl[:, x, t, :], nmean[:, x, t:t + 1],
                                                    rstd[:, x, t:t + 1], ALU.add, ALU.mult).then_inc(xn_done, 1)

                def turn(x, k, j):
                    for h in range(NH):
                        c = slice(h * HT, (h + 1) * HT)
                        pool.wait_ge(cs_done[x], 6 * j + 2 * k + h + 1)
                        nc.gpsimd.tensor_tensor(S[k + 1][:, x, 1, c], cs[:, x, c], S[k][:, x, 0, c],
                                                ALU.mult).then_inc(b_done[x], 1)

                def pair(j, first=False, last=False):
                    for step, x, k in ffn_steps(first, last):
                        if step == "L34":
                            turn(x, k, j - 1 if (x, k) == (1, 2) else j)
                        if step == "LN":
                            norm(j + 1)

                norm(0)
                pair(0, first=True)
                with pool.Fori(1, PAIRS - 1) as j:
                    pair(j)
                pair(PAIRS - 1, last=True)
                turn(1, 2, PAIRS - 1)

            @block.vector
            def _(dve):
                def layernorm_stats(j):
                    dve.wait_ge(xl_loaded, 32 * (j + 1))
                    if not isinstance(j, int) or j > 0:
                        dve.wait_ge(mv_done, 2 * NT * j)
                        dve.wait_ge(xn_done, 2 * NT * j)
                    for x in range(2):
                        for t in range(NT):
                            nc.vector.bn_stats(stats[:, x, t, :], xl[:, x, t, :]).then_inc(stats_done, 1)
                    dve.wait_ge(stats_done, 2 * NT * (j + 1))
                    dve.sem_inc(passed, 1)
                    for x in range(2):
                        for t in range(NT):
                            nc.vector.bn_aggr(mv[:, x, t, :], stats[:, x, t, :]).then_inc(mv_done, 1)

                def turn(x, k, j, end=False):
                    for h in range(NH):
                        c = slice(h * HT, (h + 1) * HT)
                        n = 6 * j + 2 * k + h
                        src, dst = S[k], S[k + 1]
                        dve.wait_ge(act_done, PRO + ACT_TILES * (j + (1 if (x, k) == (1, 2) else 0)) + (0 if end else act_at[("L34", x, k)]) + 2 + h)
                        dve.wait_ge(k2_done, j + 1)
                        if not isinstance(n, int) or n > 0:
                            dve.wait_ge(state_done[x], n)
                        nc.vector.tensor_scalar(cs[:, x, c], th[:, x, c], k1, k2[:, x:x + 1], ALU.mult, ALU.add).then_inc(cs_done[x], 1)
                        dve.wait_ge(cs_done[x], n + 1)
                        nc.vector.tensor_tensor(dst[:, x, 0, c], cs[:, x, c], src[:, x, 1, c], ALU.mult).then_inc(a_done[x], 1)
                        dve.wait_ge(a_done[x], n + 1)
                        nc.vector.tensor_tensor(dst[:, x, 0, c], dst[:, x, 0, c], src[:, x, 0, c], ALU.add)
                        dve.wait_ge(b_done[x], n + 1)
                        nc.vector.tensor_tensor(dst[:, x, 1, c], src[:, x, 1, c], dst[:, x, 1, c], ALU.subtract).then_inc(state_done[x], 1)

                def residual(x, j, at):
                    dve.wait_ge(xr_loaded, 32 * j)
                    for g in range(4):
                        dve.wait_ge(tile_ready, PRO + TILES * j + at + g + 1)
                        v = xr[:, x, 2 * g:2 * g + 2, :].rearrange("p t d -> p (t d)")
                        nc.vector.tensor_tensor(v, v, po[:, (at + g) % RING, :], ALU.add).then_inc(out_done, 1)

                def coupling_base(j):
                    dve.wait_ge(g_act, 3 * (j + 1))
                    nc.vector.tensor_scalar(k2[:], thg[:], c07, c01, ALU.mult, ALU.add).then_inc(k2_done, 1)

                def pair(j, first=False, last=False):
                    at = 0
                    for step, x, k in ffn_steps(first, last):
                        kind = real(step, x, k, at)
                        if step == "L34":
                            turn(x, k, j - 1 if (x, k) == (1, 2) else j)
                        if step == "outT":
                            residual(x, j, at)
                        if step == "skip" and kind == "outT":
                            nc.vector.sem_inc(out_done, 4)
                        if step == "LN":
                            layernorm_stats(j + 1)
                        if step == "G3":
                            if not first:
                                dve.wait_ge(state_done[1], 6 * j)
                            coupling_base(j)
                        at += tiles_of(step, kind)

                layernorm_stats(0)
                nc.vector.memset(sign[0:M3, :], 1.0).then_inc(setup_v, 1)
                nc.vector.memset(sign[M3:P, :], -1.0).then_inc(setup_v, 1)
                dve.wait_ge(w_loaded, N_W)
                dve.wait_ge(setup_p, 5)
                dve.wait_ge(setup_v, 2)
                nc.vector.tensor_scalar(k1, sign, ar, 0.3, ALU.mult, ALU.mult).then_inc(setup_v, 1)
                nc.vector.tensor_scalar(c07, sign, ar, 0.7, ALU.mult, ALU.mult).then_inc(setup_v, 1)
                nc.vector.tensor_scalar(c01, sign, 0.1, None, ALU.mult).then_inc(setup_v, 1)
                nc.vector.tensor_scalar(hb4, hb4, 0.5, None, ALU.mult).then_inc(setup_v, 1)
                nc.vector.tensor_scalar(hgb3, hgb3, 0.5, None, ALU.mult).then_inc(setup_v, 1)
                for h in range(2):
                    r = slice(h * M3, (h + 1) * M3)
                    nc.vector.tensor_scalar(w4r[r, h, :], ones[r, :], w4c[r, :], None, ALU.mult).then_inc(setup_v, 1)
                nc.vector.tensor_scalar(gw3r[0:M3, :], ones[0:M3, :], gw3c[0:M3, :], None, ALU.mult).then_inc(setup_v, 1)
                dve.wait_ge(setup_v, 10)
                pair(0, first=True)
                with dve.Fori(1, PAIRS - 1) as j:
                    pair(j)
                pair(PAIRS - 1, last=True)
                turn(1, 2, PAIRS - 1, end=True)
                for x in range(2):
                    residual(x, PAIRS, 4 * x + 3)

            @block.scalar
            def _(act):
                nc.scalar.preload_act_table(ACT.Gelu)

                def gelu(dst, at, j, bias, rows=P):
                    pass

                def take(j, at):
                    act.wait_ge(tile_ready, PRO + TILES * j + at + 1)
                    return po[:, at % RING, :]

                def features(x, j, at, base=None):
                    for i in range(2 * KD):
                        f, h = i // 2, i % 2
                        act.wait_ge(tile_ready, (PRO + TILES * j + at if base is None else base) + i + 1)
                        nc.scalar.activation(S[0][:, x, f, h * HT:(h + 1) * HT], po[:, (at + i) % RING, :], ACT.Copy,
                                             accum_out=sums[:, i, x:x + 1]).then_inc(act_done, 1)

                def pair(j, first=False, last=False):
                    at = 0
                    for step, x, k in ffn_steps(first, last):
                        kind = real(step, x, k, at)
                        if step == "skip" and kind != "outT":
                            n = tiles_of(step, kind)
                            act.wait_ge(act_done, PRO + ACT_TILES * j + act_at[(kind, x, k)])
                            nc.scalar.sem_inc(act_done, n)
                        if step == "L1":
                            for i in range(4):
                                h, m = i // 2, i % 2
                                p = take(j, at + i)
                                nc.scalar.activation(h1[:, x, m, h * HT:(h + 1) * HT], p, ACT.Gelu, bias=b1_sb[:, m:m + 1]).then_inc(act_done, 1)
                        if step == "L2":
                            for h in range(2):
                                p = take(j, at + h)
                                nc.scalar.activation(h2[:, x, h * HT:(h + 1) * HT], p, ACT.Gelu, bias=b2_sb[:]).then_inc(act_done, 1)
                        if step == "L34":
                            p = take(j, at)
                            nc.scalar.activation(h3[:, x], p, ACT.Gelu, bias=b3_sb[:]).then_inc(act_done, 1)
                            jj = j - 1 if (x, k) == (1, 2) else j
                            for h in range(2):
                                p = take(j, at + 1 + h)
                                n = 6 * jj + 2 * k + h
                                if not isinstance(n, int) or n >= 2:
                                    act.wait_ge(cs_done[x], n - 1)
                                nc.scalar.activation(th[:, x, h * HT:(h + 1) * HT], p, ACT.Tanh, scale=0.5, bias=hb4).then_inc(act_done, 1)
                        if step == "inT":
                            act.wait_ge(state_done[x], 6 * j + 2)
                            features(x, j, at)
                        if step == "G1":
                            g_step(j + 1, 0)
                        if step == "G2":
                            g_step(j + 1, 1)
                        if step == "G3":
                            if not first:
                                act.wait_ge(k2_done, j)
                            g_step(j, 2)
                        at += tiles_of(step, kind)

                def g_step(j, i):
                    act.wait_ge(g_psum, 3 * j + i + 1)
                    if i == 0:
                        nc.scalar.activation(gh1[:], pg[:, 0:2], ACT.Gelu, scale=1.0 / T, bias=gb1_sb[:]).then_inc(g_act, 1)
                    if i == 1:
                        nc.scalar.activation(gh2[0:M3, :], pg[0:M3, 2:4], ACT.Gelu, bias=gb2_sb[0:M3, :]).then_inc(g_act, 1)
                    if i == 2:
                        nc.scalar.activation(thg[:], pg[:, 4:6], ACT.Tanh, scale=0.5, bias=hgb3).then_inc(g_act, 1)

                for x in range(2):
                    features(x, 0, TILES - PRO + 4 * x, base=4 * x)
                act.wait_ge(w_loaded, N_W)
                act.wait_ge(setup_v, 10)
                g_step(0, 0)
                g_step(0, 1)
                pair(0, first=True)
                with act.Fori(1, PAIRS - 1) as j:
                    pair(j)
                pair(PAIRS - 1, last=True)
                p = take(PAIRS, 0)
                nc.scalar.activation(h3[:, 1], p, ACT.Gelu, bias=b3_sb[:]).then_inc(act_done, 1)
                for h in range(2):
                    p = take(PAIRS, 1 + h)
                    act.wait_ge(cs_done[1], 6 * PAIRS - 3 + h)
                    nc.scalar.activation(th[:, 1, h * HT:(h + 1) * HT], p, ACT.Tanh, scale=0.5, bias=hb4).then_inc(act_done, 1)

            @block.tensor
            def _(pe):
                def free(j, at, first):
                    if at < RING:
                        if first:
                            return
                        who, n = plan[at - RING]
                        if who == "a":
                            pe.wait_ge(act_done, PRO + ACT_TILES * (j - 1) + n + 1)
                        else:
                            pe.wait_ge(out_done, 8 * (j - 1) + n + 1)
                    else:
                        who, n = plan[at - RING]
                        if who == "a":
                            pe.wait_ge(act_done, PRO + ACT_TILES * j + n + 1)
                        else:
                            pe.wait_ge(out_done, 8 * j + n + 1)
                    

                def l3(x, bank):
                    for h in range(2):
                        i = nc.tensor.matmul(po[h * M3:(h + 1) * M3, bank, :], w3_sb[:], h2[:, x, h * HT:(h + 1) * HT],
                                             start=True, stop=True, skip_group_check=True)
                    i.then_inc(tile_ready, 1)

                def l4(x, h, bank):
                    nc.tensor.matmul(po[:, bank, :], w4r[:, h, :], h3[:, x, :], start=True, stop=True).then_inc(tile_ready, 1)

                def in_tile(x, i, bank):
                    f, h = i // 2, i % 2
                    for q in range(4):
                        m = nc.tensor.transpose(po[:, bank, q * P:(q + 1) * P], xl[:, x, 4 * h + q, f * P:(f + 1) * P], ident[:])
                    m.then_inc(tile_ready, 1)

                def out_tile(x, g, bank):
                    for q in range(4):
                        t, f = 2 * g + q // 2, q % 2
                        m = nc.tensor.transpose(po[:, bank, q * P:(q + 1) * P], S[3][:, x, f, t * P:(t + 1) * P], ident[:])
                    m.then_inc(tile_ready, 1)

                def g_step(j, i):
                    if i == 0:
                        for q in range(2 * KD):
                            m = nc.tensor.matmul(pg[:, 0:2], gw1_sb[:, q // 2, :], sums[:, q, :], start=q == 0, stop=q == 2 * KD - 1)
                    if i == 1:
                        pe.wait_ge(g_act, 3 * j + 1)
                        m = nc.tensor.matmul(pg[0:M3, 2:4], gw2_sb[:], gh1[:], start=True, stop=True)
                    if i == 2:
                        pe.wait_ge(g_act, 3 * j + 2)
                        m = nc.tensor.matmul(pg[:, 4:6], gw3r[0:M3, :], gh2[0:M3, :], start=True, stop=True)
                    m.then_inc(g_psum, 1)

                def pair(j, first=False, last=False):
                    at = 0
                    for step, x, k in ffn_steps(first, last):
                        kind = real(step, x, k, at)
                        n = tiles_of(step, kind)
                        base = PRO + ACT_TILES * j
                        if step == "skip":
                            pe.wait_ge(tile_ready, PRO + TILES * j + at)
                            nc.tensor.sem_inc(tile_ready, n)
                        if step == "L1":
                            for i in range(4):
                                h, m = i // 2, i % 2
                                free(j, at + i, first)
                                if m == 0 and k > 0:
                                    pe.wait_ge(state_done[x], 6 * j + 2 * (k - 1) + h + 1)
                                if m == 0 and k == 0 and not first:
                                    pe.wait_ge(act_done, PRO + ACT_TILES * (j - 1) + act_at[("inT", x, None)] + 4)
                                for f in range(KD):
                                    q = nc.tensor.matmul(po[:, (at + i) % RING, :], w1_sb[:, f, m * P:(m + 1) * P],
                                                         S[k][:, x, f, h * HT:(h + 1) * HT], start=f == 0, stop=f == KD - 1)
                                q.then_inc(tile_ready, 1)
                        if step == "L2":
                            for h in range(2):
                                free(j, at + h, first)
                                pe.wait_ge(act_done, base + act_at[("L1", x, k)] + 2 * h + 2)
                                for f in range(KD):
                                    q = nc.tensor.matmul(po[:, (at + h) % RING, :], w2_sb[:, f, :],
                                                         h1[:, x, f, h * HT:(h + 1) * HT], start=f == 0, stop=f == KD - 1)
                                q.then_inc(tile_ready, 1)
                        if step == "L34":
                            free(j, at, first)
                            if (x, k) == (1, 2):
                                pe.wait_ge(act_done, PRO + ACT_TILES * (j - 1) + act_at[("L2", x, k)] + 2)
                            else:
                                pe.wait_ge(act_done, base + act_at[("L2", x, k)] + 2)
                            l3(x, at % RING)
                            for h in range(2):
                                free(j, at + 1 + h, first)
                                pe.wait_ge(act_done, base + act_at[("L34", x, k)] + 1)
                                l4(x, h, (at + 1 + h) % RING)
                        if step == "inT":
                            pe.wait_ge(xn_done, 2 * NT * (j + 1) + NT * (x + 1))
                            for i in range(4):
                                free(j, at + i, first)
                                in_tile(x, i, (at + i) % RING)
                        if step == "outT":
                            pe.wait_ge(state_done[x], 6 * j)
                            for i in range(4):
                                free(j, at + i, first)
                                out_tile(x, i, (at + i) % RING)
                        if step == "G1":
                            pe.wait_ge(act_done, base + act_at[("inT", 1, None)] + 4)
                            pe.wait_ge(g_act, 3 * (j + 1))
                            g_step(j + 1, 0)
                        if step == "G2":
                            g_step(j + 1, 1)
                        if step == "G3":
                            g_step(j, 2)
                        at += n

                pe.wait_ge(setup_p, 2)
                for x in range(2):
                    pe.wait_ge(xn_done, NT * (x + 1))
                    for i in range(4):
                        n = 4 * x + i
                        if n >= RING:
                            pe.wait_ge(act_done, n - RING + 1)
                        in_tile(x, i, (TILES - PRO + n) % RING)
                pe.wait_ge(act_done, PRO)
                pe.wait_ge(w_loaded, N_W)
                pe.wait_ge(setup_v, 10)
                g_step(0, 0)
                g_step(0, 1)
                pair(0, first=True)
                with pe.Fori(1, PAIRS - 1) as j:
                    pair(j)
                pair(PAIRS - 1, last=True)
                L = PAIRS - 1
                ab = PRO + ACT_TILES * PAIRS
                pe.wait_ge(act_done, ab)
                l3(1, 0)
                for h in range(2):
                    pe.wait_ge(act_done, ab + 1)
                    l4(1, h, 1 + h)
                for x in range(2):
                    pe.wait_ge(state_done[x], 6 * PAIRS)
                    for i in range(4):
                        at = 3 + 4 * x + i
                        if at >= RING:
                            pe.wait_ge(act_done, ab + 3)
                            if at - RING >= 3:
                                pe.wait_ge(out_done, 8 * PAIRS + at - RING - 3 + 1)
                        out_tile(x, i, at % RING)


Q_PART = [0, 0, 0, 1, 1, 1, 2, 2]
K_PART = [0, 1, 2, 0, 1, 2, 0, 1]


STEPS = {
    1: [("v", 3, 0), ("inT", 0, 1)],
    2: [("out", 3, -1), ("inT", 1, 1), ("lamb", 0, 1)],
    3: [("proj", 0, 1)], 5: [("proj", 1, 1), ("root", 0, 1)], 6: [("y", 0, 1)],
    7: [("proj", 2, 1), ("root", 1, 1), ("ln", 0, 1)], 8: [("exp", 0, 1), ("y", 1, 1)],
    9: [("sign", 0, 1), ("proj", 3, 1), ("root", 2, 1), ("ln", 1, 1)],
    10: [("out", 0, 0), ("exp", 1, 1), ("y", 2, 1)], 11: [("sign", 1, 1), ("root", 3, 1), ("ln", 2, 1)],
    12: [("exp", 2, 1), ("y", 3, 1)], 13: [("sign", 2, 1), ("ln", 3, 1), ("pair", 0, 1)],
    14: [("exp", 3, 1)], 15: [("sign", 3, 1), ("sum", 0, 1)], 16: [("pair", 1, 1)], 17: [("sum", 1, 1)],
    18: [("out", 1, 0), ("fac", 0, 1)], 20: [("facb", 0, 1)],
    21: [("facb", 1, 1), ("split", 0, 1)], 22: [("split", 2, 1)], 23: [("split", 1, 1)],
    25: [("split", 3, 1)], 26: [("out", 2, 0)], 27: [("v", 0, 1), ("stats", 0, 2)],
    28: [("rstd", 0, 2)], 29: [("v", 1, 1), ("lam", 0, 2)], 31: [("v", 2, 1)]}
PROLOGUE = [(step[:-1], int(step[-1]), 0) for step in (
    "stats0 rstd0 lam0 inT0 inT1 lamb0 proj0 proj1 proj2 proj3 root0 root1 v0 y0 ln0 root2 y1 v1 exp0 ln1 root3 "
    "y2 v2 exp1 sign0 ln2 y3 v3 exp2 sign1 ln3 exp3 sign2 pair0 sum0 sign3 pair1 sum1 fac0 facb0 facb1 "
    "split0 split2 split1 split3").split()] + [("stats", 0, 1), ("rstd", 0, 1), ("lam", 0, 1)]
N_TILES = {"inT": 2, "lamb": 2, "proj": 2, "v": 1, "sum": 1, "facb": 2, "out": 2}


def steps_at(blk, first, left):
    return [(kind, i, off) for kind, i, off in STEPS.get(blk, [])
            if off <= left and not (first and (kind, i) in (("out", 3), ("v", 3)))]


def phase_b(nc, x_in, x_out, zq, bq, zk, bk, wvT, bv):
    B, T, D = x_in.shape
    NT, KD, DK = T // P, D // P, 16
    H = D // DK
    V1 = DK + 1
    G = H // 4
    scratch = nc.dram_tensor("b_scratch", [2, 3, D, T], BF16, kind="Internal").ap()
    BLK = G * NT
    SC = 0.25
    STAGE = len(Q_PART)
    xi = x_in.rearrange("b (t p) d -> b p t d", p=P)
    xo = x_out.rearrange("b (t p) d -> b p t d", p=P)

    with Scope(nc, "b") as s:
        passed = s.passed
        z_sb = s.sb("z", [P, 2, KD, D])
        wv_sb = s.sb("wv", [P, KD, D])
        bvb = s.sb("bvb", [P, D])
        ident = s.sb("ident", [P, P])
        ones = s.sb("ones", [P, P])
        cst = s.sb("cst", [P, 4])
        cols = s.sb("cols", [P, 8, 4])
        stats = s.sb("stats", [P, NT, 6])
        mv = s.sb("mv", [P, NT, 2])
        sm = s.sb("sm", [P, 6, NT])
        fs = s.sb("fs", [P, 3, 2, NT])
        rec = s.sb("rec", [P, 4, 4])
        tmp = s.sb("tmp", [P, 4, 4, DK])
        xl = s.sb("xl", [P, NT, D])
        xr = s.sb("xr", [P, NT, D])
        xnT = s.sb("xnT", [P, KD, T])
        lamb = s.sb("lamb", [P, T])
        dg = s.sb("dg", [P, 2, NT, P])
        A = s.sb("A", [P, 4, T])
        SQ = s.sb("SQ", [P, 4, T])
        EP = s.sb("EP", [P, 2, T])
        vaug = s.sb("vaug", [P, NT, H * V1 + 32 - V1])
        parts = s.sb("parts", [P, 2, 3, KD, T], BF16)
        st = s.sb("st", [P, 2, 2, 4, T], BF16)
        pr = s.sb("pr", [P, 8, T])
        osb = s.sb("osb", [P, T])
        ps = s.ps("ps", [P, 2, T])
        acc = s.ps("acc", [P, T])
        pm = s.ps("pm", [P, 2, 512])
        ve, rstd, nmean, l1, lam, var2 = (sm[:, i, :] for i in range(6))
        rcol, znc, tanh2, ep2, em2, kap, sh, zt = (cols[:, i, :] for i in range(8))
        zn2, zn2m = cols[:, 3, :], cols[:, 4, :]

        names = ("w_loaded setup_p setup_v setup_a setup_m xl_loaded xr_loaded stored stats_done mv_done rstd_done "
                 "xn_done lam_done dlam_done misc_ready misc_taken inT_done a_done sq_done root_done abs_done y_done ln_done e_done "
                 "d_done sign_done d2_done pair_done fsum_done froot_done fac_done dfac_done split_done parts_done "
                 "scores_ready probs_done pv_done acc_taken vaug_done out_mul out_step").split()
        S = {n: s.sem(n) for n in names}
        parts_stored = [s.sem(f"parts_stored{f}") for f in range(KD)]
        st_loaded = [s.sem(f"st_loaded{i}") for i in range(2)]
        N_W = 16 * 8
        N_G = 16 * 16

        PRO = sum(N_TILES.get(kind, 0) for kind, _, _ in PROLOGUE)
        TILES = sum(N_TILES.get(kind, 0) for blk in range(BLK) for kind, _, _ in STEPS.get(blk, []))
        LATE = N_TILES["out"] + N_TILES["v"]

        LAST = sum(N_TILES.get(kind, 0) for blk in range(BLK) for kind, _, off in STEPS.get(blk, []) if off > 0)

        def misc_base(b, first):
            return (PRO, PRO % 2) if first else (PRO - LATE + TILES * b, (PRO - LATE) % 2)

        def store_parts(sp, b, f):
            sp.wait_ge(S["parts_done"], 4 * b + 2 * f + 2)
            if not (isinstance(b, int) and b == 0):
                sp.sem_inc(passed, 1)
            for o in range(2):
                sp.dma_start(scratch[o, :, f * P:(f + 1) * P].rearrange("w p t -> p w t"), parts[:, o, :, f, :])\
                    .then_inc(parts_stored[f], 16)

        def gather(sp, b, g):
            slot = g % 2
            for o, part in enumerate((Q_PART, K_PART)):
                for i0, n in ((0, 3), (3, 3), (6, 2)):
                    if o == 0:
                        w, rows = part[i0], DK
                        for r in range(n):
                            sp.dma_start(st[(i0 + r) * DK:(i0 + r + 1) * DK, slot, o],
                                         scratch[o, w, 64 * g:64 * g + 64, :].rearrange("(h d) t -> d h t", d=DK))\
                                .then_inc(st_loaded[slot], 16)
                    else:
                        for r in range(n):
                            sp.dma_start(st[(i0 + r) * DK:(i0 + r + 1) * DK, slot, o],
                                         scratch[o, r, 64 * g:64 * g + 64, :].rearrange("(h d) t -> d h t", d=DK))\
                                .then_inc(st_loaded[slot], 16)

        with nc.Block() as block:

            @block.sync
            def _(sp):
                def col(v):
                    return v.rearrange("(c p) -> p c", p=P)
                sp.dma_start(xl[:], xi[0]).then_inc(S["xl_loaded"], 16)
                for o, z in enumerate((zq, zk)):
                    sp.dma_start(z_sb[:, o], z.rearrange("(k p) n -> p k n", p=P)).then_inc(S["w_loaded"], 16)
                for o, r in enumerate((bq, bk)):
                    for f in range(KD):
                        sp.dma_start(rcol[:, 2 * o + f:2 * o + f + 1],
                                     r[f * P:(f + 1) * P].rearrange("(p o) -> p o", o=1)).then_inc(S["w_loaded"], 16)
                sp.dma_start(wv_sb[:], wvT.rearrange("(k p) n -> p k n", p=P)).then_inc(S["w_loaded"], 16)
                sp.dma_start(bvb[:], bv.rearrange("(o n) -> o n", o=1).broadcast_to([P, D])).then_inc(S["w_loaded"], 16)
                sp.dma_start(xr[:], xi[0]).then_inc(S["xr_loaded"], 16)
                sp.wait_ge(S["inT_done"], 1)
                sp.dma_start(xl[:], xi[1]).then_inc(S["xl_loaded"], 16)
                store_parts(sp, 0, 0)
                sp.wait_ge(parts_stored[0], 32)
                gather(sp, 0, 0)
                store_parts(sp, 0, 1)
                gather(sp, 0, 1)

                def dram(v, b):
                    return v[b] if isinstance(b, int) else v[bass.ds(b, 1)].rearrange("o p t d -> (o p) t d")

                def batch(b, first=False, left=2):
                    if not first:
                        sp.wait_ge(S["out_step"], 8 * b)
                        sp.sem_inc(passed, 1)
                        sp.dma_start(dram(xo, b - 1), xr[:]).then_inc(S["stored"], 16)
                        sp.wait_ge(S["stored"], 16 * b)
                        sp.sem_inc(passed, 1)
                        sp.dma_start(xr[:], dram(xi, b)).then_inc(S["xr_loaded"], 16)
                    if left > 1:
                        sp.wait_ge(S["inT_done"], b + 2)
                        sp.sem_inc(passed, 1)
                        sp.dma_start(xl[:], dram(xi, b + 2)).then_inc(S["xl_loaded"], 16)
                    sp.wait_ge(parts_stored[1], 32 * (b + 1))
                    if not first:
                        sp.sem_inc(passed, 1)
                    for g in (2, 3):
                        sp.wait_ge(S["scores_ready"], 4 * BLK * b + 32 * (g - 1))
                        sp.sem_inc(passed, 1)
                        gather(sp, b, g)
                    if left > 0:
                        for q in range(2):
                            sp.wait_ge(st_loaded[q], 2 * N_G * (b + 1))
                            sp.sem_inc(passed, 1)
                        store_parts(sp, b + 1, 0)
                        sp.wait_ge(parts_stored[0], 32 * (b + 2))
                        sp.sem_inc(passed, 1)
                        sp.wait_ge(S["scores_ready"], 4 * BLK * b + 32 * 3)
                        sp.sem_inc(passed, 1)
                        gather(sp, b + 1, 0)
                        store_parts(sp, b + 1, 1)
                        sp.wait_ge(S["scores_ready"], 4 * BLK * b + 32 * 4)
                        sp.sem_inc(passed, 1)
                        gather(sp, b + 1, 1)

                batch(0, first=True)
                with sp.Fori(1, B - 2) as b:
                    batch(b)
                batch(B - 2, left=1)
                batch(B - 1, left=0)
                sp.wait_ge(S["out_step"], 8 * B)
                sp.dma_start(xo[B - 1], xr[:]).then_inc(S["stored"], 16)
                sp.wait_ge(S["stored"], 16 * B)

            @block.gpsimd
            def _(pool):
                make_identity(nc, pool, ident, S["setup_p"])
                nc.gpsimd.memset(ones[:], 1.0).then_inc(S["setup_p"], 1)
                nc.gpsimd.memset(cst[:, 0:1], -0.5).then_inc(S["setup_p"], 1)
                nc.gpsimd.memset(cst[:, 1:2], 0.5).then_inc(S["setup_p"], 1)
                nc.gpsimd.memset(cst[:, 2:3], 0.25).then_inc(S["setup_p"], 1)
                nc.gpsimd.memset(cst[:, 3:4], 1.0).then_inc(S["setup_p"], 1)
                nc.gpsimd.memset(vaug[:], 1.0).then_inc(S["setup_p"], 1)
                pool.wait_ge(S["setup_v"], 2)
                nc.gpsimd.tensor_tensor(znc, znc, cst[:, 1:2].broadcast_to([P, 4]), ALU.pow).then_inc(S["setup_p"], 1)

                def again(b):
                    return not isinstance(b, int) or b > 0

                def step(kind, i, b):
                    if kind == "rstd":
                        pool.wait_ge(S["mv_done"], NT * b + NT)
                        if again(b):
                            pool.wait_ge(S["xn_done"], NT * b)
                            pool.wait_ge(S["lam_done"], 5 * b)
                        pool.sem_inc(passed, 1)
                        nc.gpsimd.tensor_scalar(ve, mv[:, :, 1], EPS, None, ALU.add).then_inc(S["rstd_done"], 1)
                        nc.gpsimd.tensor_scalar(nmean, mv[:, :, 0], -1.0, None, ALU.mult).then_inc(S["rstd_done"], 1)
                        pool.wait_ge(S["rstd_done"], 3 * b + 1)
                        nc.gpsimd.tensor_tensor(rstd, ve, cst[:, 0:1].broadcast_to([P, NT]), ALU.pow).then_inc(S["rstd_done"], 1)
                        pool.wait_ge(S["rstd_done"], 3 * b + 3)
                        pool.sem_inc(passed, 1)
                        for t in range(NT):
                            nc.gpsimd.tensor_scalar(xl[:, t, :], xl[:, t, :], nmean[:, t:t + 1], rstd[:, t:t + 1],
                                                    ALU.add, ALU.mult).then_inc(S["xn_done"], 1)
                    if kind == "lam":
                        pool.wait_ge(S["lam_done"], 5 * b + 5)
                        if again(b):
                            pool.wait_ge(S["parts_done"], 4 * b)
                            pool.wait_ge(S["dfac_done"], 2 * NT * b)
                        pool.sem_inc(passed, 1)
                        for t in range(NT):
                            nc.gpsimd.tensor_scalar(dg[:, 0, t, :], ident[:], lam[:, t:t + 1], 0.0, ALU.mult, ALU.add).then_inc(S["dlam_done"], 1)
                    if kind == "proj":
                        pool.wait_ge(S["a_done"], 4 * b + i + 1)
                        nc.gpsimd.tensor_tensor(SQ[:, i, :], A[:, i, :], A[:, i, :], ALU.mult).then_inc(S["sq_done"], 1)
                    if kind == "exp":
                        pool.wait_ge(S["e_done"], 4 * b + i + 1)
                        nc.gpsimd.tensor_tensor(SQ[:, i, :], EP[:, i % 2, :], SQ[:, i, :], ALU.subtract).then_inc(S["d_done"], 1)
                    if kind == "sign":
                        pool.wait_ge(S["sign_done"], 4 * b + i + 1)
                        nc.gpsimd.tensor_tensor(A[:, i, :], SQ[:, i, :], SQ[:, i, :], ALU.mult).then_inc(S["d2_done"], 1)
                    if kind == "pair":
                        pool.wait_ge(S["d2_done"], 4 * b + 2 * i + 2)
                        nc.gpsimd.tensor_tensor(A[:, 2 * i, :], A[:, 2 * i, :], A[:, 2 * i + 1, :], ALU.add)\
                            .then_inc(S["pair_done"], 1)
                    if kind == "fac":
                        pool.wait_ge(S["fsum_done"], 2 * b + 2)
                        nc.gpsimd.tensor_tensor(fs[:, 1], fs[:, 0], cst[:, 1:2].unsqueeze(2).broadcast_to([P, 2, NT]),
                                                ALU.pow).then_inc(S["froot_done"], 1)
                        pool.wait_ge(S["fac_done"], 3 * b + 3)
                        pool.wait_ge(S["dlam_done"], NT * b + NT)
                        pool.sem_inc(passed, 1)
                        for o in range(2):
                            for t in range(NT):
                                nc.gpsimd.tensor_scalar(dg[:, o, t, :], ident[:], fs[:, 2, o, t:t + 1], None,
                                                        ALU.mult).then_inc(S["dfac_done"], 1)

                def batch(b, first=False, left=2):
                    for blk in range(BLK):
                        for kind, i, off in steps_at(blk, first, left):
                            step(kind, i, b + off)

                for kind, i, off in PROLOGUE:
                    step(kind, i, off)
                batch(0, first=True)
                with pool.Fori(1, B - 2) as b:
                    batch(b)
                batch(B - 2, left=1)

            @block.vector
            def _(dve):
                def again(b):
                    return not isinstance(b, int) or b > 0

                def tile(m):
                    dve.wait_ge(S["misc_ready"], m + 1)

                def step(kind, i, b, m, par):
                    if kind == "stats":
                        dve.wait_ge(S["xl_loaded"], 16 * b + 16)
                        if again(b):
                            dve.wait_ge(S["lam_done"], 5 * b)
                            dve.wait_ge(S["xn_done"], NT * b)
                        for t in range(NT):
                            nc.vector.bn_stats(stats[:, t, :], xl[:, t, :]).then_inc(S["stats_done"], 1)
                        dve.wait_ge(S["stats_done"], NT * b + NT)
                        dve.sem_inc(passed, 1)
                        for t in range(NT):
                            nc.vector.bn_aggr(mv[:, t, :], stats[:, t, :]).then_inc(S["mv_done"], 1)
                    if kind == "lam":
                        dve.wait_ge(S["rstd_done"], 3 * b + 3)
                        dve.wait_ge(S["mv_done"], NT * b + NT)
                        if again(b):
                            dve.wait_ge(S["dlam_done"], NT * b)
                        nc.vector.tensor_tensor(l1, rstd, rstd, ALU.mult).then_inc(S["lam_done"], 1)
                        dve.wait_ge(S["lam_done"], 5 * b + 1)
                        nc.vector.tensor_tensor(var2, l1, mv[:, :, 1], ALU.mult).then_inc(S["lam_done"], 1)
                        dve.wait_ge(S["lam_done"], 5 * b + 2)
                        nc.vector.tensor_scalar(l1, var2, -float(D), 1.0, ALU.mult, ALU.add).then_inc(S["lam_done"], 1)
                        dve.wait_ge(S["lam_done"], 5 * b + 3)
                        nc.vector.reciprocal(var2, l1).then_inc(S["lam_done"], 1)
                        dve.wait_ge(S["lam_done"], 5 * b + 4)
                        nc.vector.tensor_scalar(lam, var2, 2.0, None, ALU.mult).then_inc(S["lam_done"], 1)
                    if kind == "inT":
                        for h in range(2):
                            tile(m + h)
                            nc.vector.tensor_copy(xnT[:, i, h * 512:(h + 1) * 512], pm[:, (par + h) % 2, :]).then_inc(S["misc_taken"], 1)
                    if kind == "lamb":
                        for h in range(2):
                            tile(m + h)
                            if again(b) and h == 0:
                                dve.wait_ge(S["a_done"], 4 * b)
                            nc.vector.tensor_copy(lamb[:, h * 512:(h + 1) * 512], pm[:, (par + h) % 2, :]).then_inc(S["misc_taken"], 1)
                        dve.wait_ge(S["misc_taken"], m + 2)
                    if kind == "proj":
                        if again(b):
                            dve.wait_ge(S["pair_done"], 2 * b)
                        for h in range(2):
                            tile(m + h)
                            c = slice(h * 512, (h + 1) * 512)
                            nc.vector.scalar_tensor_tensor(A[:, i, c], pm[:, (par + h) % 2, :], zt[:, i:i + 1], lamb[:, c],
                                                           ALU.subtract, ALU.mult).then_inc(S["misc_taken"], 1)
                        dve.wait_ge(S["misc_taken"], m + 2)
                        nc.vector.tensor_scalar(A[:, i, :], A[:, i, :], kap[:, i:i + 1], sh[:, i:i + 1], ALU.mult, ALU.add)\
                            .then_inc(S["a_done"], 1)
                    if kind == "y":
                        spare = EP[:, i % 2, :]
                        if i >= 2:
                            dve.wait_ge(S["d_done"], 4 * b + i - 1)
                        elif again(b):
                            dve.wait_ge(S["d_done"], 4 * b)
                        nc.vector.tensor_scalar(spare.bitcast(I32), A[:, i, :].bitcast(I32), 2147483647, None,
                                                ALU.bitwise_and).then_inc(S["abs_done"], 1)
                        dve.wait_ge(S["root_done"], 8 * b + 2 * i + 2)
                        dve.wait_ge(S["abs_done"], 4 * b + i + 1)
                        nc.vector.tensor_tensor(SQ[:, i, :], spare, SQ[:, i, :], ALU.add).then_inc(S["y_done"], 1)
                    if kind == "sign":
                        dve.wait_ge(S["d_done"], 4 * b + i + 1)
                        nc.vector.scalar_tensor_tensor(SQ[:, i, :].bitcast(I32), A[:, i, :].bitcast(I32), -2147483648,
                                                       SQ[:, i, :].bitcast(I32), ALU.bitwise_and, ALU.bitwise_or)\
                            .then_inc(S["sign_done"], 1)
                    if kind == "v":
                        tile(m)
                        if again(b):
                            dve.wait_ge(S["pv_done"], 2 * (BLK * b - NT + 2 * i + 2))
                        for t in range(2):
                            nc.vector.tensor_tensor(vaug[:, 2 * i + t, 0:H * V1].rearrange("p (h c) -> p h c", c=V1)[:, :, 0:DK],
                                                    pm[:, par % 2, t * D:(t + 1) * D].rearrange("p (h c) -> p h c", c=DK),
                                                    bvb[:].rearrange("p (h c) -> p h c", c=DK), ALU.add).then_inc(S["vaug_done"], 1)
                        dve.wait_ge(S["vaug_done"], 8 * b + 2 * i + 2)
                        nc.vector.sem_inc(S["misc_taken"], 1)
                    if kind == "sum":
                        tile(m)
                        if again(b):
                            dve.wait_ge(S["froot_done"], b)
                        nc.vector.tensor_scalar(fs[:, 0, i, :], pm[:, par % 2, 0:NT], 1.0, None, ALU.add).then_inc(S["fsum_done"], 1)
                        dve.wait_ge(S["fsum_done"], 2 * b + i + 1)
                        nc.vector.sem_inc(S["misc_taken"], 1)
                    if kind == "fac":
                        dve.wait_ge(S["froot_done"], b + 1)
                        if again(b):
                            dve.wait_ge(S["dfac_done"], 2 * NT * b)
                        nc.vector.tensor_scalar(fs[:, 1], fs[:, 1], 2.0, 2.0, ALU.mult, ALU.add).then_inc(S["fac_done"], 1)
                        dve.wait_ge(S["fac_done"], 3 * b + 1)
                        nc.vector.reciprocal(fs[:, 2], fs[:, 1]).then_inc(S["fac_done"], 2)
                    if kind == "facb":
                        for h in range(2):
                            tile(m + h)
                            c = slice(h * 512, (h + 1) * 512)
                            v = SQ[:, 2 * i:2 * i + 2, c]
                            nc.vector.tensor_tensor(v, v, pm[:, (par + h) % 2, :].unsqueeze(1).broadcast_to([P, 2, 512]),
                                                    ALU.mult).then_inc(S["misc_taken"], 1)
                        dve.wait_ge(S["misc_taken"], m + 2)
                    if kind == "split":
                        if again(b):
                            dve.wait_ge(parts_stored[i % 2], 32 * b)
                        q = SQ[:, i, :]
                        p1, p2, p3 = (parts[:, i // 2, w, i % 2, :] for w in range(3))
                        n = 16 * b + 4 * (2 * (i % 2) + i // 2)
                        nc.vector.tensor_copy(p1, q).then_inc(S["split_done"], 1)
                        dve.wait_ge(S["split_done"], n + 1)
                        nc.vector.tensor_tensor(q, q, p1, ALU.subtract).then_inc(S["split_done"], 1)
                        dve.wait_ge(S["split_done"], n + 2)
                        nc.vector.tensor_copy(p2, q).then_inc(S["split_done"], 1)
                        dve.wait_ge(S["split_done"], n + 3)
                        nc.vector.tensor_tensor(p3, q, p2, ALU.subtract).then_inc(S["split_done"], 1)
                        dve.wait_ge(S["split_done"], n + 4)
                        nc.vector.sem_inc(S["parts_done"], 1)

                def take_acc(grp, h):
                    dve.wait_ge(S["pv_done"], 2 * (NT * grp + NT) - 1 + h)
                    if again(grp):
                        dve.wait_ge(S["out_step"], 2 * grp)
                    c = slice(h * 512, (h + 1) * 512)
                    nc.vector.tensor_copy(osb[:, c], acc[:, c]).then_inc(S["acc_taken"], 1)

                def out(grp, g, b, m, par):
                    dve.wait_ge(S["xr_loaded"], 16 * (b + 1))
                    for h in range(2):
                        tile(m + h)
                        o = pm[:, (par + h) % 2, :].rearrange("p (t j c) -> p t j c", t=4, j=4)
                        if again(grp) or h > 0:
                            dve.wait_ge(S["out_step"], 2 * grp + h)
                        nc.vector.reciprocal(rec[:], o[:, :, :, DK]).then_inc(S["out_mul"], 1)
                        dve.wait_ge(S["out_mul"], 4 * grp + 2 * h + 1)
                        nc.vector.tensor_tensor(tmp[:], o[:, :, :, 0:DK], rec[:].unsqueeze(3).broadcast_to([P, 4, 4, DK]),
                                                ALU.mult).then_inc(S["out_mul"], 1)
                        dve.wait_ge(S["out_mul"], 4 * grp + 2 * h + 2)
                        nc.vector.sem_inc(S["misc_taken"], 1)
                        x = xr[:, 4 * h:4 * h + 4, 64 * g:64 * g + 64]
                        nc.vector.tensor_tensor(x, x, tmp[:].rearrange("p t j c -> p t (j c)"), ALU.add).then_inc(S["out_step"], 1)

                def batch(b, first=False, left=2):
                    m, par = misc_base(b, first)
                    for blk in range(BLK):
                        if blk % NT <= 1 and not (first and blk <= 1):
                            take_acc(G * b + blk // NT - 1, blk % NT)
                        for kind, i, off in steps_at(blk, first, left):
                            if kind == "out":
                                out(G * (b + off) + i, i, b + off, m, par)
                            else:
                                step(kind, i, b + off, m, par)
                            m, par = m + N_TILES.get(kind, 0), par + N_TILES.get(kind, 0)

                dve.wait_ge(S["w_loaded"], N_W)
                nc.vector.tensor_tensor(A[:, 0, :], z_sb[:].rearrange("p o k n -> p (o k n)"),
                                        z_sb[:].rearrange("p o k n -> p (o k n)"), ALU.mult).then_inc(S["setup_v"], 1)
                dve.wait_ge(S["setup_m"], 1)
                nc.vector.tensor_copy(znc, pm[:, 0, 0:4]).then_inc(S["setup_v"], 1)
                dve.wait_ge(S["setup_p"], 9)
                dve.wait_ge(S["setup_a"], 3)
                c = [3]

                def link(ins):
                    ins.then_inc(S["setup_v"], 1)
                    dve.wait_ge(S["setup_v"], c[0])
                    c[0] += 1
                link(nc.vector.tensor_scalar(znc, znc, 1e-15, None, ALU.max))
                link(nc.vector.tensor_tensor(ep2, ep2, em2, ALU.add))
                link(nc.vector.tensor_scalar(ep2, ep2, 0.5, None, ALU.mult))
                link(nc.vector.tensor_tensor(sh, tanh2, ep2, ALU.mult))
                link(nc.vector.tensor_tensor(zt, tanh2, znc, ALU.mult))
                link(nc.vector.reciprocal(kap, znc))
                link(nc.vector.tensor_tensor(kap, kap, ep2, ALU.mult))
                link(nc.vector.tensor_scalar(zn2, znc, 2.0, None, ALU.mult))
                link(nc.vector.tensor_scalar(zn2m, znc, -2.0, None, ALU.mult))
                m = 0
                for kind, i, off in PROLOGUE:
                    step(kind, i, off, m, m)
                    m += N_TILES.get(kind, 0)
                batch(0, first=True)
                with dve.Fori(1, B - 2) as b:
                    batch(b)
                batch(B - 2, left=1)
                batch(B - 1, left=0)
                for h in range(2):
                    take_acc(G * B - 1, h)
                m, par = misc_base(B, False)
                out(G * B - 1, 3, B - 1, m - LAST, par + LAST)

            @block.scalar
            def _(act):
                act.wait_ge(S["w_loaded"], N_W)
                nc.scalar.activation(tanh2, rcol, ACT.Tanh, scale=2.0).then_inc(S["setup_a"], 1)
                nc.scalar.activation(ep2, rcol, ACT.Exp, scale=2.0).then_inc(S["setup_a"], 1)
                nc.scalar.activation(em2, rcol, ACT.Exp, scale=-2.0).then_inc(S["setup_a"], 1)
                nc.scalar.preload_act_table_set("natural_log_exp_and_others")
                act.wait_ge(S["setup_v"], 11)
                act.wait_ge(S["setup_p"], 7)

                def step(kind, i, b):
                    if kind == "root":
                        act.wait_ge(S["sq_done"], 4 * b + i + 1)
                        nc.scalar.activation(SQ[:, i, :], SQ[:, i, :], ACT.Ln, bias=cst[:, 3:4]).then_inc(S["root_done"], 1)
                        act.wait_ge(S["root_done"], 8 * b + 2 * i + 1)
                        nc.scalar.activation(SQ[:, i, :], SQ[:, i, :], ACT.Exp, scale=0.5).then_inc(S["root_done"], 1)
                    if kind == "ln":
                        act.wait_ge(S["y_done"], 4 * b + i + 1)
                        nc.scalar.activation(SQ[:, i, :], SQ[:, i, :], ACT.Ln).then_inc(S["ln_done"], 1)
                    if kind == "exp":
                        act.wait_ge(S["ln_done"], 4 * b + i + 1)
                        n = 4 * b + i
                        if not isinstance(n, int) or n >= 2:
                            act.wait_ge(S["d_done"], n - 1)
                        nc.scalar.activation(EP[:, i % 2, :], SQ[:, i, :], ACT.Exp, scale=zn2[:, i:i + 1])
                        nc.scalar.activation(SQ[:, i, :], SQ[:, i, :], ACT.Exp, scale=zn2m[:, i:i + 1]).then_inc(S["e_done"], 1)

                def batch(b, first=False, left=2):
                    for blk in range(BLK):
                        for kind, i, off in steps_at(blk, first, left):
                            step(kind, i, b + off)
                        for j in range(4):
                            n = 4 * BLK * b + 4 * blk + j
                            act.wait_ge(S["scores_ready"], n + 1)
                            if not (first and blk < 2):
                                act.wait_ge(S["pv_done"], 2 * (BLK * b + blk - 1))
                            nc.scalar.activation(pr[:, 4 * (blk % 2) + j, :], ps[:, j % 2, :], ACT.Exp, scale=SC).then_inc(S["probs_done"], 1)

                for kind, i, off in PROLOGUE:
                    step(kind, i, off)
                batch(0, first=True)
                with act.Fori(1, B - 2) as b:
                    batch(b)
                batch(B - 2, left=1)
                batch(B - 1, left=0)

            @block.tensor
            def _(pe):
                def bank_free(m):
                    if not isinstance(m, int) or m >= 2:
                        pe.wait_ge(S["misc_taken"], m - 1)

                def step(kind, i, b, m, par, h):
                    bank = pm[:, par % 2, :]
                    if kind == "inT":
                        if h == 0:
                            pe.wait_ge(S["xn_done"], NT * b + NT)
                        bank_free(m)
                        for q in range(4):
                            x = nc.tensor.transpose(bank[:, q * P:(q + 1) * P], xl[:, 4 * h + q, i * P:(i + 1) * P], ident[:])
                    if kind in ("lamb", "facb"):
                        if h == 0:
                            if kind == "lamb":
                                pe.wait_ge(S["dlam_done"], NT * b + NT)
                            else:
                                pe.wait_ge(S["dfac_done"], 2 * NT * b + NT * (i + 1))
                        bank_free(m)
                        x = nc.tensor.matmul(bank, ones[:], dg[:, i, 4 * h:4 * h + 4, :].rearrange("p t n -> p (t n)"),
                                             start=True, stop=True)
                    if kind == "proj":
                        bank_free(m)
                        if i == 0 and h == 0:
                            pe.wait_ge(S["misc_taken"], m - 2)
                        for k in range(KD):
                            x = nc.tensor.matmul(bank, z_sb[:, i // 2, k, (i % 2) * P:(i % 2 + 1) * P],
                                                 xnT[:, k, h * 512:(h + 1) * 512], start=k == 0, stop=k == KD - 1)
                    if kind == "v":
                        bank_free(m)
                        for t in range(2):
                            for k in range(KD):
                                x = nc.tensor.matmul(bank[:, t * D:(t + 1) * D], xnT[:, k, (2 * i + t) * P:(2 * i + t + 1) * P],
                                                     wv_sb[:, k, :], start=k == 0, stop=k == KD - 1)
                    if kind == "sum":
                        pe.wait_ge(S["pair_done"], 2 * b + i + 1)
                        bank_free(m)
                        for t in range(NT):
                            x = nc.tensor.matmul(bank[:, t:t + 1], A[:, 2 * i, t * P:(t + 1) * P], cst[:, 2:3],
                                                 start=True, stop=True)
                    x.then_inc(S["misc_ready"], 1)
                    if kind == "inT" and i == 1 and h == 1:
                        pe.wait_ge(S["misc_ready"], m + 1)
                        pe.sem_inc(S["inT_done"], 1)

                def out(grp, m, par, h):
                    pe.wait_ge(S["acc_taken"], 2 * grp + h + 1)
                    bank_free(m + h)
                    for q in range(4):
                        x = nc.tensor.transpose(pm[:, (par + h) % 2, q * P:(q + 1) * P],
                                                osb[:, (4 * h + q) * P:(4 * h + q + 1) * P], ident[:])
                    x.then_inc(S["misc_ready"], 1)

                def weigh(b, blk, h, first=False):
                    g, kt = blk // NT, blk % NT
                    if h == 0:
                        pe.wait_ge(S["probs_done"], 4 * BLK * b + 4 * blk + 4)
                        if g == 0 and kt % 2 == 0:
                            pe.wait_ge(S["vaug_done"], 8 * b + kt + 2)
                    if kt == 0 and not (first and g == 0):
                        pe.wait_ge(S["acc_taken"], 2 * (G * b + g - 1) + h + 1)
                    for j in range(4):
                        c = V1 * (4 * g + j)
                        x = nc.tensor.matmul(acc[32 * j:32 * j + 32, h * 512:(h + 1) * 512], vaug[:, kt, c:c + 32],
                                             pr[:, 4 * (kt % 2) + j, h * 512:(h + 1) * 512],
                                             start=kt == 0, stop=kt == NT - 1, skip_group_check=True)
                    x.then_inc(S["pv_done"], 1)

                def batch(b, first=False, left=2):
                    m, par = misc_base(b, first)
                    for blk in range(BLK):
                        g, kt = blk // NT, blk % NT
                        tiles = [(kind, i, off, h) for kind, i, off in steps_at(blk, first, left)
                                 for h in range(N_TILES.get(kind, 0))]
                        if kt == 0:
                            pe.wait_ge(st_loaded[g % 2], N_G * (2 * b + g // 2 + 1))
                        for j in range(4):
                            u = 4 * BLK * b + 4 * blk + j
                            if not (first and 4 * blk + j < 2):
                                pe.wait_ge(S["probs_done"], u - 1)
                            for h in range(2):
                                x = nc.tensor.matmul(ps[:, j % 2, h * 512:(h + 1) * 512],
                                                     st[:, g % 2, 1, j, kt * P:(kt + 1) * P],
                                                     st[:, g % 2, 0, j, h * 512:(h + 1) * 512], start=True, stop=True)
                            x.then_inc(S["scores_ready"], 1)
                            if j % 2 == 1:
                                if blk >= 1:
                                    weigh(b, blk - 1, j // 2, first)
                                elif not first:
                                    weigh(b - 1, BLK - 1, j // 2)
                            for q, (kind, i, off, h) in enumerate(tiles):
                                if (4 * q // len(tiles) if len(tiles) > 1 else 2) == j:
                                    if kind == "out":
                                        out(G * (b + off) + i, m - h, par - h, h)
                                    else:
                                        step(kind, i, b + off, m, par, h)
                                    m, par = m + 1, par + 1

                pe.wait_ge(S["setup_p"], 8)
                pe.wait_ge(S["setup_v"], 1)
                for o in range(2):
                    for f in range(2):
                        for k in range(KD):
                            a = (o * KD + k) * D + f * P
                            x = nc.tensor.matmul(pm[:, 0, 2 * o + f:2 * o + f + 1], A[:, 0, a:a + P], cst[:, 3:4],
                                                 start=k == 0, stop=k == KD - 1)
                x.then_inc(S["setup_m"], 1)
                pe.wait_ge(S["setup_v"], 2)
                m = 0
                for kind, i, off in PROLOGUE:
                    for h in range(N_TILES.get(kind, 0)):
                        step(kind, i, off, m, m, h)
                        m += 1
                batch(0, first=True)
                with pe.Fori(1, B - 2) as b:
                    batch(b)
                batch(B - 2, left=1)
                batch(B - 1, left=0)
                for h in range(2):
                    weigh(B - 1, BLK - 1, h)
                m, par = misc_base(B, False)
                for h in range(2):
                    out(G * B - 1, m - LAST, par + LAST, h)


def build_layer(nc, a, out):
    x = a["L0_attn_a_x"]
    x1, x2, x3 = (nc.dram_tensor(name, x.shape, F32, kind="Internal").ap() for name in ("x1", "x2", "x3"))
    cn = [a[f"L0_ffn_cn_{v}{i}"] for i in range(1, 5) for v in "wb"]
    gc = [a[f"L0_ffn_gc_{v}{i}"] for i in range(1, 4) for v in "wb"]
    phase_a(nc, x, *(a["L0_attn_a_" + n] for n in ("Wk", "Wv", "Wo", "gate", "freqs")), x1)
    phase_f(nc, "f1", x1, x2, cn, gc, a["L0_ffn_adaptive_range"])
    phase_b(nc, x2, x3, *(a["L0_attn_b_" + n] for n in ("z_q", "b_q", "z_k", "b_k", "w_v", "b_v")))
    phase_f(nc, "f2", x3, out, cn, gc, a["L0_ffn_adaptive_range"])


def kernel(**inputs):
    import numpy as _np
    import concourse.bacc as _bacc
    from concourse.bass_utils import run_bass_kernel_spmd as _run

    nc = _bacc.Bacc("TRN2", target_bir_lowering=False, num_devices=1)
    inputs["L0_attn_b_w_v"] = _np.asarray(inputs["L0_attn_b_w_v"]).T
    arrays, args = {}, {}
    for name, v in inputs.items():
        v = _np.ascontiguousarray(v)
        arrays[f"in_{name}_dram"] = v
        args[name] = nc.dram_tensor(f"in_{name}_dram", v.shape, mybir.dt.from_np(v.dtype), kind="ExternalInput").ap()
    out = nc.dram_tensor("out_0_dram", inputs["L0_attn_a_x"].shape, F32, kind="ExternalOutput").ap()
    build_layer(nc, args, out)
    r = _run(nc, [arrays], core_ids=[0])
    return r.results[0]["out_0_dram"]
```

```python
from contextlib import ExitStack

import concourse.bass as bass
from concourse import mybir

F32 = mybir.dt.float32
I32 = mybir.dt.int32
BF16 = mybir.dt.bfloat16
ALU = mybir.AluOpType
ACT = mybir.ActivationFunctionType

P = 128
MAGIC = 12582912.0
TWO_PI = 6.283185307179586
TWO_PI_LOW = 6.2831849
PI_LOW = 3.1415925
EPS = 1e-5


class Scope:

    def __init__(self, nc, tag):
        self.nc, self.tag, self.ctx = nc, tag, ExitStack()

    def __enter__(self):
        self.ctx.__enter__()
        self.passed = self.sem("passed")
        return self

    def __exit__(self, *e):
        return self.ctx.__exit__(*e)

    def sb(self, name, shape, dt=F32):
        return self.ctx.enter_context(self.nc.sbuf_tensor(f"{self.tag}_{name}", shape, dt))

    def ps(self, name, shape, dt=F32):
        return self.ctx.enter_context(self.nc.psum_tensor(f"{self.tag}_{name}", shape, dt))

    def sem(self, name):
        return self.ctx.enter_context(self.nc.semaphore(f"{self.tag}_{name}"))


def make_identity(nc, pool, ident, done):
    nc.gpsimd.memset(ident[:], 0.0).then_inc(done, 1)
    pool.wait_ge(done, 1)
    nc.gpsimd.affine_select(out=ident[:], in_=ident[:], compare_op=ALU.not_equal, fill=1.0, base=0,
                            pattern=[[-1, P]], channel_multiplier=1).then_inc(done, 1)


def phase_a(nc, x_in, wk, wv, wo, gate, freqs, x_out):
    B, T, D = x_in.shape
    H, DH = freqs.shape
    HD = H * DH
    KD = D // P
    NT = T // P
    NC = HD // P
    HPT = P // DH
    HC = NC // 2
    NG = NT // 2
    SUMS_AT, VARS_AT = 1, 2
    NORM_AT = {3: range(0, 3), 4: range(3, 6), 5: range(6, NT)}
    TURN = 10.0 / TWO_PI
    C1 = 6.28125
    C2 = TWO_PI - C1
    xi = x_in.rearrange("b (t p) d -> b p t d", p=P)
    xo = x_out.rearrange("b (t p) d -> b p t d", p=P)

    with Scope(nc, "a") as s:
        passed = s.passed
        wk_sb = s.sb("wk", [P, KD, HD])
        wv_sb = s.sb("wv", [P, KD, HD])
        wo_sb = s.sb("wo", [P, NC, D])
        cos_t = s.sb("cos_t", [P, NC, T])
        sin_t = s.sb("sin_t", [P, NC, T])
        ident = s.sb("ident", [P, P])
        diag = s.sb("diag", [P, NT, P])
        freq_rows = s.sb("freq_rows", [NC, P])
        freq = s.sb("freq", [P, NC])
        gates = s.sb("gates", [P, NC, 2])
        sm = s.sb("sm", [P, 9, NT])
        cst = s.sb("cst", [P, 4])
        xl = s.sb("xl", [P, NT, D])
        xr = s.sb("xr", [P, NT, D])
        xnT = s.sb("xnT", [P, KD, T])
        rnd = s.sb("rnd", [P, T])
        frac = s.sb("frac", [P, T])
        sin_k = s.sb("sin_k", [P, 2, T + 2])
        cos_k = s.sb("cos_k", [P, 2, T + 2])
        va = s.sb("va", [P, T])
        vp = s.sb("vp", [P, T])
        xs = s.sb("xs", [P, T])
        yc = s.sb("yc", [P, 2, T])
        ys = s.sb("ys", [P, T])
        out = s.sb("out", [P, NC, T])
        pu = s.ps("pu", [P, T])
        pv = s.ps("pv", [P, T])
        pt = s.ps("pt", [P, 2, 512])
        py = s.ps("py", [P, 2, 512])

        w_loaded = s.sem("w_loaded")
        freq_loaded = s.sem("freq_loaded")
        freq_psum = s.sem("freq_psum")
        freq_done = s.sem("freq_done")
        id_done = s.sem("id_done")
        setup_p = s.sem("setup_p")
        setup_v = s.sem("setup_v")
        angle_done = s.sem("angle_done")
        wk_scaled = s.sem("wk_scaled")
        reduced = s.sem("reduced")
        wrapped = s.sem("wrapped")
        wrap_done = s.sem("wrap_done")
        clamped = s.sem("clamped")
        setup_a = s.sem("setup_a")
        xl_loaded = s.sem("xl_loaded")
        xsum_done = s.sem("xsum_done")
        mean_done = s.sem("mean_done")
        vsum_done = s.sem("vsum_done")
        rstd_done = s.sem("rstd_done")
        xn_done = s.sem("xn_done")
        xt_psum = s.sem("xt_psum")
        xt_done = s.sem("xt_done")
        u_psum = s.sem("u_psum")
        v_psum = s.sem("v_psum")
        rnd_done = s.sem("rnd_done")
        frac_done = s.sem("frac_done")
        abs_done = s.sem("abs_done")
        trig_done = s.sem("trig_done")
        va_done = s.sem("va_done")
        vp_done = s.sem("vp_done")
        xpre = s.sem("xpre")
        ypre = s.sem("ypre")
        xscan = s.sem("xscan")
        yscan = s.sem("yscan")
        xpost = s.sem("xpost")
        ypost = s.sem("ypost")
        unit_done = s.sem("unit_done")
        wo_psum = s.sem("wo_psum")
        wo_done = s.sem("wo_done")
        xr_loaded = s.sem("xr_loaded")
        stored = s.sem("stored")

        xsum, vsum, ve, rstd, nmean = (sm[:, i, :] for i in range(5))
        tcol, root, iroot, nmr = (sm[:, i, :] for i in range(5, 9))
        N_W = 16 * (3 + HPT)
        N_SA = 3 * NC
        tail = [v[:, i * 512:i * 512 + D] for v in (py[:].rearrange("p a n -> p (a n)"), pt[:].rearrange("p a n -> p (a n)"),
                                                    pu[:], pv[:]) for i in range(2)]

        with nc.Block() as block:

            @block.sync
            def _(sp):
                sp.dma_start(freq_rows[:], freqs.rearrange("(c a) d -> c (a d)", a=HPT)).then_inc(freq_loaded, 16)
                sp.dma_start(wk_sb[:], wk.rearrange("(k p) n -> p k n", p=P)).then_inc(w_loaded, 16)
                gv = gate.rearrange("(c a) g -> a c g", a=HPT)
                for a in range(HPT):
                    sp.dma_start(gates[a * DH:(a + 1) * DH, :, :], gv[a:a + 1].broadcast_to([DH, NC, 2])).then_inc(w_loaded, 16)
                sp.dma_start(xl[:], xi[0]).then_inc(xl_loaded, 16)
                sp.dma_start(wv_sb[:], wv.rearrange("(k p) n -> p k n", p=P)).then_inc(w_loaded, 16)
                sp.dma_start(wo_sb[:], wo.rearrange("(c p) n -> p c n", p=P)).then_inc(w_loaded, 16)
                sp.dma_start(xr[:], xi[0]).then_inc(xr_loaded, 16 * 1)

                def dram(v, b):
                    return v[b] if isinstance(b, int) else v[bass.ds(b, 1)].rearrange("o p t d -> (o p) t d")

                def load_xl(b):
                    sp.wait_ge(xt_psum, 4 * b)
                    sp.sem_inc(passed, 1)
                    sp.dma_start(xl[:], dram(xi, b)).then_inc(xl_loaded, 16)

                def batch(b):
                    for g in range(NG):
                        sp.wait_ge(wo_done, 2 * NG * b + NG + g + 1)
                        sp.sem_inc(passed, 1)
                        sp.dma_start(dram(xo, b)[:, 2 * g:2 * g + 2, :], xr[:, 2 * g:2 * g + 2, :]).then_inc(stored, 16)
                        sp.wait_ge(stored, 16 * NG * b + 16 * (g + 1))
                        sp.sem_inc(passed, 1)
                        sp.dma_start(xr[:, 2 * g:2 * g + 2, :], dram(xi, b + 1)[:, 2 * g:2 * g + 2, :]).then_inc(xr_loaded, 16)

                load_xl(1)
                with sp.Fori(0, B - 2) as b:
                    load_xl(b + 2)
                    batch(b)
                batch(B - 2)
                for g in range(NG):
                    sp.wait_ge(wo_done, 2 * NG * (B - 1) + NG + g + 1)
                    sp.sem_inc(passed, 1)
                    sp.dma_start(xo[B - 1, :, 2 * g:2 * g + 2, :], xr[:, 2 * g:2 * g + 2, :]).then_inc(stored, 16)
                sp.wait_ge(stored, 16 * NG * B)

            @block.gpsimd
            def _(pool):
                make_identity(nc, pool, ident, id_done)
                nc.gpsimd.iota(rnd[:].bitcast(I32), [[1, T]], base=0, channel_multiplier=0).then_inc(setup_p, 1)
                nc.gpsimd.iota(tcol.bitcast(I32), [[P, NT]], base=1, channel_multiplier=1).then_inc(setup_p, 1)
                nc.gpsimd.memset(cst[:, 0:1], MAGIC).then_inc(setup_p, 1)
                nc.gpsimd.memset(cst[:, 1:2], TWO_PI / 4).then_inc(setup_p, 1)
                nc.gpsimd.memset(cst[:, 2:3], 0.5).then_inc(setup_p, 1)
                nc.gpsimd.memset(cst[:, 3:4], -0.5).then_inc(setup_p, 1)
                for j in range(2):
                    nc.gpsimd.memset(sin_k[:, j, 0:1], 0.0).then_inc(setup_p, 1)
                    nc.gpsimd.memset(cos_k[:, j, 0:1], 0.0).then_inc(setup_p, 1)
                def means(b):
                    pool.wait_ge(xsum_done, NT * b + NT)
                    if not isinstance(b, int) or b > 0:
                        pool.wait_ge(xn_done, NT * b)
                    pool.sem_inc(passed, 1)
                    nc.gpsimd.tensor_scalar(nmean, xsum, -1.0 / D, None, ALU.mult).then_inc(mean_done, 1)

                def scales(b):
                    pool.wait_ge(vsum_done, NT * b + NT)
                    pool.sem_inc(passed, 1)
                    nc.gpsimd.tensor_scalar(ve, vsum, 1.0 / D, EPS, ALU.mult, ALU.add).then_inc(rstd_done, 1)
                    pool.wait_ge(rstd_done, 3 * b + 1)
                    nc.gpsimd.tensor_tensor(rstd, ve, cst[:, 3:4].broadcast_to([P, NT]), ALU.pow).then_inc(rstd_done, 1)
                    pool.wait_ge(rstd_done, 3 * b + 2)
                    nc.gpsimd.tensor_tensor(nmr, nmean, rstd, ALU.mult).then_inc(rstd_done, 1)

                def pre(n, c):
                    pool.wait_ge(vp_done, n + 1)
                    nc.gpsimd.tensor_tensor(yc[:, c % 2, :], vp[:], cos_t[:, c, :], ALU.mult).then_inc(ypre, 1)
                    nc.gpsimd.tensor_tensor(ys[:], vp[:], sin_t[:, c, :], ALU.mult).then_inc(ypre, 1)

                def post(n, c):
                    pool.wait_ge(yscan, 2 * n + 1)
                    nc.gpsimd.tensor_tensor(yc[:, c % 2, :], yc[:, c % 2, :], cos_t[:, c, :], ALU.mult).then_inc(ypost, 1)
                    pool.wait_ge(yscan, 2 * n + 2)
                    nc.gpsimd.tensor_tensor(ys[:], ys[:], sin_t[:, c, :], ALU.mult).then_inc(ypost, 1)
                    pool.wait_ge(ypost, 3 * n + 2)
                    nc.gpsimd.tensor_tensor(yc[:, c % 2, :], yc[:, c % 2, :], ys[:], ALU.add).then_inc(ypost, 1)
                    pool.wait_ge(ypost, 3 * n + 3)

                def batch(b, last=False):
                    for c in range(NC):
                        post(NC * b + c, c)
                        if not (last and c == NC - 1):
                            if c >= 1 or not isinstance(b, int) or b > 0:
                                pool.wait_ge(unit_done, NC * b + c)
                            pre(NC * b + c + 1, (c + 1) % NC)
                        if c == SUMS_AT and not last:
                            means(b + 1)
                        if c == VARS_AT and not last:
                            scales(b + 1)

                def angle(c):
                    nc.gpsimd.tensor_scalar(sin_t[:, c, :], yc[:, 0, :], freq[:, c:c + 1], 0.0, ALU.mult, ALU.add).then_inc(angle_done, 1)

                def wrap(c):
                    k = cos_t[:, c, :]
                    pool.wait_ge(reduced, c + 1)
                    nc.gpsimd.tensor_scalar(k, sin_t[:, c, :], 1.0 / TWO_PI, MAGIC, ALU.mult, ALU.add).then_inc(wrap_done, 1)
                    pool.wait_ge(wrap_done, 2 * c + 1)
                    nc.gpsimd.tensor_scalar(k, k, -MAGIC, -TWO_PI, ALU.add, ALU.mult).then_inc(wrap_done, 1)

                pool.wait_ge(freq_done, 1)
                pool.wait_ge(setup_v, 2)
                for c in range(3):
                    angle(c)
                pool.wait_ge(setup_p, 10)
                nc.gpsimd.tensor_tensor(root, ve, cst[:, 2:3].broadcast_to([P, NT]), ALU.pow).then_inc(setup_p, 1)
                nc.gpsimd.tensor_tensor(iroot, ve, cst[:, 3:4].broadcast_to([P, NT]), ALU.pow).then_inc(setup_p, 1)
                pool.wait_ge(setup_p, 12)
                means(0)
                for c in range(NC):
                    wrap(c)
                    if c == 3:
                        for t in range(NT):
                            nc.gpsimd.tensor_scalar(diag[:, t, :], ident[:], root[:, t:t + 1], 0.0, ALU.mult, ALU.add)\
                                .then_inc(setup_p, 1)
                    if c + 3 < NC:
                        angle(c + 3)
                    if c == 0:
                        scales(0)
                pool.wait_ge(clamped, NC)
                pool.wait_ge(setup_a, N_SA)
                pre(0, 0)
                batch(0)
                with pool.Fori(1, B - 1) as b:
                    batch(b)
                batch(B - 1, last=True)

            @block.vector
            def _(dve):
                dve.wait_ge(setup_p, 2)
                nc.vector.tensor_copy(yc[:, 0, :], rnd[:].bitcast(I32)).then_inc(setup_v, 1)
                nc.vector.tensor_copy(ve, tcol.bitcast(I32)).then_inc(setup_v, 1)
                dve.wait_ge(freq_psum, 1)
                nc.vector.tensor_copy(freq[:], pt[:, 0, 0:NC]).then_inc(freq_done, 1)

                def fraction(n):
                    dve.wait_ge(rnd_done, n + 1)
                    if not isinstance(n, int) or n > 0:
                        dve.wait_ge(trig_done, n)
                    nc.vector.scalar_tensor_tensor(frac[:], rnd[:], MAGIC, pu[:], ALU.subtract, ALU.subtract).then_inc(frac_done, 1)

                def reduce(c):
                    th, k = sin_t[:, c, :], cos_t[:, c, :]
                    dve.wait_ge(angle_done, c + 1)
                    nc.vector.tensor_scalar(k, th, 1.0 / TWO_PI, MAGIC, ALU.mult, ALU.add).then_inc(setup_v, 1)
                    dve.wait_ge(setup_v, 2 + 3 * c + 1)
                    nc.vector.tensor_scalar(k, k, MAGIC, -C1, ALU.subtract, ALU.mult).then_inc(setup_v, 1)
                    dve.wait_ge(setup_v, 2 + 3 * c + 2)
                    nc.vector.tensor_tensor(th, th, k, ALU.add).then_inc(setup_v, 1)
                    dve.wait_ge(setup_v, 2 + 3 * c + 3)
                    nc.vector.scalar_tensor_tensor(th, k, C2 / C1, th, ALU.mult, ALU.add).then_inc(reduced, 1)

                def clamp(c):
                    th = sin_t[:, c, :]
                    dve.wait_ge(wrap_done, 2 * c + 2)
                    nc.vector.tensor_tensor(th, th, cos_t[:, c, :], ALU.add).then_inc(wrapped, 1)
                    dve.wait_ge(wrapped, c + 1)
                    nc.vector.tensor_scalar(th, th, PI_LOW, -PI_LOW, ALU.min, ALU.max).then_inc(clamped, 1)

                for c in range(NC):
                    reduce(c)
                    if c == 1:
                        dve.wait_ge(w_loaded, N_W)
                        nc.vector.tensor_scalar(wk_sb[:], wk_sb[:], TURN, None, ALU.mult).then_inc(wk_scaled, 1)
                    if c >= 1:
                        clamp(c - 1)
                    if c == NC - 1:
                        fraction(0)
                clamp(NC - 1)

                def finish(n, c):
                    dve.wait_ge(ypost, 3 * n + 3)
                    dve.wait_ge(xpost, 3 * n + 3)
                    nc.vector.tensor_tensor(out[:, c, :], out[:, c, :], yc[:, c % 2, :], ALU.add).then_inc(unit_done, 1)

                def step(n, c, first, last, free):
                    o = out[:, c, :]
                    dve.wait_ge(trig_done, n + 1)
                    dve.wait_ge(va_done, n + 1)
                    if free is not None:
                        dve.wait_ge(wo_psum, free)
                    nc.vector.tensor_tensor(o, va[:], cos_k[:, c % 2, 0:T], ALU.mult).then_inc(xpre, 1)
                    nc.vector.tensor_tensor(xs[:], va[:], sin_k[:, c % 2, 0:T], ALU.mult).then_inc(xpre, 1)
                    if not first:
                        finish(n - 1, (c - 1) % NC)
                    dve.wait_ge(xpre, 2 * n + 1)
                    nc.vector.tensor_tensor_scan(o, o, o, 0.0, ALU.add, ALU.bypass).then_inc(xscan, 1)
                    dve.wait_ge(xpre, 2 * n + 2)
                    nc.vector.tensor_tensor_scan(xs[:], xs[:], xs[:], 0.0, ALU.add, ALU.bypass).then_inc(xscan, 1)
                    if not last:
                        fraction(n + 1)
                    y = yc[:, c % 2, :]
                    dve.wait_ge(ypre, 2 * n + 1)
                    nc.vector.tensor_tensor_scan(y, y, y, 0.0, ALU.add, ALU.bypass).then_inc(yscan, 1)
                    dve.wait_ge(ypre, 2 * n + 2)
                    nc.vector.tensor_tensor_scan(ys[:], ys[:], ys[:], 0.0, ALU.add, ALU.bypass).then_inc(yscan, 1)
                    dve.wait_ge(xscan, 2 * n + 2)
                    nc.vector.tensor_tensor(o, o, cos_k[:, c % 2, 1:T + 1], ALU.mult).then_inc(xpost, 1)
                    nc.vector.tensor_tensor(xs[:], xs[:], sin_k[:, c % 2, 1:T + 1], ALU.mult).then_inc(xpost, 1)
                    dve.wait_ge(xpost, 3 * n + 2)
                    nc.vector.tensor_tensor(o, o, xs[:], ALU.add).then_inc(xpost, 1)
                    dve.wait_ge(xpost, 3 * n + 3)

                def batch(b, first=False, last=False):
                    for c in range(NC):
                        free = None
                        if not first and c in (0, HC):
                            free = 2 * NG * (b - 1) + (NG if c == 0 else 2 * NG)
                        step(NC * b + c, c, first and c == 0, last and c == NC - 1, free)

                batch(0, first=True)
                with dve.Fori(1, B - 1) as b:
                    batch(b)
                batch(B - 1, last=True)
                finish(NC * B - 1, NC - 1)

            @block.scalar
            def _(act):
                act.wait_ge(setup_p, 10)
                nc.scalar.preload_act_table(ACT.Sin)

                def token_sums(b):
                    act.wait_ge(xl_loaded, 16 * b + 16)
                    if not isinstance(b, int) or b > 0:
                        act.wait_ge(xt_done, 4 * b)
                        act.wait_ge(rstd_done, 3 * b)
                    else:
                        act.wait_ge(freq_done, 1)
                    for t in range(NT):
                        if t >= 4:
                            act.wait_ge(xsum_done, NT * b + t - 3)
                        nc.scalar.activation(spare(t), xl[:, t, :], ACT.Copy, accum_out=xsum[:, t:t + 1]).then_inc(xsum_done, 1)

                def token_vars(b):
                    act.wait_ge(mean_done, b + 1)
                    for t in range(NT):
                        if t >= 4:
                            act.wait_ge(vsum_done, NT * b + t - 3)
                        nc.scalar.activation(spare(t), xl[:, t, :], ACT.Square, bias=nmean[:, t:t + 1],
                                             accum_out=vsum[:, t:t + 1]).then_inc(vsum_done, 1)

                def spare(t):
                    return pt[:, t % 4 // 2, t % 2 * D:(t % 2 + 1) * D]

                def normalise(b, tiles):
                    act.wait_ge(rstd_done, 3 * b + 3)
                    for t in tiles:
                        nc.scalar.activation(xl[:, t, :], xl[:, t, :], ACT.Identity, bias=nmr[:, t:t + 1],
                                             scale=rstd[:, t:t + 1]).then_inc(xn_done, 1)

                def transposed(b):
                    for g in range(2 * KD):
                        act.wait_ge(xt_psum, 4 * b + g + 1)
                        if g == 0 and (not isinstance(b, int) or b > 0):
                            act.wait_ge(v_psum, NC * b)
                        f, h = g // 2, g % 2
                        nc.scalar.activation(xnT[:, f, h * 512:(h + 1) * 512], pt[:, g % 2, :], ACT.Copy).then_inc(xt_done, 1)

                def front(n, c, first=False, used=False, nxt=None):
                    act.wait_ge(u_psum, n + 1)
                    if not first:
                        act.wait_ge(trig_done, n)
                    nc.scalar.activation(rnd[:], pu[:], ACT.Identity, bias=cst[:, 0:1]).then_inc(rnd_done, 1)
                    act.wait_ge(v_psum, n + 1)
                    if not first:
                        act.wait_ge(xpre, 2 * n)
                    nc.scalar.activation(va[:], pv[:], ACT.Copy, scale=gates[:, c, 1:2]).then_inc(va_done, 1)
                    act.wait_ge(frac_done, n + 1)
                    nc.scalar.activation(rnd[:], frac[:], ACT.Abs).then_inc(abs_done, 1)
                    if not first:
                        act.wait_ge(ypre, 2 * n)
                    nc.scalar.activation(vp[:], pv[:], ACT.Copy, scale=gates[:, c, 0:1]).then_inc(vp_done, 1)
                    if nxt is not None:
                        transposed(nxt)
                    act.wait_ge(abs_done, n + 1)
                    if used:
                        act.wait_ge(xpost, 3 * (n - 1) - 1)
                    nc.scalar.activation(cos_k[:, c % 2, 1:T + 1], rnd[:], ACT.Sin, bias=cst[:, 1:2], scale=-TWO_PI_LOW)
                    nc.scalar.activation(sin_k[:, c % 2, 1:T + 1], frac[:], ACT.Sin, scale=-TWO_PI_LOW).then_inc(trig_done, 1)

                def project_out(k, g):
                    act.wait_ge(wo_psum, k + 1)
                    for j in range(2):
                        t = 2 * g + j
                        i = nc.scalar.activation(xr[:, t, :], py[:, g % 2, j * D:(j + 1) * D], ACT.Copy, scale=iroot[:, t:t + 1])
                    i.then_inc(wo_done, 1)

                def batch(b, first=False, last=False):
                    for c in range(NC):
                        if not (last and c == NC - 1):
                            front(NC * b + c + 1, (c + 1) % NC, used=c >= 1 or not first,
                                  nxt=b + 1 if c == NC - 2 and not last else None)
                        if c >= HC:
                            project_out(2 * NG * b + c - HC, c - HC)
                        elif not first:
                            project_out(2 * NG * (b - 1) + NG + c, c)
                        if c == SUMS_AT and not last:
                            token_sums(b + 1)
                        if c == VARS_AT and not last:
                            token_vars(b + 1)
                        if c in NORM_AT and not last:
                            normalise(b + 1, NORM_AT[c])

                token_sums(0)
                token_vars(0)
                normalise(0, range(NT))
                transposed(0)
                for c in range(NC):
                    th, k = sin_t[:, c, :], cos_t[:, c, :]
                    act.wait_ge(clamped, c + 1)
                    nc.scalar.activation(k, th, ACT.Abs).then_inc(setup_a, 1)
                    act.wait_ge(setup_a, 3 * c + 1)
                    nc.scalar.activation(k, k, ACT.Sin, bias=cst[:, 1:2], scale=-1.0).then_inc(setup_a, 1)
                    nc.scalar.activation(th, th, ACT.Sin).then_inc(setup_a, 1)
                    if c == NC - 3:
                        front(0, 0, first=True)
                act.wait_ge(setup_p, 12)
                batch(0, first=True)
                with act.Fori(1, B - 1) as b:
                    batch(b)
                batch(B - 1, last=True)
                for t in range(NT):
                    act.wait_ge(wo_psum, 2 * NG * (B - 1) + NG + t // 2 + 1)
                    i = nc.scalar.activation(xr[:, t, :], tail[t], ACT.Copy, scale=iroot[:, t:t + 1])
                    if t % 2:
                        i.then_inc(wo_done, 1)

            @block.tensor
            def _(pe):
                def transposes(b):
                    pe.wait_ge(xn_done, NT * b + NT)
                    for g in range(2 * KD):
                        f, h = g // 2, g % 2
                        if g >= 2 or not isinstance(b, int) or b > 0:
                            pe.wait_ge(xt_done, 4 * b + g - 1)
                        for j in range(4):
                            t = 4 * h + j
                            i = nc.tensor.transpose(pt[:, g % 2, j * P:(j + 1) * P], xl[:, t, f * P:(f + 1) * P], ident[:])
                        i.then_inc(xt_psum, 1)

                def project(n, c, first=False):
                    if not first:
                        pe.wait_ge(frac_done, n)
                    for h in range(2):
                        for k in range(KD):
                            i = nc.tensor.matmul(pu[:, h * 512:(h + 1) * 512], wk_sb[:, k, c * P:(c + 1) * P],
                                                 xnT[:, k, h * 512:(h + 1) * 512], start=k == 0, stop=k == KD - 1)
                    i.then_inc(u_psum, 1)
                    if not first:
                        pe.wait_ge(vp_done, n)
                    for h in range(2):
                        for k in range(KD):
                            i = nc.tensor.matmul(pv[:, h * 512:(h + 1) * 512], wv_sb[:, k, c * P:(c + 1) * P],
                                                 xnT[:, k, h * 512:(h + 1) * 512], start=k == 0, stop=k == KD - 1)
                    i.then_inc(v_psum, 1)

                def project_out(k, g, units, c0, x_loads, free):
                    pe.wait_ge(unit_done, units)
                    pe.wait_ge(xr_loaded, x_loads)
                    if free:
                        pe.wait_ge(wo_done, k - 1)
                    for j in range(2):
                        t = 2 * g + j
                        o = py[:, g % 2, j * D:(j + 1) * D]
                        nc.tensor.matmul(o, diag[:, t, :], xr[:, t, :], start=True, stop=False)
                        for c in range(c0, c0 + HC):
                            i = nc.tensor.matmul(o, out[:, c, t * P:(t + 1) * P], wo_sb[:, c, :], start=False, stop=c == c0 + HC - 1)
                    i.then_inc(wo_psum, 1)

                def batch(b, first=False, last=False):
                    for c in range(NC):
                        if c == NC - 1 and not last:
                            pe.wait_ge(xt_done, 4 * (b + 1) + 4)
                        if not (last and c == NC - 1):
                            project(NC * b + c + 1, (c + 1) % NC)
                        if c == NC - 2 and not last:
                            transposes(b + 1)
                        if c >= HC:
                            g = c - HC
                            loads = 16 if first else 16 + 16 * (NG * (b - 1) + g + 1)
                            project_out(2 * NG * b + g, g, NC * b + HC, 0, loads, not first or g >= 2)
                        elif not first:
                            project_out(2 * NG * (b - 1) + NG + c, c, NC * b, HC, 16, True)

                pe.wait_ge(id_done, 2)
                pe.wait_ge(freq_loaded, 16)
                nc.tensor.transpose(pt[:, 0, 0:NC], freq_rows[:], ident[0:NC, 0:NC]).then_inc(freq_psum, 1)
                pe.wait_ge(freq_done, 1)
                transposes(0)
                pe.wait_ge(xt_done, 4)
                pe.wait_ge(wk_scaled, 1)
                pe.wait_ge(w_loaded, N_W)
                project(0, 0, first=True)
                pe.wait_ge(setup_p, 12 + NT)
                batch(0, first=True)
                with pe.Fori(1, B - 1) as b:
                    batch(b)
                batch(B - 1, last=True)
                pe.wait_ge(unit_done, NC * B - 1)
                pe.wait_ge(wo_done, 2 * NG * (B - 1) + NG)
                pe.wait_ge(xt_done, 4 * B)
                pe.wait_ge(frac_done, NC * B)
                pe.wait_ge(vp_done, NC * B)
                for t in range(NT):
                    nc.tensor.matmul(tail[t], diag[:, t, :], xr[:, t, :], start=True, stop=False)
                    for c in range(HC, NC - 1):
                        nc.tensor.matmul(tail[t], out[:, c, t * P:(t + 1) * P], wo_sb[:, c, :], start=False, stop=False)
                pe.wait_ge(unit_done, NC * B)
                for t in range(NT):
                    i = nc.tensor.matmul(tail[t], out[:, NC - 1, t * P:(t + 1) * P], wo_sb[:, NC - 1, :], start=False, stop=True)
                    if t % 2:
                        i.then_inc(wo_psum, 1)


def ffn_steps(first, last):
    late = "skip" if first else None
    early = "skip" if last else None

    def beside(x, k, y, behind):
        return [("L1a", x, k), ("L3", y, behind), ("L1b", x, k), ("L4", y, behind)]

    out = []
    for k in range(3):
        if k == 0:
            out += [("L1", 0, 0), (late or "L34", 1, 2)]
        else:
            out += beside(0, k, 1, k - 1)
        if k == 0:
            out.append((late or "outT", 0, None))
        if k == 1:
            out.append((early or "inT", 0, None))
        if k == 2 and not last:
            out.append(("G1", None, None))
        if k == 0:
            out.append(("G3", None, None))
            if not last:
                out.append(("LN", 0, None))
        out.append(("L2", 0, k))
        out += beside(1, k, 0, k)
        if k == 0:
            out.append((late or "outT", 1, None))
            if not last:
                out.append(("LN", 1, None))
        if k == 1:
            out.append((early or "inT", 1, None))
        if k == 2 and not last:
            out.append(("G2", None, None))
        out.append(("L2", 1, k))
    return out


L1_TILES = {"L1": range(4), "L1a": range(3), "L1b": range(3, 4)}


def tiles_of(step, skipped_as):
    return {"L1": 4, "L1a": 3, "L1b": 1, "L2": 2, "L34": 3, "L3": 1, "L4": 2, "outT": 4, "inT": 4}.get(skipped_as if step == "skip" else step, 0)


def phase_f(nc, tag, x_in, x_out, cn, gc, arange):
    w1, b1, w2, b2, w3, b3, w4, b4 = cn
    gw1, gb1, gw2, gb2, gw3, gb3 = gc
    B, T, D = x_in.shape
    NT = T // P
    KD = D // P
    HT = 512
    NH = T // HT
    M3 = w3.shape[1]
    PAIRS = B // 2
    RING = 7
    TILES, ACT_TILES = 70, 62
    PRO = 2 * KD * NH
    xi = x_in.rearrange("b (t p) d -> b p t d", p=P)
    xo = x_out.rearrange("b (t p) d -> b p t d", p=P)

    with Scope(nc, tag) as s:
        passed = s.passed
        w1_sb = s.sb("w1", [P, KD, D])
        w2_sb = s.sb("w2", [P, KD, P])
        w3_sb = s.sb("w3", [P, M3])
        w4c = s.sb("w4c", [P, 1])
        w4r = s.sb("w4r", [P, 2, P])
        gw1_sb = s.sb("gw1", [P, KD, P])
        gw2_sb = s.sb("gw2", [P, M3])
        gw3c = s.sb("gw3c", [P, 1])
        gw3r = s.sb("gw3r", [P, P])
        b1_sb = s.sb("b1", [P, KD])
        b2_sb = s.sb("b2", [P, 1])
        b3_sb = s.sb("b3", [P, 1])
        gb1_sb = s.sb("gb1", [P, 1])
        gb2_sb = s.sb("gb2", [P, 1])
        sc = s.sb("sc", [P, 12])
        ident = s.sb("ident", [P, P])
        ones = s.sb("ones", [P, P])
        stats = s.sb("stats", [P, 2, NT, 6])
        mv = s.sb("mv", [P, 2, NT, 2])
        sm = s.sb("sm", [P, 3, 2, NT])
        mhalf = s.sb("mhalf", [P, 1])
        xl = s.sb("xl", [P, 2, NT, D])
        xr = s.sb("xr", [P, 2, NT, D])
        S = [s.sb(f"s{i}", [P, 2, KD, T]) for i in range(4)]
        h1 = s.sb("h1", [P, 2, KD, T])
        h2 = s.sb("h2", [P, 2, T])
        h3 = s.sb("h3", [P, 2, HT])
        th = s.sb("th", [P, 2, T])
        cs = s.sb("cs", [P, 2, T])
        sums = s.sb("sums", [P, 2 * KD, 2])
        gh1 = s.sb("gh1", [P, 2])
        gh2 = s.sb("gh2", [P, 2])
        thg = s.sb("thg", [P, 2])
        k2 = s.sb("k2", [P, 2])
        po = s.ps("po", [P, RING, HT])
        pg = s.ps("pg", [P, HT])
        ar, sign, k1, c07, c01, hb4, hgb3 = (sc[:, i:i + 1] for i in range(7))

        w_loaded = s.sem("w_loaded")
        setup_p = s.sem("setup_p")
        setup_v = s.sem("setup_v")
        xl_loaded = [s.sem(f"xl_loaded{x}") for x in range(2)]
        xr_loaded = s.sem("xr_loaded")
        stored = s.sem("stored")
        stats_done = s.sem("stats_done")
        mv_done = s.sem("mv_done")
        rstd_done = s.sem("rstd_done")
        xn_done = s.sem("xn_done")
        tile_ready = s.sem("tile_ready")
        act_done = s.sem("act_done")
        out_done = s.sem("out_done")
        g_psum = s.sem("g_psum")
        g_act = s.sem("g_act")
        k2_done = s.sem("k2_done")
        cs_done = [s.sem(f"cs_done{x}") for x in range(2)]
        a_done = [s.sem(f"a_done{x}") for x in range(2)]
        b_done = [s.sem(f"b_done{x}") for x in range(2)]
        state_done = [s.sem(f"state_done{x}") for x in range(2)]

        ve, rstd, nmean = (sm[:, i] for i in range(3))

        tile_at, act_at, out_at = {}, {}, {}
        plan, t0, a0, o0 = [], 0, 0, 0
        for step in ffn_steps(False, False):
            n = tiles_of(step[0], None)
            tile_at[step] = t0
            if step[0] == "outT":
                out_at[step] = o0
                o0 += n
            else:
                act_at[step] = a0
                a0 += n
            for i in range(n):
                plan.append(("v", out_at[step] + i) if step[0] == "outT" else ("a", act_at[step] + i))
            t0 += n

        def l1_at(x, k, i):
            if ("L1", x, k) in act_at:
                return act_at[("L1", x, k)] + i
            return act_at[("L1a", x, k)] + i if i < 3 else act_at[("L1b", x, k)]

        def l34_at(x, k, i):
            if ("L34", x, k) in act_at:
                return act_at[("L34", x, k)] + i
            return act_at[("L3", x, k)] if i == 0 else act_at[("L4", x, k)] + i - 1

        assert (t0, a0, o0) == (TILES, ACT_TILES, 8) and TILES % RING == 0

        def real(step, x, k, at):
            if step != "skip":
                return step
            if k == 2:
                return "L34"
            return "outT" if at < TILES // 3 else "inT"

        with nc.Block() as block:
            N_W = 16 * 18

            @block.sync
            def _(sp):
                def col(v):
                    return v.rearrange("(p o) -> p o", o=1)
                sp.dma_start(xl[:, 0], xi[0]).then_inc(xl_loaded[0], 16)
                sp.dma_start(xl[:, 1], xi[1]).then_inc(xl_loaded[1], 16)
                loads = [
                    (w1_sb[:], w1.rearrange("(k p) n -> p k n", p=P)),
                    (w2_sb[:], w2.rearrange("(k p) n -> p k n", p=P)),
                    (w3_sb[:], w3), (gw1_sb[:], gw1.rearrange("(k p) n -> p k n", p=P)), (gw2_sb[:], gw2),
                    (w4c[0:M3, :], w4), (w4c[M3:P, :], w4), (gw3c[0:M3, :], gw3),
                    (b1_sb[:, 0:1], col(b1[0:P])), (b1_sb[:, 1:2], col(b1[P:D])), (b2_sb[:], col(b2)),
                    (b3_sb[0:M3, :], col(b3)), (b3_sb[M3:P, :], col(b3)),
                    (gb1_sb[:], col(gb1)), (gb2_sb[0:M3, :], col(gb2)),
                    (ar, arange.rearrange("(a o) -> a o", o=1).broadcast_to([P, 1])),
                    (hb4, b4.rearrange("(a o) -> a o", o=1).broadcast_to([P, 1])),
                    (hgb3, gb3.rearrange("(a o) -> a o", o=1).broadcast_to([P, 1])),
                ]
                assert len(loads) * 16 == N_W
                for dst, src in loads:
                    sp.dma_start(dst, src).then_inc(w_loaded, 16)
                sp.dma_start(xr[:, 0], xi[0]).then_inc(xr_loaded, 16)
                sp.dma_start(xr[:, 1], xi[1]).then_inc(xr_loaded, 16)

                def dram(v, b):
                    return v[b] if isinstance(b, int) else v[bass.ds(b, 1)].rearrange("o p t d -> (o p) t d")

                def pair(j, first=False, last=False):
                    if not last:
                        for x in range(2):
                            if first:
                                sp.wait_ge(tile_ready, PRO)
                            else:
                                sp.wait_ge(tile_ready, PRO + TILES * (j - 1) + tile_at[("inT", x, None)] + 4)
                            sp.sem_inc(passed, 1)
                            sp.dma_start(xl[:, x], dram(xi, 2 * j + 2 + x)).then_inc(xl_loaded[x], 16)
                    if not first:
                        for x in range(2):
                            sp.wait_ge(out_done, 8 * j + 4 * x + 4)
                            sp.sem_inc(passed, 1)
                            sp.dma_start(dram(xo, 2 * j - 2 + x), xr[:, x]).then_inc(stored, 16)
                        for x in range(2):
                            sp.wait_ge(stored, 32 * j)
                            sp.sem_inc(passed, 1)
                            sp.dma_start(xr[:, x], dram(xi, 2 * j + x)).then_inc(xr_loaded, 16)

                pair(0, first=True)
                with sp.Fori(1, PAIRS - 1) as j:
                    pair(j)
                pair(PAIRS - 1, last=True)
                for x in range(2):
                    sp.wait_ge(out_done, 8 * PAIRS + 4 * x + 4)
                    sp.dma_start(xo[B - 2 + x], xr[:, x]).then_inc(stored, 16)
                sp.wait_ge(stored, 32 * PAIRS)

            @block.gpsimd
            def _(pool):
                make_identity(nc, pool, ident, setup_p)
                nc.gpsimd.memset(ones[:], 1.0).then_inc(setup_p, 1)
                nc.gpsimd.memset(mhalf[:], -0.5).then_inc(setup_p, 1)
                nc.gpsimd.memset(w4r[:], 0.0).then_inc(setup_p, 1)

                def scales(x, j):
                    n = 2 * j + x
                    pool.wait_ge(mv_done, NT * (n + 1))
                    if not isinstance(j, int) or j > 0:
                        pool.wait_ge(xn_done, NT * n)
                    pool.sem_inc(passed, 1)
                    nc.gpsimd.tensor_scalar(ve[:, x], mv[:, x, :, 1], EPS, None, ALU.add).then_inc(rstd_done, 1)
                    nc.gpsimd.tensor_scalar(nmean[:, x], mv[:, x, :, 0], -1.0, None, ALU.mult).then_inc(rstd_done, 1)
                    pool.wait_ge(rstd_done, 3 * n + 1)
                    nc.gpsimd.tensor_tensor(rstd[:, x], ve[:, x], mhalf[:, 0:1].broadcast_to([P, NT]), ALU.pow).then_inc(rstd_done, 1)

                def norm(x, j):
                    scales(x, j)
                    pool.wait_ge(rstd_done, 3 * (2 * j + x) + 3)
                    pool.sem_inc(passed, 1)
                    for t in range(NT):
                        nc.gpsimd.tensor_scalar(xl[:, x, t, :], xl[:, x, t, :], nmean[:, x, t:t + 1],
                                                rstd[:, x, t:t + 1], ALU.add, ALU.mult).then_inc(xn_done, 1)

                def turn(x, k, j):
                    for h in range(NH):
                        c = slice(h * HT, (h + 1) * HT)
                        pool.wait_ge(cs_done[x], 6 * j + 2 * k + h + 1)
                        nc.gpsimd.tensor_tensor(S[k + 1][:, x, 1, c], cs[:, x, c], S[k][:, x, 0, c],
                                                ALU.mult).then_inc(b_done[x], 1)

                def pair(j, first=False, last=False):
                    for step, x, k in ffn_steps(first, last):
                        if step in ("L34", "L4"):
                            turn(x, k, j - 1 if (x, k) == (1, 2) else j)
                        if step == "LN":
                            norm(x, j + 1)

                scales(0, 0)
                scales(1, 0)
                pair(0, first=True)
                with pool.Fori(1, PAIRS - 1) as j:
                    pair(j)
                pair(PAIRS - 1, last=True)
                turn(1, 2, PAIRS - 1)

            @block.vector
            def _(dve):
                def layernorm_stats(x, j):
                    n = 2 * j + x
                    dve.wait_ge(xl_loaded[x], 16 * (j + 1))
                    if not isinstance(j, int) or j > 0:
                        dve.wait_ge(mv_done, NT * (n - 1))
                        dve.wait_ge(xn_done, NT * (n - 1))
                    for t in range(NT):
                        nc.vector.bn_stats(stats[:, x, t, :], xl[:, x, t, :]).then_inc(stats_done, 1)
                    dve.wait_ge(stats_done, NT * (n + 1))
                    dve.sem_inc(passed, 1)
                    for t in range(NT):
                        nc.vector.bn_aggr(mv[:, x, t, :], stats[:, x, t, :]).then_inc(mv_done, 1)

                def turn(x, k, j, end=False):
                    for h in range(NH):
                        c = slice(h * HT, (h + 1) * HT)
                        n = 6 * j + 2 * k + h
                        src, dst = S[k], S[k + 1]
                        dve.wait_ge(act_done, PRO + ACT_TILES * (j + (1 if (x, k) == (1, 2) else 0)) + (h + 2 if end else l34_at(x, k, 1 + h) + 1))
                        dve.wait_ge(k2_done, j + 1)
                        if not isinstance(n, int) or n > 0:
                            dve.wait_ge(state_done[x], n)
                        nc.vector.tensor_scalar(cs[:, x, c], th[:, x, c], k1, k2[:, x:x + 1], ALU.mult, ALU.add).then_inc(cs_done[x], 1)
                        dve.wait_ge(cs_done[x], n + 1)
                        nc.vector.tensor_tensor(dst[:, x, 0, c], cs[:, x, c], src[:, x, 1, c], ALU.mult).then_inc(a_done[x], 1)
                        dve.wait_ge(a_done[x], n + 1)
                        nc.vector.tensor_tensor(dst[:, x, 0, c], dst[:, x, 0, c], src[:, x, 0, c], ALU.add)
                        dve.wait_ge(b_done[x], n + 1)
                        nc.vector.tensor_tensor(dst[:, x, 1, c], src[:, x, 1, c], dst[:, x, 1, c], ALU.subtract).then_inc(state_done[x], 1)

                def residual(x, j, at):
                    dve.wait_ge(xr_loaded, 32 * j)
                    for g in range(4):
                        dve.wait_ge(tile_ready, PRO + TILES * j + at + g + 1)
                        v = xr[:, x, 2 * g:2 * g + 2, :].rearrange("p t d -> p (t d)")
                        nc.vector.tensor_tensor(v, v, po[:, (at + g) % RING, :], ALU.add).then_inc(out_done, 1)

                def coupling_base(j):
                    dve.wait_ge(g_act, 3 * (j + 1))
                    nc.vector.tensor_scalar(k2[:], thg[:], c07, c01, ALU.mult, ALU.add).then_inc(k2_done, 1)

                def pair(j, first=False, last=False):
                    at = 0
                    for step, x, k in ffn_steps(first, last):
                        kind = real(step, x, k, at)
                        if step in ("L34", "L4"):
                            turn(x, k, j - 1 if (x, k) == (1, 2) else j)
                        if step == "outT":
                            residual(x, j, at)
                        if step == "skip" and kind == "outT":
                            nc.vector.sem_inc(out_done, 4)
                        if step == "LN":
                            layernorm_stats(x, j + 1)
                        if step == "G3":
                            if not first:
                                dve.wait_ge(state_done[1], 6 * j)
                            coupling_base(j)
                        at += tiles_of(step, kind)

                layernorm_stats(0, 0)
                layernorm_stats(1, 0)
                for x in range(2):
                    dve.wait_ge(rstd_done, 3 * x + 3)
                    for t in range(NT):
                        nc.vector.tensor_scalar(xl[:, x, t, :], xl[:, x, t, :], nmean[:, x, t:t + 1],
                                                rstd[:, x, t:t + 1], ALU.add, ALU.mult).then_inc(xn_done, 1)
                nc.vector.memset(sign[0:M3, :], 1.0).then_inc(setup_v, 1)
                nc.vector.memset(sign[M3:P, :], -1.0).then_inc(setup_v, 1)
                dve.wait_ge(w_loaded, N_W)
                dve.wait_ge(setup_p, 5)
                dve.wait_ge(setup_v, 2)
                nc.vector.tensor_scalar(k1, sign, ar, 0.3, ALU.mult, ALU.mult).then_inc(setup_v, 1)
                nc.vector.tensor_scalar(c07, sign, ar, 0.7, ALU.mult, ALU.mult).then_inc(setup_v, 1)
                nc.vector.tensor_scalar(c01, sign, 0.1, None, ALU.mult).then_inc(setup_v, 1)
                nc.vector.tensor_scalar(hb4, hb4, 0.5, None, ALU.mult).then_inc(setup_v, 1)
                nc.vector.tensor_scalar(hgb3, hgb3, 0.5, None, ALU.mult).then_inc(setup_v, 1)
                for h in range(2):
                    r = slice(h * M3, (h + 1) * M3)
                    nc.vector.tensor_scalar(w4r[r, h, :], ones[r, :], w4c[r, :], None, ALU.mult).then_inc(setup_v, 1)
                nc.vector.tensor_scalar(gw3r[0:M3, :], ones[0:M3, :], gw3c[0:M3, :], None, ALU.mult).then_inc(setup_v, 1)
                dve.wait_ge(setup_v, 10)
                pair(0, first=True)
                with dve.Fori(1, PAIRS - 1) as j:
                    pair(j)
                pair(PAIRS - 1, last=True)
                turn(1, 2, PAIRS - 1, end=True)
                for x in range(2):
                    residual(x, PAIRS, 4 * x + 3)

            @block.scalar
            def _(act):
                nc.scalar.preload_act_table(ACT.Gelu)

                def take(j, at):
                    act.wait_ge(tile_ready, PRO + TILES * j + at + 1)
                    return po[:, at % RING, :]

                def features(x, j, at, base=None):
                    for i in range(2 * KD):
                        f, h = i // 2, i % 2
                        act.wait_ge(tile_ready, (PRO + TILES * j + at if base is None else base) + i + 1)
                        nc.scalar.activation(S[0][:, x, f, h * HT:(h + 1) * HT], po[:, (at + i) % RING, :], ACT.Copy,
                                             accum_out=sums[:, i, x:x + 1]).then_inc(act_done, 1)

                def pair(j, first=False, last=False):
                    at = 0
                    for step, x, k in ffn_steps(first, last):
                        kind = real(step, x, k, at)
                        if step == "skip" and kind != "outT":
                            n = tiles_of(step, kind)
                            act.wait_ge(act_done, PRO + ACT_TILES * j + act_at[(kind, x, k)])
                            nc.scalar.sem_inc(act_done, n)
                        for q, i in enumerate(L1_TILES.get(step, ())):
                            h, m = i // 2, i % 2
                            p = take(j, at + q)
                            nc.scalar.activation(h1[:, x, m, h * HT:(h + 1) * HT], p, ACT.Gelu, bias=b1_sb[:, m:m + 1]).then_inc(act_done, 1)
                        if step == "L2":
                            for h in range(2):
                                p = take(j, at + h)
                                nc.scalar.activation(h2[:, x, h * HT:(h + 1) * HT], p, ACT.Gelu, bias=b2_sb[:]).then_inc(act_done, 1)
                        if step in ("L34", "L3"):
                            p = take(j, at)
                            nc.scalar.activation(h3[:, x], p, ACT.Gelu, bias=b3_sb[:]).then_inc(act_done, 1)
                        if step in ("L34", "L4"):
                            jj = j - 1 if (x, k) == (1, 2) else j
                            for h in range(2):
                                p = take(j, at + h + (step == "L34"))
                                n = 6 * jj + 2 * k + h
                                if not isinstance(n, int) or n >= 2:
                                    act.wait_ge(cs_done[x], n - 1)
                                nc.scalar.activation(th[:, x, h * HT:(h + 1) * HT], p, ACT.Tanh, scale=0.5, bias=hb4).then_inc(act_done, 1)
                        if step == "inT":
                            act.wait_ge(state_done[x], 6 * j + 2)
                            features(x, j, at)
                        if step == "G1":
                            g_step(j + 1, 0)
                        if step == "G2":
                            g_step(j + 1, 1)
                        if step == "G3":
                            if not first:
                                act.wait_ge(k2_done, j)
                            g_step(j, 2)
                        at += tiles_of(step, kind)

                def g_step(j, i):
                    act.wait_ge(g_psum, 3 * j + i + 1)
                    if i == 0:
                        nc.scalar.activation(gh1[:], pg[:, 0:2], ACT.Gelu, scale=1.0 / T, bias=gb1_sb[:]).then_inc(g_act, 1)
                    if i == 1:
                        nc.scalar.activation(gh2[0:M3, :], pg[0:M3, 2:4], ACT.Gelu, bias=gb2_sb[0:M3, :]).then_inc(g_act, 1)
                    if i == 2:
                        nc.scalar.activation(thg[:], pg[:, 4:6], ACT.Tanh, scale=0.5, bias=hgb3).then_inc(g_act, 1)

                for x in range(2):
                    features(x, 0, TILES - PRO + 4 * x, base=4 * x)
                act.wait_ge(w_loaded, N_W)
                act.wait_ge(setup_v, 10)
                g_step(0, 0)
                g_step(0, 1)
                pair(0, first=True)
                with act.Fori(1, PAIRS - 1) as j:
                    pair(j)
                pair(PAIRS - 1, last=True)
                p = take(PAIRS, 0)
                nc.scalar.activation(h3[:, 1], p, ACT.Gelu, bias=b3_sb[:]).then_inc(act_done, 1)
                for h in range(2):
                    p = take(PAIRS, 1 + h)
                    act.wait_ge(cs_done[1], 6 * PAIRS - 3 + h)
                    nc.scalar.activation(th[:, 1, h * HT:(h + 1) * HT], p, ACT.Tanh, scale=0.5, bias=hb4).then_inc(act_done, 1)

            @block.tensor
            def _(pe):
                def free(j, at, first):
                    if at < RING:
                        if first:
                            return
                        who, n = plan[at - RING]
                        if who == "a":
                            pe.wait_ge(act_done, PRO + ACT_TILES * (j - 1) + n + 1)
                        else:
                            pe.wait_ge(out_done, 8 * (j - 1) + n + 1)
                    else:
                        who, n = plan[at - RING]
                        if who == "a":
                            pe.wait_ge(act_done, PRO + ACT_TILES * j + n + 1)
                        else:
                            pe.wait_ge(out_done, 8 * j + n + 1)

                def l3(x, bank):
                    for h in range(2):
                        i = nc.tensor.matmul(po[h * M3:(h + 1) * M3, bank, :], w3_sb[:], h2[:, x, h * HT:(h + 1) * HT],
                                             start=True, stop=True, skip_group_check=True)
                    i.then_inc(tile_ready, 1)

                def l4(x, h, bank):
                    nc.tensor.matmul(po[:, bank, :], w4r[:, h, :], h3[:, x, :], start=True, stop=True).then_inc(tile_ready, 1)

                def in_tile(x, i, bank):
                    f, h = i // 2, i % 2
                    for q in range(4):
                        m = nc.tensor.transpose(po[:, bank, q * P:(q + 1) * P], xl[:, x, 4 * h + q, f * P:(f + 1) * P], ident[:])
                    m.then_inc(tile_ready, 1)

                def out_tile(x, g, bank):
                    for q in range(4):
                        t, f = 2 * g + q // 2, q % 2
                        m = nc.tensor.transpose(po[:, bank, q * P:(q + 1) * P], S[3][:, x, f, t * P:(t + 1) * P], ident[:])
                    m.then_inc(tile_ready, 1)

                def g_step(j, i):
                    if i == 0:
                        for q in range(2 * KD):
                            m = nc.tensor.matmul(pg[:, 0:2], gw1_sb[:, q // 2, :], sums[:, q, :], start=q == 0, stop=q == 2 * KD - 1)
                    if i == 1:
                        pe.wait_ge(g_act, 3 * j + 1)
                        m = nc.tensor.matmul(pg[0:M3, 2:4], gw2_sb[:], gh1[:], start=True, stop=True)
                    if i == 2:
                        pe.wait_ge(g_act, 3 * j + 2)
                        m = nc.tensor.matmul(pg[:, 4:6], gw3r[0:M3, :], gh2[0:M3, :], start=True, stop=True)
                    m.then_inc(g_psum, 1)

                def pair(j, first=False, last=False):
                    at = 0
                    for step, x, k in ffn_steps(first, last):
                        kind = real(step, x, k, at)
                        n = tiles_of(step, kind)
                        base = PRO + ACT_TILES * j
                        if step == "skip":
                            pe.wait_ge(tile_ready, PRO + TILES * j + at)
                            nc.tensor.sem_inc(tile_ready, n)
                        for t, i in enumerate(L1_TILES.get(step, ())):
                            h, m = i // 2, i % 2
                            free(j, at + t, first)
                            if m == 0 and k > 0:
                                pe.wait_ge(state_done[x], 6 * j + 2 * (k - 1) + h + 1)
                            if m == 0 and k == 0 and not first:
                                pe.wait_ge(act_done, PRO + ACT_TILES * (j - 1) + act_at[("inT", x, None)] + 4)
                            for f in range(KD):
                                q = nc.tensor.matmul(po[:, (at + t) % RING, :], w1_sb[:, f, m * P:(m + 1) * P],
                                                     S[k][:, x, f, h * HT:(h + 1) * HT], start=f == 0, stop=f == KD - 1)
                            q.then_inc(tile_ready, 1)
                        if step == "L2":
                            for h in range(2):
                                free(j, at + h, first)
                                pe.wait_ge(act_done, base + l1_at(x, k, 2 * h + 1) + 1)
                                for f in range(KD):
                                    q = nc.tensor.matmul(po[:, (at + h) % RING, :], w2_sb[:, f, :],
                                                         h1[:, x, f, h * HT:(h + 1) * HT], start=f == 0, stop=f == KD - 1)
                                q.then_inc(tile_ready, 1)
                        if step in ("L34", "L3"):
                            free(j, at, first)
                            if (x, k) == (1, 2):
                                pe.wait_ge(act_done, PRO + ACT_TILES * (j - 1) + act_at[("L2", x, k)] + 2)
                            else:
                                pe.wait_ge(act_done, base + act_at[("L2", x, k)] + 2)
                            l3(x, at % RING)
                        if step in ("L34", "L4"):
                            for h in range(2):
                                t = at + h + (step == "L34")
                                free(j, t, first)
                                pe.wait_ge(act_done, base + l34_at(x, k, 0) + 1)
                                l4(x, h, t % RING)
                        if step == "inT":
                            pe.wait_ge(xn_done, 2 * NT * (j + 1) + NT * (x + 1))
                            for i in range(4):
                                free(j, at + i, first)
                                in_tile(x, i, (at + i) % RING)
                        if step == "outT":
                            pe.wait_ge(state_done[x], 6 * j)
                            for i in range(4):
                                free(j, at + i, first)
                                out_tile(x, i, (at + i) % RING)
                        if step == "G1":
                            pe.wait_ge(act_done, base + act_at[("inT", 1, None)] + 4)
                            pe.wait_ge(g_act, 3 * (j + 1))
                            g_step(j + 1, 0)
                        if step == "G2":
                            g_step(j + 1, 1)
                        if step == "G3":
                            g_step(j, 2)
                        at += n

                pe.wait_ge(setup_p, 2)
                for x in range(2):
                    pe.wait_ge(xn_done, NT * (x + 1))
                    for i in range(4):
                        n = 4 * x + i
                        if n >= RING:
                            pe.wait_ge(act_done, n - RING + 1)
                        in_tile(x, i, (TILES - PRO + n) % RING)
                pe.wait_ge(act_done, PRO)
                pe.wait_ge(w_loaded, N_W)
                pe.wait_ge(setup_v, 10)
                g_step(0, 0)
                g_step(0, 1)
                pair(0, first=True)
                with pe.Fori(1, PAIRS - 1) as j:
                    pair(j)
                pair(PAIRS - 1, last=True)
                L = PAIRS - 1
                ab = PRO + ACT_TILES * PAIRS
                pe.wait_ge(act_done, ab)
                l3(1, 0)
                for h in range(2):
                    pe.wait_ge(act_done, ab + 1)
                    l4(1, h, 1 + h)
                for x in range(2):
                    pe.wait_ge(state_done[x], 6 * PAIRS)
                    for i in range(4):
                        at = 3 + 4 * x + i
                        if at >= RING:
                            pe.wait_ge(act_done, ab + 3)
                            if at - RING >= 3:
                                pe.wait_ge(out_done, 8 * PAIRS + at - RING - 3 + 1)
                        out_tile(x, i, at % RING)


Q_PART = [0, 0, 0, 1, 1, 1, 2, 2]
K_PART = [0, 1, 2, 0, 1, 2, 0, 1]


STEPS = {
    1: [("inT", 0, 1)],
    2: [("out", 3, -1), ("inT", 1, 1)],
    3: [("lamb", 0, 1)], 4: [("proj", 0, 1), ("proj", 1, 1), ("vaug", 3, 0)], 5: [("proj", 2, 1)], 6: [("square", 0, 1), ("proj", 3, 1)],
    7: [("root", 0, 1), ("y", 0, 1), ("v", 0, 1)], 8: [("ln", 0, 1), ("square", 1, 1), ("proj", 4, 1)],
    9: [("up", 0, 1), ("root", 1, 1), ("y", 1, 1), ("proj", 5, 1)],
    10: [("out", 0, 0), ("down", 0, 1), ("v", 1, 1)],
    11: [("sign", 0, 1), ("ln", 1, 1), ("square", 2, 1), ("proj", 6, 1)],
    12: [("up", 1, 1), ("root", 2, 1), ("y", 2, 1), ("proj", 7, 1)], 13: [("down", 1, 1), ("v", 2, 1)],
    14: [("sign", 1, 1), ("ln", 2, 1), ("square", 3, 1), ("v", 3, 1)],
    15: [("up", 2, 1), ("root", 3, 1), ("y", 3, 1), ("v", 4, 1), ("pair", 0, 1)],
    16: [("down", 2, 1), ("v", 5, 1)], 17: [("sign", 2, 1), ("ln", 3, 1), ("up", 3, 1), ("sum", 0, 1)],
    18: [("out", 1, 0), ("down", 3, 1)], 19: [("sign", 3, 1)], 20: [("pair", 1, 1), ("v", 6, 1)],
    21: [("sum", 1, 1)], 22: [("fac", 0, 1), ("v", 7, 1)], 23: [("facb", 0, 1), ("split", 0, 1)],
    24: [("facb", 1, 1)], 25: [("split", 2, 1)], 26: [("out", 2, 0)], 27: [("split", 1, 1), ("vaug", 0, 1)],
    28: [("split", 3, 1), ("stats", 0, 2)], 29: [("vaug", 1, 1), ("rstd", 0, 2)], 30: [("lam", 0, 2)], 31: [("vaug", 2, 1)]}
PROLOGUE = [(step[:-1], int(step[-1]), 0) for step in (
    "stats0 rstd0 lam0 inT0 inT1 lamb0 proj0 proj1 square0 proj2 proj3 root0 y0 square1 proj4 proj5 ln0 root1 y1 "
    "square2 proj6 proj7 up0 down0 root2 v0 v1 ln1 sign0 y2 square3 v2 v3 up1 down1 root3 ln2 sign1 y3 v4 v5 "
    "up2 down2 ln3 sign2 v6 v7 up3 down3 sign3 pair0 sum0 "
    "pair1 sum1 fac0 facb0 facb1 split0 split2 split1 split3 vaug0 vaug1 vaug2 vaug3").split()] + \
    [("stats", 0, 1), ("rstd", 0, 1), ("lam", 0, 1)]
UNIT_OF = {1: (2,), 2: (0, 2), 3: (0, 1, 3), 4: (0, 1, 2, 3)}
N_TILES = {"inT": 2, "lamb": 2, "proj": 1, "v": 1, "sum": 1, "facb": 2, "out": 2}


def steps_at(blk, first, left):
    return [(kind, i, off) for kind, i, off in STEPS.get(blk, [])
            if off <= left and not (first and (kind, i) in (("out", 3), ("vaug", 3)))]


def phase_b(nc, x_in, x_out, zq, bq, zk, bk, wvT, bv):
    B, T, D = x_in.shape
    NT, KD, DK = T // P, D // P, 16
    H = D // DK
    V1 = DK + 1
    G = H // 4
    scratch = nc.dram_tensor("b_scratch", [2, 3, D, T], BF16, kind="Internal").ap()
    BLK = G * NT
    SC = 0.25
    xi = x_in.rearrange("b (t p) d -> b p t d", p=P)
    xo = x_out.rearrange("b (t p) d -> b p t d", p=P)

    with Scope(nc, "b") as s:
        passed = s.passed
        z_sb = s.sb("z", [P, 2, KD, D])
        wv_sb = s.sb("wv", [P, KD, D])
        bvb = s.sb("bvb", [P, D])
        ident = s.sb("ident", [P, P])
        ones = s.sb("ones", [P, P])
        cst = s.sb("cst", [P, 4])
        cols = s.sb("cols", [P, 8, 4])
        stats = s.sb("stats", [P, NT, 6])
        mv = s.sb("mv", [P, NT, 2])
        sm = s.sb("sm", [P, 6, NT])
        fs = s.sb("fs", [P, 3, 2, NT])
        rec = s.sb("rec", [P, 4, 4])
        tmp = s.sb("tmp", [P, 4, 4, DK])
        xl = s.sb("xl", [P, NT, D])
        xr = s.sb("xr", [P, NT, D])
        xnT = s.sb("xnT", [P, KD, T])
        lamb = s.sb("lamb", [P, T])
        dg = s.sb("dg", [P, 2, NT, P])
        A = s.sb("A", [P, 4, T])
        SQ = s.sb("SQ", [P, 4, T])
        EP = s.sb("EP", [P, 2, T])
        vnew = s.sb("vnew", [P, NT, D])
        vaug = s.sb("vaug", [P, NT, H * V1 + 32 - V1])
        parts = s.sb("parts", [P, 2, 3, KD, T], BF16)
        st = s.sb("st", [P, 2, 2, 4, T], BF16)
        pr = s.sb("pr", [P, 8, T])
        osb = s.sb("osb", [P, T])
        ps = s.ps("ps", [P, 2, T])
        acc = s.ps("acc", [P, T])
        pm = s.ps("pm", [P, 2, 512])
        ve, rstd, nmean, l1, lam, var2 = (sm[:, i, :] for i in range(6))
        rcol, znc, tanh2, ep2, em2, kap, sh, zt = (cols[:, i, :] for i in range(8))
        zn2, zn2m = cols[:, 3, :], cols[:, 4, :]

        names = ("w_loaded setup_p setup_v setup_a setup_m xl_loaded xr_loaded stored stats_done mv_done rstd_done "
                 "xn_done lam_done dlam_done misc_ready misc_taken inT_done a_done sq_done root_done abs_done y_done ln_done e_done "
                 "d_done sign_done d2_done pair_done fsum_done froot_done fac_done dfac_done split_done parts_done "
                 "scores_ready probs_done pv_done acc_taken vaug_done out_mul out_step").split()
        S = {n: s.sem(n) for n in names}
        parts_stored = [s.sem(f"parts_stored{f}") for f in range(KD)]
        st_loaded = [s.sem(f"st_loaded{i}") for i in range(2)]
        N_W = 16 * 8
        N_G = 16 * 16

        PRO = sum(N_TILES.get(kind, 0) for kind, _, _ in PROLOGUE)
        TILES = sum(N_TILES.get(kind, 0) for blk in range(BLK) for kind, _, _ in STEPS.get(blk, []))
        LATE = N_TILES["out"]

        LAST = sum(N_TILES.get(kind, 0) for blk in range(BLK) for kind, _, off in STEPS.get(blk, []) if off > 0)

        def misc_base(b, first):
            return (PRO, PRO % 2) if first else (PRO - LATE + TILES * b, (PRO - LATE) % 2)

        def store_parts(sp, b, f):
            sp.wait_ge(S["parts_done"], 4 * b + 2 * f + 2)
            if not (isinstance(b, int) and b == 0):
                sp.sem_inc(passed, 1)
            for o in range(2):
                sp.dma_start(scratch[o, :, f * P:(f + 1) * P].rearrange("w p t -> p w t"), parts[:, o, :, f, :])\
                    .then_inc(parts_stored[f], 16)

        def gather(sp, b, g):
            slot = g % 2
            for o, part in enumerate((Q_PART, K_PART)):
                for i, w in enumerate(part):
                    sp.dma_start(st[i * DK:(i + 1) * DK, slot, o],
                                 scratch[o, w, 64 * g:64 * g + 64, :].rearrange("(h d) t -> d h t", d=DK))\
                        .then_inc(st_loaded[slot], 16)

        with nc.Block() as block:

            @block.sync
            def _(sp):
                sp.dma_start(xl[:], xi[0]).then_inc(S["xl_loaded"], 16)
                for o, z in enumerate((zq, zk)):
                    sp.dma_start(z_sb[:, o], z.rearrange("(k p) n -> p k n", p=P)).then_inc(S["w_loaded"], 16)
                for o, r in enumerate((bq, bk)):
                    for f in range(KD):
                        sp.dma_start(rcol[:, 2 * o + f:2 * o + f + 1],
                                     r[f * P:(f + 1) * P].rearrange("(p o) -> p o", o=1)).then_inc(S["w_loaded"], 16)
                sp.dma_start(wv_sb[:], wvT.rearrange("(k p) n -> p k n", p=P)).then_inc(S["w_loaded"], 16)
                sp.dma_start(bvb[:], bv.rearrange("(o n) -> o n", o=1).broadcast_to([P, D])).then_inc(S["w_loaded"], 16)
                sp.dma_start(xr[:], xi[0]).then_inc(S["xr_loaded"], 16)
                sp.wait_ge(S["inT_done"], 1)
                sp.dma_start(xl[:], xi[1]).then_inc(S["xl_loaded"], 16)
                store_parts(sp, 0, 0)
                sp.wait_ge(parts_stored[0], 32)
                gather(sp, 0, 0)
                store_parts(sp, 0, 1)
                gather(sp, 0, 1)

                def dram(v, b):
                    return v[b] if isinstance(b, int) else v[bass.ds(b, 1)].rearrange("o p t d -> (o p) t d")

                def batch(b, first=False, left=2):
                    if not first:
                        sp.wait_ge(S["out_step"], 8 * b)
                        sp.sem_inc(passed, 1)
                        sp.dma_start(dram(xo, b - 1), xr[:]).then_inc(S["stored"], 16)
                        sp.wait_ge(S["stored"], 16 * b)
                        sp.sem_inc(passed, 1)
                        sp.dma_start(xr[:], dram(xi, b)).then_inc(S["xr_loaded"], 16)
                    if left > 1:
                        sp.wait_ge(S["inT_done"], b + 2)
                        sp.sem_inc(passed, 1)
                        sp.dma_start(xl[:], dram(xi, b + 2)).then_inc(S["xl_loaded"], 16)
                    sp.wait_ge(parts_stored[1], 32 * (b + 1))
                    if not first:
                        sp.sem_inc(passed, 1)
                    for g in (2, 3):
                        sp.wait_ge(S["scores_ready"], 4 * BLK * b + 32 * (g - 1))
                        sp.sem_inc(passed, 1)
                        gather(sp, b, g)
                    if left > 0:
                        for q in range(2):
                            sp.wait_ge(st_loaded[q], 2 * N_G * (b + 1))
                            sp.sem_inc(passed, 1)
                        store_parts(sp, b + 1, 0)
                        sp.wait_ge(parts_stored[0], 32 * (b + 2))
                        sp.sem_inc(passed, 1)
                        sp.wait_ge(S["scores_ready"], 4 * BLK * b + 32 * 3)
                        sp.sem_inc(passed, 1)
                        gather(sp, b + 1, 0)
                        store_parts(sp, b + 1, 1)
                        sp.wait_ge(S["scores_ready"], 4 * BLK * b + 32 * 4)
                        sp.sem_inc(passed, 1)
                        gather(sp, b + 1, 1)

                batch(0, first=True)
                with sp.Fori(1, B - 2) as b:
                    batch(b)
                batch(B - 2, left=1)
                batch(B - 1, left=0)
                sp.wait_ge(S["out_step"], 8 * B)
                sp.dma_start(xo[B - 1], xr[:]).then_inc(S["stored"], 16)
                sp.wait_ge(S["stored"], 16 * B)

            @block.gpsimd
            def _(pool):
                make_identity(nc, pool, ident, S["setup_p"])
                eye = ident[:].unsqueeze(1).broadcast_to([P, NT, P])
                nc.gpsimd.memset(ones[:], 1.0).then_inc(S["setup_p"], 1)
                nc.gpsimd.memset(cst[:, 0:1], -0.5).then_inc(S["setup_p"], 1)
                nc.gpsimd.memset(cst[:, 1:2], 0.5).then_inc(S["setup_p"], 1)
                nc.gpsimd.memset(cst[:, 2:3], 0.25).then_inc(S["setup_p"], 1)
                nc.gpsimd.memset(cst[:, 3:4], 1.0).then_inc(S["setup_p"], 1)
                nc.gpsimd.memset(vaug[:], 1.0).then_inc(S["setup_p"], 1)
                def again(b):
                    return not isinstance(b, int) or b > 0

                def step(kind, i, b):
                    if kind == "rstd":
                        pool.wait_ge(S["mv_done"], NT * b + NT)
                        if again(b):
                            pool.wait_ge(S["xn_done"], NT * b)
                            pool.wait_ge(S["lam_done"], 5 * b)
                        pool.sem_inc(passed, 1)
                        nc.gpsimd.tensor_scalar(ve, mv[:, :, 1], EPS, None, ALU.add).then_inc(S["rstd_done"], 1)
                        nc.gpsimd.tensor_scalar(nmean, mv[:, :, 0], -1.0, None, ALU.mult).then_inc(S["rstd_done"], 1)
                        pool.wait_ge(S["rstd_done"], 3 * b + 1)
                        nc.gpsimd.tensor_tensor(rstd, ve, cst[:, 0:1].broadcast_to([P, NT]), ALU.pow).then_inc(S["rstd_done"], 1)
                        pool.wait_ge(S["rstd_done"], 3 * b + 3)
                        pool.sem_inc(passed, 1)
                        for t in range(NT):
                            nc.gpsimd.tensor_scalar(xl[:, t, :], xl[:, t, :], nmean[:, t:t + 1], rstd[:, t:t + 1],
                                                    ALU.add, ALU.mult).then_inc(S["xn_done"], 1)
                    if kind == "lam":
                        pool.wait_ge(S["lam_done"], 5 * b + 5)
                        if again(b):
                            pool.wait_ge(S["parts_done"], 4 * b)
                            pool.wait_ge(S["dfac_done"], 2 * b)
                        nc.gpsimd.tensor_tensor(dg[:, 0], eye, lam.unsqueeze(2).broadcast_to([P, NT, P]), ALU.mult)\
                            .then_inc(S["dlam_done"], 1)
                    if kind == "proj":
                        if i % 2:
                            q = i // 2
                            pool.wait_ge(S["a_done"], 8 * b + i + 1)
                            nc.gpsimd.tensor_tensor(SQ[:, q, :], A[:, q, :], A[:, q, :], ALU.mult).then_inc(S["sq_done"], 1)
                    if kind == "down":
                        pool.wait_ge(S["e_done"], 8 * b + 2 * i + 2)
                        nc.gpsimd.tensor_tensor(SQ[:, i, :], EP[:, i % 2, :], SQ[:, i, :], ALU.subtract).then_inc(S["d_done"], 1)
                    if kind == "sign":
                        pool.wait_ge(S["sign_done"], 4 * b + i + 1)
                        nc.gpsimd.tensor_tensor(A[:, i, :], SQ[:, i, :], SQ[:, i, :], ALU.mult).then_inc(S["d2_done"], 1)
                    if kind == "pair":
                        pool.wait_ge(S["d2_done"], 4 * b + 2 * i + 2)
                        nc.gpsimd.tensor_tensor(A[:, 2 * i, :], A[:, 2 * i, :], A[:, 2 * i + 1, :], ALU.add)\
                            .then_inc(S["pair_done"], 1)
                    if kind == "fac":
                        pool.wait_ge(S["fsum_done"], 2 * b + 2)
                        nc.gpsimd.tensor_tensor(fs[:, 1], fs[:, 0], cst[:, 1:2].unsqueeze(2).broadcast_to([P, 2, NT]),
                                                ALU.pow).then_inc(S["froot_done"], 1)
                        pool.wait_ge(S["fac_done"], 3 * b + 3)
                        pool.wait_ge(S["dlam_done"], b + 1)
                        pool.sem_inc(passed, 1)
                        for o in range(2):
                            nc.gpsimd.tensor_tensor(dg[:, o], eye, fs[:, 2, o, :].unsqueeze(2).broadcast_to([P, NT, P]), ALU.mult)\
                                .then_inc(S["dfac_done"], 1)

                def batch(b, first=False, left=2):
                    for blk in range(BLK):
                        for kind, i, off in steps_at(blk, first, left):
                            step(kind, i, b + off)

                step("rstd", 0, 0)
                pool.wait_ge(S["setup_v"], 2)
                nc.gpsimd.tensor_tensor(znc, znc, cst[:, 1:2].broadcast_to([P, 4]), ALU.pow).then_inc(S["setup_p"], 1)
                for kind, i, off in PROLOGUE[2:]:
                    step(kind, i, off)
                batch(0, first=True)
                with pool.Fori(1, B - 2) as b:
                    batch(b)
                batch(B - 2, left=1)

            @block.vector
            def _(dve):
                def again(b):
                    return not isinstance(b, int) or b > 0

                def tile(m):
                    dve.wait_ge(S["misc_ready"], m + 1)

                def step(kind, i, b, m, par):
                    if kind == "stats":
                        dve.wait_ge(S["xl_loaded"], 16 * b + 16)
                        if again(b):
                            dve.wait_ge(S["lam_done"], 5 * b)
                            dve.wait_ge(S["xn_done"], NT * b)
                        for t in range(NT):
                            nc.vector.bn_stats(stats[:, t, :], xl[:, t, :]).then_inc(S["stats_done"], 1)
                        dve.wait_ge(S["stats_done"], NT * b + NT)
                        dve.sem_inc(passed, 1)
                        for t in range(NT):
                            nc.vector.bn_aggr(mv[:, t, :], stats[:, t, :]).then_inc(S["mv_done"], 1)
                    if kind == "lam":
                        dve.wait_ge(S["rstd_done"], 3 * b + 3)
                        dve.wait_ge(S["mv_done"], NT * b + NT)
                        if again(b):
                            dve.wait_ge(S["dlam_done"], b)
                        nc.vector.tensor_tensor(l1, rstd, rstd, ALU.mult).then_inc(S["lam_done"], 1)
                        dve.wait_ge(S["lam_done"], 5 * b + 1)
                        nc.vector.tensor_tensor(var2, l1, mv[:, :, 1], ALU.mult).then_inc(S["lam_done"], 1)
                        dve.wait_ge(S["lam_done"], 5 * b + 2)
                        nc.vector.tensor_scalar(l1, var2, -float(D), 1.0, ALU.mult, ALU.add).then_inc(S["lam_done"], 1)
                        dve.wait_ge(S["lam_done"], 5 * b + 3)
                        nc.vector.reciprocal(var2, l1).then_inc(S["lam_done"], 1)
                        dve.wait_ge(S["lam_done"], 5 * b + 4)
                        nc.vector.tensor_scalar(lam, var2, 2.0, None, ALU.mult).then_inc(S["lam_done"], 1)
                    if kind == "inT":
                        for h in range(2):
                            tile(m + h)
                            nc.vector.tensor_copy(xnT[:, i, h * 512:(h + 1) * 512], pm[:, (par + h) % 2, :]).then_inc(S["misc_taken"], 1)
                    if kind == "lamb":
                        for h in range(2):
                            tile(m + h)
                            if again(b) and h == 0:
                                dve.wait_ge(S["a_done"], 8 * b)
                            nc.vector.tensor_copy(lamb[:, h * 512:(h + 1) * 512], pm[:, (par + h) % 2, :]).then_inc(S["misc_taken"], 1)
                        dve.wait_ge(S["misc_taken"], m + 2)
                    if kind == "proj":
                        if again(b):
                            dve.wait_ge(S["pair_done"], 2 * b)
                        q, h = i // 2, i % 2
                        tile(m)
                        c = slice(h * 512, (h + 1) * 512)
                        nc.vector.scalar_tensor_tensor(A[:, q, c], pm[:, par % 2, :], zt[:, q:q + 1], lamb[:, c],
                                                       ALU.subtract, ALU.mult).then_inc(S["misc_taken"], 1)
                        dve.wait_ge(S["misc_taken"], m + 1)
                        nc.vector.tensor_scalar(A[:, q, c], A[:, q, c], kap[:, q:q + 1], sh[:, q:q + 1], ALU.mult, ALU.add)\
                            .then_inc(S["a_done"], 1)
                    if kind == "y":
                        spare = EP[:, i % 2, :]
                        if i >= 2:
                            dve.wait_ge(S["d_done"], 4 * b + i - 1)
                        elif again(b):
                            dve.wait_ge(S["d_done"], 4 * b)
                        nc.vector.tensor_scalar(spare.bitcast(I32), A[:, i, :].bitcast(I32), 2147483647, None,
                                                ALU.bitwise_and).then_inc(S["abs_done"], 1)
                        dve.wait_ge(S["root_done"], 8 * b + 2 * i + 2)
                        dve.wait_ge(S["abs_done"], 4 * b + i + 1)
                        nc.vector.tensor_tensor(SQ[:, i, :], spare, SQ[:, i, :], ALU.add).then_inc(S["y_done"], 1)
                    if kind == "sign":
                        dve.wait_ge(S["d_done"], 4 * b + i + 1)
                        nc.vector.scalar_tensor_tensor(SQ[:, i, :].bitcast(I32), A[:, i, :].bitcast(I32), -2147483648,
                                                       SQ[:, i, :].bitcast(I32), ALU.bitwise_and, ALU.bitwise_or)\
                            .then_inc(S["sign_done"], 1)
                    if kind == "v":
                        tile(m)
                        if again(b):
                            dve.wait_ge(S["vaug_done"], 4 * b)
                        nc.vector.tensor_tensor(vnew[:, i, :], pm[:, par % 2, 0:D], bvb[:], ALU.add).then_inc(S["misc_taken"], 1)
                        dve.wait_ge(S["misc_taken"], m + 1)
                    if kind == "vaug":
                        if again(b):
                            dve.wait_ge(S["pv_done"], 2 * (BLK * b - NT + 2 * i + 2))
                        t = slice(2 * i, 2 * i + 2)
                        nc.vector.tensor_copy(vaug[:, t, 0:H * V1].rearrange("p t (h c) -> p t h c", c=V1)[:, :, :, 0:DK],
                                              vnew[:, t, :].rearrange("p t (h c) -> p t h c", c=DK)).then_inc(S["vaug_done"], 1)
                    if kind == "sum":
                        tile(m)
                        if again(b):
                            dve.wait_ge(S["froot_done"], b)
                        nc.vector.tensor_scalar(fs[:, 0, i, :], pm[:, par % 2, 0:NT], 1.0, None, ALU.add).then_inc(S["fsum_done"], 1)
                        dve.wait_ge(S["fsum_done"], 2 * b + i + 1)
                        nc.vector.sem_inc(S["misc_taken"], 1)
                    if kind == "fac":
                        dve.wait_ge(S["froot_done"], b + 1)
                        if again(b):
                            dve.wait_ge(S["dfac_done"], 2 * b)
                        nc.vector.tensor_scalar(fs[:, 1], fs[:, 1], 2.0, 2.0, ALU.mult, ALU.add).then_inc(S["fac_done"], 1)
                        dve.wait_ge(S["fac_done"], 3 * b + 1)
                        nc.vector.reciprocal(fs[:, 2], fs[:, 1]).then_inc(S["fac_done"], 2)
                    if kind == "facb":
                        for h in range(2):
                            tile(m + h)
                            c = slice(h * 512, (h + 1) * 512)
                            v = SQ[:, 2 * i:2 * i + 2, c]
                            nc.vector.tensor_tensor(v, v, pm[:, (par + h) % 2, :].unsqueeze(1).broadcast_to([P, 2, 512]),
                                                    ALU.mult).then_inc(S["misc_taken"], 1)
                        dve.wait_ge(S["misc_taken"], m + 2)
                    if kind == "split":
                        if again(b):
                            dve.wait_ge(parts_stored[i % 2], 32 * b)
                        q = SQ[:, i, :]
                        p1, p2, p3 = (parts[:, i // 2, w, i % 2, :] for w in range(3))
                        n = 16 * b + 4 * (2 * (i % 2) + i // 2)
                        nc.vector.tensor_copy(p1, q).then_inc(S["split_done"], 1)
                        dve.wait_ge(S["split_done"], n + 1)
                        nc.vector.tensor_tensor(q, q, p1, ALU.subtract).then_inc(S["split_done"], 1)
                        dve.wait_ge(S["split_done"], n + 2)
                        nc.vector.tensor_copy(p2, q).then_inc(S["split_done"], 1)
                        dve.wait_ge(S["split_done"], n + 3)
                        nc.vector.tensor_tensor(p3, q, p2, ALU.subtract).then_inc(S["split_done"], 1)
                        dve.wait_ge(S["split_done"], n + 4)
                        nc.vector.sem_inc(S["parts_done"], 1)

                def take_acc(grp, h):
                    dve.wait_ge(S["pv_done"], 2 * (NT * grp + NT) - 1 + h)
                    if again(grp):
                        dve.wait_ge(S["out_step"], 2 * grp)
                    c = slice(h * 512, (h + 1) * 512)
                    nc.vector.tensor_copy(osb[:, c], acc[:, c]).then_inc(S["acc_taken"], 1)

                def out(grp, g, b, m, par):
                    dve.wait_ge(S["xr_loaded"], 16 * (b + 1))
                    for h in range(2):
                        tile(m + h)
                        o = pm[:, (par + h) % 2, :].rearrange("p (t j c) -> p t j c", t=4, j=4)
                        if again(grp) or h > 0:
                            dve.wait_ge(S["out_step"], 2 * grp + h)
                        nc.vector.reciprocal(rec[:], o[:, :, :, DK]).then_inc(S["out_mul"], 1)
                        dve.wait_ge(S["out_mul"], 4 * grp + 2 * h + 1)
                        nc.vector.tensor_tensor(tmp[:], o[:, :, :, 0:DK], rec[:].unsqueeze(3).broadcast_to([P, 4, 4, DK]),
                                                ALU.mult).then_inc(S["out_mul"], 1)
                        dve.wait_ge(S["out_mul"], 4 * grp + 2 * h + 2)
                        nc.vector.sem_inc(S["misc_taken"], 1)
                        x = xr[:, 4 * h:4 * h + 4, 64 * g:64 * g + 64]
                        nc.vector.tensor_tensor(x, x, tmp[:].rearrange("p t j c -> p t (j c)"), ALU.add).then_inc(S["out_step"], 1)

                def batch(b, first=False, left=2):
                    m, par = misc_base(b, first)
                    for blk in range(BLK):
                        if blk % NT <= 1 and not (first and blk <= 1):
                            take_acc(G * b + blk // NT - 1, blk % NT)
                        for kind, i, off in steps_at(blk, first, left):
                            if kind == "out":
                                out(G * (b + off) + i, i, b + off, m, par)
                            else:
                                step(kind, i, b + off, m, par)
                            m, par = m + N_TILES.get(kind, 0), par + N_TILES.get(kind, 0)

                step("stats", 0, 0, 0, 0)
                dve.wait_ge(S["w_loaded"], N_W)
                nc.vector.tensor_tensor(A[:, 0, :], z_sb[:].rearrange("p o k n -> p (o k n)"),
                                        z_sb[:].rearrange("p o k n -> p (o k n)"), ALU.mult).then_inc(S["setup_v"], 1)
                dve.wait_ge(S["setup_m"], 1)
                nc.vector.tensor_copy(znc, pm[:, 0, 0:4]).then_inc(S["setup_v"], 1)
                dve.wait_ge(S["setup_p"], 9)
                dve.wait_ge(S["setup_a"], 3)
                c = [3]

                def link(ins):
                    ins.then_inc(S["setup_v"], 1)
                    dve.wait_ge(S["setup_v"], c[0])
                    c[0] += 1
                link(nc.vector.tensor_scalar(znc, znc, 1e-15, None, ALU.max))
                link(nc.vector.tensor_tensor(ep2, ep2, em2, ALU.add))
                link(nc.vector.tensor_scalar(ep2, ep2, 0.5, None, ALU.mult))
                link(nc.vector.tensor_tensor(sh, tanh2, ep2, ALU.mult))
                link(nc.vector.tensor_tensor(zt, tanh2, znc, ALU.mult))
                link(nc.vector.reciprocal(kap, znc))
                link(nc.vector.tensor_tensor(kap, kap, ep2, ALU.mult))
                link(nc.vector.tensor_scalar(zn2, znc, 2.0, None, ALU.mult))
                link(nc.vector.tensor_scalar(zn2m, znc, -2.0, None, ALU.mult))
                m = 0
                for kind, i, off in PROLOGUE[1:]:
                    step(kind, i, off, m, m)
                    m += N_TILES.get(kind, 0)
                batch(0, first=True)
                with dve.Fori(1, B - 2) as b:
                    batch(b)
                batch(B - 2, left=1)
                batch(B - 1, left=0)
                for h in range(2):
                    take_acc(G * B - 1, h)
                m, par = misc_base(B, False)
                out(G * B - 1, 3, B - 1, m - LAST, par + LAST)

            @block.scalar
            def _(act):
                act.wait_ge(S["w_loaded"], N_W)
                nc.scalar.activation(tanh2, rcol, ACT.Tanh, scale=2.0).then_inc(S["setup_a"], 1)
                nc.scalar.activation(ep2, rcol, ACT.Exp, scale=2.0).then_inc(S["setup_a"], 1)
                nc.scalar.activation(em2, rcol, ACT.Exp, scale=-2.0).then_inc(S["setup_a"], 1)
                nc.scalar.preload_act_table_set("natural_log_exp_and_others")
                act.wait_ge(S["setup_v"], 11)
                act.wait_ge(S["setup_p"], 7)

                def step(kind, i, b):
                    if kind == "square":
                        act.wait_ge(S["sq_done"], 4 * b + i + 1)
                        nc.scalar.activation(SQ[:, i, :], SQ[:, i, :], ACT.Ln, bias=cst[:, 3:4]).then_inc(S["root_done"], 1)
                    if kind == "root":
                        act.wait_ge(S["root_done"], 8 * b + 2 * i + 1)
                        nc.scalar.activation(SQ[:, i, :], SQ[:, i, :], ACT.Exp, scale=0.5).then_inc(S["root_done"], 1)
                    if kind == "ln":
                        act.wait_ge(S["y_done"], 4 * b + i + 1)
                        nc.scalar.activation(SQ[:, i, :], SQ[:, i, :], ACT.Ln).then_inc(S["ln_done"], 1)
                    if kind == "up":
                        act.wait_ge(S["ln_done"], 4 * b + i + 1)
                        n = 4 * b + i
                        if not isinstance(n, int) or n >= 2:
                            act.wait_ge(S["d_done"], n - 1)
                        nc.scalar.activation(EP[:, i % 2, :], SQ[:, i, :], ACT.Exp, scale=zn2[:, i:i + 1]).then_inc(S["e_done"], 1)
                    if kind == "down":
                        act.wait_ge(S["e_done"], 8 * b + 2 * i + 1)
                        nc.scalar.activation(SQ[:, i, :], SQ[:, i, :], ACT.Exp, scale=zn2m[:, i:i + 1]).then_inc(S["e_done"], 1)

                def batch(b, first=False, left=2):
                    for blk in range(BLK):
                        steps = [x for x in steps_at(blk, first, left) if x[0] in ("square", "root", "ln", "up", "down")]
                        for j in range(4):
                            for kind, i, off in steps[j // 2:j // 2 + 1] if j % 2 == 0 else ():
                                step(kind, i, b + off)
                            n = 4 * BLK * b + 4 * blk + j
                            act.wait_ge(S["scores_ready"], n + 1)
                            if not (first and blk < 2):
                                act.wait_ge(S["pv_done"], 2 * (BLK * b + blk - 1))
                            nc.scalar.activation(pr[:, 4 * (blk % 2) + j, :], ps[:, j % 2, :], ACT.Exp, scale=SC).then_inc(S["probs_done"], 1)

                for kind, i, off in PROLOGUE:
                    step(kind, i, off)
                batch(0, first=True)
                with act.Fori(1, B - 2) as b:
                    batch(b)
                batch(B - 2, left=1)
                batch(B - 1, left=0)

            @block.tensor
            def _(pe):
                def bank_free(m):
                    if not isinstance(m, int) or m >= 2:
                        pe.wait_ge(S["misc_taken"], m - 1)

                def step(kind, i, b, m, par, h):
                    bank = pm[:, par % 2, :]
                    if kind == "inT":
                        if h == 0:
                            pe.wait_ge(S["xn_done"], NT * b + NT)
                        bank_free(m)
                        for q in range(4):
                            x = nc.tensor.transpose(bank[:, q * P:(q + 1) * P], xl[:, 4 * h + q, i * P:(i + 1) * P], ident[:])
                    if kind in ("lamb", "facb"):
                        if h == 0:
                            if kind == "lamb":
                                pe.wait_ge(S["dlam_done"], b + 1)
                            else:
                                pe.wait_ge(S["dfac_done"], 2 * b + i + 1)
                        bank_free(m)
                        x = nc.tensor.matmul(bank, ones[:], dg[:, i, 4 * h:4 * h + 4, :].rearrange("p t n -> p (t n)"),
                                             start=True, stop=True)
                    if kind == "proj":
                        bank_free(m)
                        if i == 0 and h == 0:
                            pe.wait_ge(S["misc_taken"], m - 2)
                        q, c = i // 2, slice((i % 2) * 512, (i % 2 + 1) * 512)
                        for k in range(KD):
                            x = nc.tensor.matmul(bank, z_sb[:, q // 2, k, (q % 2) * P:(q % 2 + 1) * P], xnT[:, k, c],
                                                 start=k == 0, stop=k == KD - 1)
                    if kind == "v":
                        bank_free(m)
                        for k in range(KD):
                            x = nc.tensor.matmul(bank[:, 0:D], xnT[:, k, i * P:(i + 1) * P], wv_sb[:, k, :],
                                                 start=k == 0, stop=k == KD - 1)
                    if kind == "sum":
                        pe.wait_ge(S["pair_done"], 2 * b + i + 1)
                        bank_free(m)
                        for t in range(NT):
                            x = nc.tensor.matmul(bank[:, t:t + 1], A[:, 2 * i, t * P:(t + 1) * P], cst[:, 2:3],
                                                 start=True, stop=True)
                    x.then_inc(S["misc_ready"], 1)
                    if kind == "inT" and i == 1 and h == 1:
                        pe.wait_ge(S["misc_ready"], m + 1)
                        pe.sem_inc(S["inT_done"], 1)

                def out(grp, m, par, h):
                    pe.wait_ge(S["acc_taken"], 2 * grp + h + 1)
                    bank_free(m + h)
                    for q in range(4):
                        x = nc.tensor.transpose(pm[:, (par + h) % 2, q * P:(q + 1) * P],
                                                osb[:, (4 * h + q) * P:(4 * h + q + 1) * P], ident[:])
                    x.then_inc(S["misc_ready"], 1)

                def weigh(b, blk, h, first=False):
                    g, kt = blk // NT, blk % NT
                    if h == 0:
                        pe.wait_ge(S["probs_done"], 4 * BLK * b + 4 * blk + 4)
                        if g == 0 and kt % 2 == 0:
                            pe.wait_ge(S["vaug_done"], 4 * b + kt // 2 + 1)
                    if kt == 0 and not (first and g == 0):
                        pe.wait_ge(S["acc_taken"], 2 * (G * b + g - 1) + h + 1)
                    for j in range(4):
                        c = V1 * (4 * g + j)
                        x = nc.tensor.matmul(acc[32 * j:32 * j + 32, h * 512:(h + 1) * 512], vaug[:, kt, c:c + 32],
                                             pr[:, 4 * (kt % 2) + j, h * 512:(h + 1) * 512],
                                             start=kt == 0, stop=kt == NT - 1, skip_group_check=True)
                    x.then_inc(S["pv_done"], 1)

                def batch(b, first=False, left=2):
                    m, par = misc_base(b, first)
                    for blk in range(BLK):
                        g, kt = blk // NT, blk % NT
                        tiles = [(kind, i, off, h) for kind, i, off in steps_at(blk, first, left)
                                 for h in range(N_TILES.get(kind, 0))]
                        if kt == 0:
                            pe.wait_ge(st_loaded[g % 2], N_G * (2 * b + g // 2 + 1))
                        for j in range(4):
                            u = 4 * BLK * b + 4 * blk + j
                            if not (first and 4 * blk + j < 2):
                                pe.wait_ge(S["probs_done"], u - 1)
                            for h in range(2):
                                x = nc.tensor.matmul(ps[:, j % 2, h * 512:(h + 1) * 512],
                                                     st[:, g % 2, 1, j, kt * P:(kt + 1) * P],
                                                     st[:, g % 2, 0, j, h * 512:(h + 1) * 512], start=True, stop=True)
                            x.then_inc(S["scores_ready"], 1)
                            if j % 2 == 1:
                                if blk >= 1:
                                    weigh(b, blk - 1, j // 2, first)
                                elif not first:
                                    weigh(b - 1, BLK - 1, j // 2)
                            for q, (kind, i, off, h) in enumerate(tiles):
                                if UNIT_OF[len(tiles)][q] == j:
                                    if kind == "out":
                                        out(G * (b + off) + i, m - h, par - h, h)
                                    else:
                                        step(kind, i, b + off, m, par, h)
                                    m, par = m + 1, par + 1

                pe.wait_ge(S["setup_p"], 8)
                pe.wait_ge(S["setup_v"], 1)
                for o in range(2):
                    for f in range(2):
                        for k in range(KD):
                            a = (o * KD + k) * D + f * P
                            x = nc.tensor.matmul(pm[:, 0, 2 * o + f:2 * o + f + 1], A[:, 0, a:a + P], cst[:, 3:4],
                                                 start=k == 0, stop=k == KD - 1)
                x.then_inc(S["setup_m"], 1)
                pe.wait_ge(S["setup_v"], 2)
                m = 0
                for kind, i, off in PROLOGUE:
                    for h in range(N_TILES.get(kind, 0)):
                        step(kind, i, off, m, m, h)
                        m += 1
                batch(0, first=True)
                with pe.Fori(1, B - 2) as b:
                    batch(b)
                batch(B - 2, left=1)
                batch(B - 1, left=0)
                for h in range(2):
                    weigh(B - 1, BLK - 1, h)
                m, par = misc_base(B, False)
                for h in range(2):
                    out(G * B - 1, m - LAST, par + LAST, h)


def build_layer(nc, a, out):
    x = a["L0_attn_a_x"]
    x1, x2, x3 = (nc.dram_tensor(name, x.shape, F32, kind="Internal").ap() for name in ("x1", "x2", "x3"))
    cn = [a[f"L0_ffn_cn_{v}{i}"] for i in range(1, 5) for v in "wb"]
    gc = [a[f"L0_ffn_gc_{v}{i}"] for i in range(1, 4) for v in "wb"]
    phase_a(nc, x, *(a["L0_attn_a_" + n] for n in ("Wk", "Wv", "Wo", "gate", "freqs")), x1)
    phase_f(nc, "f1", x1, x2, cn, gc, a["L0_ffn_adaptive_range"])
    phase_b(nc, x2, x3, *(a["L0_attn_b_" + n] for n in ("z_q", "b_q", "z_k", "b_k", "w_v", "b_v")))
    phase_f(nc, "f2", x3, out, cn, gc, a["L0_ffn_adaptive_range"])


def kernel(**inputs):
    import numpy as _np
    import concourse.bacc as _bacc
    from concourse.bass_utils import run_bass_kernel_spmd as _run

    nc = _bacc.Bacc("TRN2", target_bir_lowering=False, num_devices=1)
    inputs["L0_attn_b_w_v"] = _np.asarray(inputs["L0_attn_b_w_v"]).T
    arrays, args = {}, {}
    for name, v in inputs.items():
        v = _np.ascontiguousarray(v)
        arrays[f"in_{name}_dram"] = v
        args[name] = nc.dram_tensor(f"in_{name}_dram", v.shape, mybir.dt.from_np(v.dtype), kind="ExternalInput").ap()
    out = nc.dram_tensor("out_0_dram", inputs["L0_attn_a_x"].shape, F32, kind="ExternalOutput").ap()
    build_layer(nc, args, out)
    r = _run(nc, [arrays], core_ids=[0])
    return r.results[0]["out_0_dram"]
```
